# Optimizing a Trainium2 kernel written in Bass

```python
import numpy as np
import jax
import jax.numpy as jnp

def _softmax(x, axis=-1):
    return jax.nn.softmax(x, axis=axis)

def _gelu(x):
    return jax.nn.gelu(x, approximate=True)

def _silu(x):
    return jax.nn.silu(x)

def _sigmoid(x):
    return jax.nn.sigmoid(x)

def _layernorm(x, axis=-1, eps=1e-05):
    m = jnp.mean(x, axis=axis, keepdims=True)
    v = jnp.var(x, axis=axis, keepdims=True)
    return (x - m) / jnp.sqrt(v + eps)

def _scatter_add(tgt, idx, src, axis=0):
    return tgt.at[idx].add(src)

def _segment_sum(src, seg, n):
    return jax.ops.segment_sum(src, seg, n)
kernel_name = 'mk_seq_postln_d1_jaxref_r2_fe3b7f'

def setup_inputs(seed: int=0):
    np.random.seed(seed)
    _w = jnp.asarray

    def _L0_attn_setup():
        import jax, jax.numpy as jnp
        import numpy as np
        B, L, D, M, R, W = (4, 1024, 1024, 64, 128, 4)
        SCALE = 1.0 / float(np.sqrt(M))
        NORM_EPS = 1e-12

        def _causal_depthwise_conv(x, w, b):
            xp = jnp.pad(x, ((0, 0), (W - 1, 0), (0, 0)))
            y = sum((xp[:, i:i + x.shape[1], :] * w[:, i] for i in range(W))) + b
            return jax.nn.silu(y)
        key = jax.random.key(seed)
        ks = jax.random.split(key, 8)
        s = lambda k, shape: jax.random.normal(k, shape, jnp.float32) * 0.02
        return dict(hidden_states=jax.random.normal(ks[0], (B, L, D), jnp.float32), conv_w=s(ks[1], (D, W)), conv_b=jnp.zeros((D,), jnp.float32), in_proj_w=s(ks[2], (2 * M, D)), ch_gate_w0=s(ks[3], (R, D)), ch_gate_w1=s(ks[4], (D, R)), ch_gate_b1=jnp.zeros((D,), jnp.float32), mem_gate_w=s(ks[5], (2 * M, D)), mem_gate_b=jax.random.normal(ks[6], (2 * M,), jnp.float32), residual_weight=jnp.ones((D,), jnp.float32))
    _L0_attn_in = _L0_attn_setup()

    def _L0_ffn_setup():
        import jax, jax.numpy as jnp
        import numpy as np
        D_MODEL = 1024
        NUM_TILES = 64
        D_SLICE = D_MODEL // NUM_TILES
        TILES_PER_CLUSTER = 8
        NUM_CLUSTERS = NUM_TILES // TILES_PER_CLUSTER
        GRID = 16
        LN_EPS = 1e-05
        DIMS = (np.arange(NUM_TILES)[:, None] * D_SLICE + np.arange(D_SLICE)[None, :]) % D_MODEL
        DIMS = jnp.asarray(DIMS, dtype=jnp.int32)

        def _forward(x, ln_gamma, ln_beta, spline_bases, spline_slopes, output_scale):
            B, S, D = x.shape
            N = B * S
            mu = jnp.mean(x, axis=-1, keepdims=True)
            var = jnp.mean(jnp.square(x - mu), axis=-1, keepdims=True)
            xn = (x - mu) * jax.lax.rsqrt(var + LN_EPS) * ln_gamma + ln_beta
            xf = xn.reshape(N, D)
            slope_sign = jnp.sign(jnp.mean(spline_slopes, axis=-1))
            tile_sigs = jnp.zeros((NUM_TILES, D), dtype=x.dtype)
            tile_sigs = tile_sigs.at[jnp.arange(NUM_TILES)[:, None], DIMS].set(slope_sign)
            cluster_sigs = jnp.sign(tile_sigs.reshape(NUM_CLUSTERS, TILES_PER_CLUSTER, D).mean(axis=1))
            cluster_assign = jnp.arange(NUM_TILES, dtype=jnp.int32) // TILES_PER_CLUSTER
            input_sigs = jnp.sign(xf)
            cluster_scores = input_sigs @ cluster_sigs.T
            best_cluster = jnp.argmax(cluster_scores, axis=-1)
            tile_scores = input_sigs @ tile_sigs.T
            in_cluster = cluster_assign[None, :] == best_cluster[:, None]
            tile_idx = jnp.argmax(jnp.where(in_cluster, tile_scores, -jnp.inf), axis=-1)
            tok_dims = DIMS[tile_idx]
            x_slice = jnp.take_along_axis(xf, tok_dims, axis=1)
            tok_min = x_slice.min(axis=1)
            tok_max = x_slice.max(axis=1)
            onehot = tile_idx[None, :] == jnp.arange(NUM_TILES)[:, None]
            tile_min = jnp.where(onehot, tok_min[None, :], jnp.inf).min(axis=1)
            tile_max = jnp.where(onehot, tok_max[None, :], -jnp.inf).max(axis=1)
            mn = tile_min[tile_idx][:, None]
            mx = tile_max[tile_idx][:, None]
            u = jnp.clip((x_slice - mn) / (mx - mn + 1e-08), 0.0, 1.0 - 1e-06)
            gi = jnp.clip((u * GRID).astype(jnp.int32), 0, GRID - 1)
            j = jnp.arange(D_SLICE)[None, :]
            b = spline_bases[tile_idx[:, None], j, gi]
            s = spline_slopes[tile_idx[:, None], j, gi]
            x_local = (u - gi.astype(u.dtype) / GRID) * GRID
            delta = (b + s * x_local) * output_scale[tile_idx][:, None]
            out = jnp.zeros_like(xf).at[jnp.arange(N)[:, None], tok_dims].set(delta)
            return x + out.reshape(B, S, D)
        key = jax.random.key(seed)
        k1, k2, k3, k4, k5, k6 = jax.random.split(key, 6)
        x = jax.random.normal(k1, (4, 2048, D_MODEL), dtype=jnp.float32)
        ln_gamma = 1.0 + 0.1 * jax.random.normal(k2, (D_MODEL,), dtype=jnp.float32)
        ln_beta = 0.1 * jax.random.normal(k3, (D_MODEL,), dtype=jnp.float32)
        spline_bases = 0.1 * jax.random.normal(k4, (NUM_TILES, D_SLICE, GRID), dtype=jnp.float32)
        spline_slopes = 0.1 + 0.1 * jax.random.normal(k5, (NUM_TILES, D_SLICE, GRID), dtype=jnp.float32)
        output_scale = 1.0 + 0.1 * jax.random.normal(k6, (NUM_TILES,), dtype=jnp.float32)
        return {'x': x, 'ln_gamma': ln_gamma, 'ln_beta': ln_beta, 'spline_bases': spline_bases, 'spline_slopes': spline_slopes, 'output_scale': output_scale}
    _L0_ffn_in = _L0_ffn_setup()
    _d = {'L0_attn_hidden_states': _L0_attn_in['hidden_states'], 'L0_attn_conv_w': _L0_attn_in['conv_w'], 'L0_attn_conv_b': _L0_attn_in['conv_b'], 'L0_attn_in_proj_w': _L0_attn_in['in_proj_w'], 'L0_attn_ch_gate_w0': _L0_attn_in['ch_gate_w0'], 'L0_attn_ch_gate_w1': _L0_attn_in['ch_gate_w1'], 'L0_attn_ch_gate_b1': _L0_attn_in['ch_gate_b1'], 'L0_attn_mem_gate_w': _L0_attn_in['mem_gate_w'], 'L0_attn_mem_gate_b': _L0_attn_in['mem_gate_b'], 'L0_attn_residual_weight': _L0_attn_in['residual_weight'], 'L0_ffn_ln_gamma': _L0_ffn_in['ln_gamma'], 'L0_ffn_ln_beta': _L0_ffn_in['ln_beta'], 'L0_ffn_spline_bases': _L0_ffn_in['spline_bases'], 'L0_ffn_spline_slopes': _L0_ffn_in['spline_slopes'], 'L0_ffn_output_scale': _L0_ffn_in['output_scale']}
    _x0 = _d['L0_attn_hidden_states']
    _d['L0_attn_hidden_states'] = jax.random.normal(jax.random.fold_in(jax.random.key(seed), 1), (2, 4096, 1024), dtype=_x0.dtype)
    del _x0
    return _d

def reference(L0_attn_hidden_states, L0_attn_conv_w, L0_attn_conv_b, L0_attn_in_proj_w, L0_attn_ch_gate_w0, L0_attn_ch_gate_w1, L0_attn_ch_gate_b1, L0_attn_mem_gate_w, L0_attn_mem_gate_b, L0_attn_residual_weight, L0_ffn_ln_gamma, L0_ffn_ln_beta, L0_ffn_spline_bases, L0_ffn_spline_slopes, L0_ffn_output_scale):

    def _L0_attn_ref(hidden_states, conv_w, conv_b, in_proj_w, ch_gate_w0, ch_gate_w1, ch_gate_b1, mem_gate_w, mem_gate_b, residual_weight):
        import jax, jax.numpy as jnp
        import numpy as np
        B, L, D, M, R, W = (4, 1024, 1024, 64, 128, 4)
        SCALE = 1.0 / float(np.sqrt(M))
        NORM_EPS = 1e-12

        def _causal_depthwise_conv(x, w, b):
            xp = jnp.pad(x, ((0, 0), (W - 1, 0), (0, 0)))
            y = sum((xp[:, i:i + x.shape[1], :] * w[:, i] for i in range(W))) + b
            return jax.nn.silu(y)
        x = hidden_states
        shift = _causal_depthwise_conv(x, conv_w, conv_b)
        residual = shift
        rk = shift @ in_proj_w.T
        r, k = (rk[..., :M], rk[..., M:])
        ch = jax.nn.sigmoid(x @ ch_gate_w0.T @ ch_gate_w1.T + ch_gate_b1)
        u = ch * x
        mg = shift @ mem_gate_w.T + mem_gate_b
        sel = jax.nn.softplus(mg[..., :M])
        tau = jax.nn.sigmoid(mg[..., M:])
        it_gate = sel ** tau
        g = -sel * tau
        k = k / jnp.maximum(jnp.linalg.norm(k, axis=-1, keepdims=True), NORM_EPS)
        k = k * it_gate

        def step(S, inp):
            r_t, k_t, u_t, g_t = inp
            S = jnp.exp(g_t)[..., None] * S + k_t[..., None] * u_t[:, None, :]
            o_t = SCALE * jnp.einsum('bm,bmd->bd', r_t, S)
            return (S, o_t)
        xs = (jnp.swapaxes(r, 0, 1), jnp.swapaxes(k, 0, 1), jnp.swapaxes(u, 0, 1), jnp.swapaxes(g, 0, 1))
        S0 = jnp.zeros((x.shape[0], M, D), jnp.float32)
        _, o = jax.lax.scan(step, S0, xs)
        o = jnp.swapaxes(o, 0, 1)
        return o + residual * residual_weight

    def _L0_ffn_ref(x, ln_gamma, ln_beta, spline_bases, spline_slopes, output_scale):
        import jax, jax.numpy as jnp
        import numpy as np
        D_MODEL = 1024
        NUM_TILES = 64
        D_SLICE = D_MODEL // NUM_TILES
        TILES_PER_CLUSTER = 8
        NUM_CLUSTERS = NUM_TILES // TILES_PER_CLUSTER
        GRID = 16
        LN_EPS = 1e-05
        DIMS = (np.arange(NUM_TILES)[:, None] * D_SLICE + np.arange(D_SLICE)[None, :]) % D_MODEL
        DIMS = jnp.asarray(DIMS, dtype=jnp.int32)

        def _forward(x, ln_gamma, ln_beta, spline_bases, spline_slopes, output_scale):
            B, S, D = x.shape
            N = B * S
            mu = jnp.mean(x, axis=-1, keepdims=True)
            var = jnp.mean(jnp.square(x - mu), axis=-1, keepdims=True)
            xn = (x - mu) * jax.lax.rsqrt(var + LN_EPS) * ln_gamma + ln_beta
            xf = xn.reshape(N, D)
            slope_sign = jnp.sign(jnp.mean(spline_slopes, axis=-1))
            tile_sigs = jnp.zeros((NUM_TILES, D), dtype=x.dtype)
            tile_sigs = tile_sigs.at[jnp.arange(NUM_TILES)[:, None], DIMS].set(slope_sign)
            cluster_sigs = jnp.sign(tile_sigs.reshape(NUM_CLUSTERS, TILES_PER_CLUSTER, D).mean(axis=1))
            cluster_assign = jnp.arange(NUM_TILES, dtype=jnp.int32) // TILES_PER_CLUSTER
            input_sigs = jnp.sign(xf)
            cluster_scores = input_sigs @ cluster_sigs.T
            best_cluster = jnp.argmax(cluster_scores, axis=-1)
            tile_scores = input_sigs @ tile_sigs.T
            in_cluster = cluster_assign[None, :] == best_cluster[:, None]
            tile_idx = jnp.argmax(jnp.where(in_cluster, tile_scores, -jnp.inf), axis=-1)
            tok_dims = DIMS[tile_idx]
            x_slice = jnp.take_along_axis(xf, tok_dims, axis=1)
            tok_min = x_slice.min(axis=1)
            tok_max = x_slice.max(axis=1)
            onehot = tile_idx[None, :] == jnp.arange(NUM_TILES)[:, None]
            tile_min = jnp.where(onehot, tok_min[None, :], jnp.inf).min(axis=1)
            tile_max = jnp.where(onehot, tok_max[None, :], -jnp.inf).max(axis=1)
            mn = tile_min[tile_idx][:, None]
            mx = tile_max[tile_idx][:, None]
            u = jnp.clip((x_slice - mn) / (mx - mn + 1e-08), 0.0, 1.0 - 1e-06)
            gi = jnp.clip((u * GRID).astype(jnp.int32), 0, GRID - 1)
            j = jnp.arange(D_SLICE)[None, :]
            b = spline_bases[tile_idx[:, None], j, gi]
            s = spline_slopes[tile_idx[:, None], j, gi]
            x_local = (u - gi.astype(u.dtype) / GRID) * GRID
            delta = (b + s * x_local) * output_scale[tile_idx][:, None]
            out = jnp.zeros_like(xf).at[jnp.arange(N)[:, None], tok_dims].set(delta)
            return x + out.reshape(B, S, D)
        return _forward(x, ln_gamma, ln_beta, spline_bases, spline_slopes, output_scale)
    x = L0_attn_hidden_states
    x = _layernorm(x + _L0_attn_ref(x, L0_attn_conv_w, L0_attn_conv_b, L0_attn_in_proj_w, L0_attn_ch_gate_w0, L0_attn_ch_gate_w1, L0_attn_ch_gate_b1, L0_attn_mem_gate_w, L0_attn_mem_gate_b, L0_attn_residual_weight), axis=-1)
    x = _layernorm(x + _L0_ffn_ref(x, L0_ffn_ln_gamma, L0_ffn_ln_beta, L0_ffn_spline_bases, L0_ffn_spline_slopes, L0_ffn_output_scale), axis=-1)
    return x

_drawn_inputs = setup_inputs


def setup_inputs(seed=0):
    import zlib

    import numpy as np

    out = dict(_drawn_inputs(seed))
    spreads = {'L0_attn_conv_b': (0.0, 0.1),
     'L0_attn_ch_gate_b1': (0.0, 0.8),
     'L0_attn_residual_weight': (1.0, 0.6)}
    factors = {'L0_attn_in_proj_w': 8.0,
     'L0_attn_ch_gate_w0': 8.0,
     'L0_attn_ch_gate_w1': 8.0,
     'L0_attn_mem_gate_w': 8.0,
     'L0_attn_mem_gate_b': 8.0,
     'L0_ffn_ln_gamma': 8.0,
     'L0_ffn_ln_beta': 7.918,
     'L0_ffn_spline_bases': 8.0,
     'L0_ffn_spline_slopes': 8.0,
     'L0_ffn_output_scale': 8.0}
    for name, (base, spread) in spreads.items():
        noise = np.random.default_rng([zlib.crc32(name.encode()), seed]).standard_normal(out[name].shape)
        drawn = base * np.exp(spread * noise) if base else spread * noise
        out[name] = jnp.asarray(drawn.astype(out[name].dtype))
    for name, factor in factors.items():
        out[name] = (out[name] * factor).astype(out[name].dtype)
    return out
```

```python
from contextlib import ExitStack

import concourse.bass as bass
from concourse import mybir

ALU = mybir.AluOpType
ACT = mybir.ActivationFunctionType
F32 = mybir.dt.float32
BF16 = mybir.dt.bfloat16
U32 = mybir.dt.uint32
AX_X = mybir.AxisListType.X

P = 128
CH = 128
CPG = 2
T = CH * CPG
LEVELS = 7
HIST = 3
SLOTS = 5
SEL_MIN = 2.0 ** -60
SS_SCALE = 2.0 ** 20
BIG = 1e30
ATANH = (2.0000000078699283, 0.6666631600410559, 0.40024852291048835, 0.27961426376095516, 0.2817466568891232)
MAGIC = float(2 ** 23)
LN_EPS = 1e-5


class Event:

    def __init__(self, sem, per_group):
        self.sem, self.per_group = sem, per_group

    def at(self, g, i=0):
        return g * self.per_group + (i + 1)


def build(nc, x, w_rk, w_mg, w0, w1, conv_w, conv_b, gate_b1, mem_b, res_w, gamma, beta, bases, slopes, oscale, out):
    B, L, D = x.shape
    M = 64
    R = w0.shape[2]
    W = conv_w.shape[2]
    NB = D // P
    NG = B * L // T
    NC = B * L // CH
    NT = bases.shape[0]
    DS = D // NT
    GRID = bases.shape[2]
    NCL = 8
    TPC = NT // NCL
    HALF = 512
    NLV = LEVELS * (CH // 2)
    assert W == HIST + 1 and R == P and D == 2 * HALF and NG % 2 == 0 and NG >= 4
    R_SCALE = 0.5 / float(M) ** 0.5

    x_g = x.rearrange("b l d -> (b l) d").rearrange("(g c p) d -> g p c d", c=CPG, p=P)
    out_g = out.rearrange("b l d -> (b l) d").rearrange("(g c p) d -> g p c d", c=CPG, p=P)
    y_dram = nc.dram_tensor("y_scratch", (B * L, D), F32, kind="Internal").ap()
    y_g = y_dram.rearrange("(g c p) d -> g p c d", c=CPG, p=P)
    y_slices = y_dram.rearrange("n (t j) -> (n t) j", j=DS)
    out_slices = out.rearrange("b l d -> (b l) d").rearrange("n (t j) -> (n t) j", j=DS)

    with ExitStack() as whole:
        def sbw(name, shape, dt=F32):
            return whole.enter_context(nc.sbuf_tensor(name, shape, dt))

        ident = sbw("ident", [P, P])
        iota_t = sbw("iota_t", [P, NT])
        minus_half = sbw("minus_half", [P, CPG])
        nm_all = sbw("nm_all", [P, NC])
        r1_all = sbw("r1_all", [P, NC])
        r12_all = sbw("r12_all", [P, NC])
        ss_all = sbw("ss_all", [P, NC])
        idx_all = sbw("idx_all", [P, NC])
        with ExitStack() as ctx:
            def sb(name, shape, dt=F32):
                return ctx.enter_context(nc.sbuf_tensor(name, shape, dt))

            def psum(name, shape, dt=F32):
                return ctx.enter_context(nc.psum_tensor(name, shape, dt))

            def sem(name):
                return ctx.enter_context(nc.semaphore(name))

            def ev(name, per_group):
                return Event(sem(name), per_group)

            w_rk_sb = sb("w_rk_sb", [P, NB, P])
            w_mg_sb = sb("w_mg_sb", [P, NB, P])
            w0_sb = sb("w0_sb", [P, NB, R])
            w1_sb = sb("w1_sb", [P, D])
            cw_sb = sb("cw_sb", [P, NB, W])
            cb_sb = sb("cb_sb", [P, NB])
            rw_sb = sb("rw_sb", [P, NB])
            mb_sb = sb("mb_sb", [P, 2])
            b1_split = sb("b1_split", [96, D], BF16)
            gam = sb("gam", [P, D])
            bet = sb("bet", [P, D])
            ones = sb("ones", [P, T])
            ones_bf = sb("ones_bf", [96, P], BF16)
            mask = sb("mask", [P, LEVELS, CH // 2])
            keep = sb("keep", [P, NG])
            ln_fix = sb("ln_fix", [P, 1])
            TWO, MINUS_1_D, ONE_D, EPS = range(4)
            consts = sb("consts", [P, 4])
            c_tile = sb("c_tile", [P, NT])
            c_cluster = sb("c_cluster", [P, NCL])

            xin = [sb(f"xin{i}", [P, CPG, D]) for i in range(2)]
            xT = [sb(f"xT{i}", [P, NB, HIST + T]) for i in range(2)]
            acc = [sb(f"acc{i}", [P, NB, T]) for i in range(2)]
            shT = sb("shT", [P, NB, T])
            tS = [sb(f"tS{i}", [P, T]) for i in range(2)]
            rr = sb("rr", [P, T])
            kk = sb("kk", [M, T])
            xs = sb("xs", [M, T])
            xa = sb("xa", [M, T])
            ge = sb("ge", [M, T])
            gw = sb("gw", [M, T])
            gl = sb("gl", [M, T])
            gw1 = sb("gw1", [M, T])
            grw = sb("grw", [M, T])
            sel = sb("sel", [M, T])
            lsel = sb("lsel", [M, T])
            gen = sb("gen", [M, T])
            tau = sb("tau", [M, T])
            gn = sb("gn", [M, T])
            tl = sb("tl", [M, T])
            ksq = sb("ksq", [M, T])
            nl = sb("nl", [M, T])
            kg = sb("kg", [M, T])
            kn = sb("kn", [P, T])
            bb = sb("bb", [P, T])
            rkp = sb("rkp", [M, T])
            X = sb("X", [P, SLOTS, T])
            E = sb("E", [P, SLOTS, T])
            RE = sb("RE", [P, SLOTS, T])
            KE = sb("KE", [P, SLOTS, T])
            keT_sb = sb("keT_sb", [P, CPG, M])
            Wm = sb("Wm", [P, LEVELS, CH // 2])
            AT = [sb(f"AT{i}", [P, CH]) for i in range(2)]
            th = [sb(f"th{i}", [P, D]) for i in range(2)]
            S = [sb(f"S{i}", [M, D]) for i in range(2)]
            y = [sb(f"y{i}", [P, CPG, D]) for i in range(2)]
            qb = sb("qb", [P, D])
            xf = [sb(f"xf{i}", [P, D]) for i in range(2)]
            sg = sb("sg", [P, CPG, D], BF16)
            ysum = sb("ysum", [P, CPG])
            nm = [sb(f"nm{i}", [P, CPG]) for i in range(2)]
            ssm = sb("ssm", [P, CPG])
            st = sb("st", [P, 6, CPG])
            ts = sb("ts", [P, CPG, NT])
            cl = sb("cl", [P, CPG, NCL])
            key = sb("key", [P, CPG, NT])
            kmax = sb("kmax", [P, CPG])
            tidx = sb("tidx", [P, CPG])

            TX = psum("TX", [P, HALF])
            PR = psum("PR", [P, HALF])
            GA = psum("GA", [P, HALF])
            AB = psum("AB", [P, HALF])
            WK = [psum(f"WK{i}", [P, HALF]) for i in range(2)]
            OB = psum("OB", [P, 2 * HALF])

            s_w = sem("s_w")
            s_sl = [sem(f"s_sl{i}") for i in range(2)]
            s_slr = sem("s_slr")
            s_c = sem("s_c")
            s_cv = sem("s_cv")
            s_ss = sem("s_ss")
            s_setup = sem("s_setup")
            s_pc = sem("s_pc")
            d_xin = [sem(f"d_xin{i}") for i in range(2)]
            d_yst = [sem(f"d_yst{i}") for i in range(2)]
            e_xtr, e_xev, e_hist = ev("e_xtr", 4), ev("e_xev", 4), ev("e_hist", 1)
            e_t, e_tev = ev("e_t", 1), ev("e_tev", 1)
            e_conv, e_silu, e_proj, e_res = ev("e_conv", NB * W), ev("e_silu", 2), ev("e_proj", 1), ev("e_res", NB)
            e_pr = ev("e_pr", 5)
            e_xa, e_ge, e_gw, e_gl, e_gw1, e_grw = (ev(n, 1) for n in ("e_xa", "e_ge", "e_gw", "e_gl", "e_gw1", "e_grw"))
            e_lg, e_sel, e_sc, e_ls, e_l2 = (ev(n, 1) for n in ("e_lg", "e_sel", "e_sc", "e_ls", "e_l2"))
            e_d, e_tau, e_gn, e_tl, e_b, e_bd = (ev(n, 1) for n in ("e_d", "e_tau", "e_gn", "e_tl", "e_b", "e_bd"))
            e_ks, e_ssq, e_n1, e_n2, e_ex, e_kg = (ev(n, 1) for n in ("e_ks", "e_ssq", "e_n1", "e_n2", "e_ex", "e_kg"))
            e_kn, e_kd, e_X, e_Ek, e_RE, e_KE, e_rkp = (
                ev(n, 1) for n in ("e_kn", "e_kd", "e_X", "e_Ek", "e_RE", "e_KE", "e_rkp"))
            e_E, e_gq = ev("e_E", 3), ev("e_gq", 4)
            e_keT, e_keTe = ev("e_keT", 1), ev("e_keTe", 1)
            e_c2, e_th, e_u = ev("e_c2", 4), ev("e_th", 4), ev("e_u", 2)
            e_Ah, e_Xl = ev("e_Ah", 2), ev("e_Xl", 1)
            e_A, e_Wm, e_at0, e_AT = ev("e_A", 2), ev("e_Wm", 2), ev("e_at0", 2), ev("e_AT", 2 * LEVELS)
            e_o, e_su, e_S, e_y = ev("e_o", 2), ev("e_su", 4), ev("e_S", 4), ev("e_y", 2)
            e_nm, e_sq, e_st = ev("e_nm", 2), ev("e_sq", 2), ev("e_st", 9)
            e_q, e_xf, e_sg = ev("e_q", 2), ev("e_xf", 2), ev("e_sg", 2)
            e_sc8, e_keep = ev("e_sc8", 8), ev("e_keep", 4)

            def wait(eng, e, g, i=0):
                eng.wait_ge(e.sem, e.at(g, i))

            def const(k, rows, n):
                return consts[0:rows, k:k + 1].to_broadcast([rows, n])

            def dma_at(g, p):
                return (g - p) * 8 + 16

            def level_halves(v, h):
                b = v.rearrange("p (n s h) -> p n s h", s=2, h=h)
                return b[:, :, 0, :], b[:, :, 1, :]

            def level_rows(l):
                return slice(0, M) if l % 2 == 0 else slice(M, P)

            def pipeline(eng, step):
                step(0, 0, True, False, False)
                step(1, 1, True, True, False)
                step(2, 0, True, True, True)
                step(3, 1, True, True, True)
                with eng.Fori(2, NG // 2) as pair:
                    step(pair * 2, 0, True, True, True)
                    step(pair * 2 + 1, 1, True, True, True)
                step(NG, 0, False, True, True)
                step(NG + 1, 1, False, False, True)

            block = ctx.enter_context(nc.Block())

            N_W = 13
            SLQ = 4
            sl_tmp = [xin[i] for i in range(2)]

            @block.sync
            def _(sp):
                for dst, src in (
                    (w_rk_sb[:], w_rk), (w_mg_sb[:], w_mg), (w0_sb[:], w0), (w1_sb[:], w1),
                    (cw_sb[:], conv_w), (cb_sb[:], conv_b), (rw_sb[:], res_w), (mb_sb[:, 0:1], mem_b),
                    (gam[:], gamma.partition_broadcast(P)), (bet[:], beta.partition_broadcast(P)),
                    (qb[0:1, :], gate_b1), (qb[32:33, :], gate_b1), (qb[64:65, :], gate_b1),
                ):
                    sp.dma_start(dst, src).then_inc(s_w, 16)
                sl = slopes.rearrange("t j g -> (t j g)").rearrange("(q n) -> q n", n=CPG * D)
                for q in range(D * GRID // (CPG * D)):
                    if q >= 2:
                        sp.wait_ge(s_slr, q - 1)
                    sp.dma_start(sl_tmp[q % 2][:].rearrange("p c d -> p (c d)"),
                                 sl[q].partition_broadcast(P)).then_inc(s_sl[q % 2], 16)
                sp.wait_ge(s_slr, D * GRID // (CPG * D))

                def step(g, p, front, mid, back):
                    if front:
                        if not (isinstance(g, int) and g < 2):
                            wait(sp, e_xtr, g - 2, 3)
                            wait(sp, e_u, g - 2, 1)
                        sp.dma_start(xin[p][:], x_g[bass.ds(g, 1)].rearrange("g p c d -> (g p) c d")
                                     if not isinstance(g, int) else x_g[g]).then_inc(d_xin[p], 16)
                    if back:
                        b = g - 2
                        wait(sp, e_y, b, 1)
                        dst = y_g[b] if isinstance(b, int) else y_g[bass.ds(b, 1)].rearrange("g p c d -> (g p) c d")
                        sp.dma_start(dst, y[p][:]).then_inc(d_yst[p], 16)

                pipeline(sp, step)
                for p in range(2):
                    sp.wait_ge(d_yst[p], NG // 2 * 16)

            @block.tensor
            def _(pe):
                pe.wait_ge(s_w, 16 * N_W)
                pe.wait_ge(s_c, 2)
                pe.wait_ge(s_cv, 1)

                def step(g, p, front, mid, back):
                    m = g - 1
                    first = isinstance(g, int) and g == 0
                    if mid:
                        wait(pe, e_ks, m)
                        if not (isinstance(m, int) and m == 0):
                            wait(pe, e_keTe, m - 1)
                        wait(pe, e_tev, m)
                        pe.matmul(GA[:, T:2 * T], ones[0:M, 0:P], ksq[:], start=True, stop=True).then_inc(e_ssq.sem, 1)
                    if front:
                        pe.wait_ge(d_xin[p], dma_at(g, p))

                        def fill(f):
                            if f > 0:
                                wait(pe, e_xev, g, f - 1)
                            elif not first:
                                wait(pe, e_xev, g - 1, 3)
                            for k in range(4):
                                b, c = 2 * f + k // 2, k % 2
                                i = pe.transpose(TX[:, (b % 2) * T + c * P:(b % 2) * T + (c + 1) * P],
                                                 xin[p][:, c, b * P:(b + 1) * P], ident[:])
                            i.then_inc(e_xtr.sem, 1)

                        def t_blocks(f):
                            wait(pe, e_xev, g, f)
                            if f == 0 and mid:
                                wait(pe, e_n1, m)
                            for b in (2 * f, 2 * f + 1):
                                i = pe.matmul(GA[:, 0:T], w0_sb[:, b, :], xT[p][:, b, HIST:HIST + T],
                                              start=(b == 0), stop=(b == NB - 1))
                            if f == 3:
                                i.then_inc(e_t.sem, 1)

                        fill(0)
                        for f in range(1, 4):
                            fill(f)
                            t_blocks(f - 1)
                        t_blocks(3)
                    if mid:
                        for i in range(4):
                            c, h = i // 2, i % 2
                            if i == 0:
                                wait(pe, e_tev, m)
                            if i >= 2:
                                wait(pe, e_th, m, i - 2)
                            elif not (isinstance(m, int) and m == 0):
                                wait(pe, e_S, m - 1, i + 2)
                            cols = slice(h * HALF, (h + 1) * HALF)
                            pe.matmul(WK[h][:], tS[1 - p][:, c * P:(c + 1) * P], w1_sb[:, cols], start=True, stop=False)
                            pe.matmul(WK[h][:], ones_bf[:], b1_split[:, cols], start=False, stop=True).then_inc(e_c2.sem, 1)

                        def scores(c):
                            if c == 0:
                                wait(pe, e_RE, m)
                                wait(pe, e_KE, m)
                                wait(pe, e_rkp, m)
                                wait(pe, e_n1, m)
                                if front:
                                    wait(pe, e_tev, g)
                                if not (isinstance(m, int) and m == 0):
                                    wait(pe, e_at0, m - 1, 1)
                            else:
                                wait(pe, e_at0, m, c - 1)
                            tok = slice(c * CH, (c + 1) * CH)
                            for l in (*range(1, LEVELS, 2), *range(0, LEVELS, 2)):
                                rows = level_rows(l)
                                if l == 0:
                                    wait(pe, e_Ah, m, c)
                                later = level_halves(RE[rows, l // 2, tok], 2 ** l)[1]
                                i = pe.matmul(AB[:, l * 64:(l + 1) * 64], KE[rows, l // 2, tok], later,
                                              start=True, stop=True)
                                if l == LEVELS - 2:
                                    i.then_inc(e_Ah.sem, 1)
                            pe.matmul(AB[:, NLV:NLV + 2], rkp[:, tok], ones[0:M, 0:2], start=True, stop=True)\
                              .then_inc(e_A.sem, 1)

                        def k_turned():
                            for c in range(CPG):
                                i = pe.transpose(GA[:, T + c * M:T + (c + 1) * M],
                                                 KE[M:P, SLOTS - 1, c * CH:(c + 1) * CH], ident[M:P, M:P])
                            i.then_inc(e_keT.sem, 1)

                        def output(c):
                            if c == 0:
                                wait(pe, e_res, m, NB - 1)
                                if not (isinstance(m, int) and m == 0):
                                    wait(pe, e_y, m - 1, 1)
                                    wait(pe, e_S, m - 1, 3)
                            else:
                                wait(pe, e_y, m, 0)
                                wait(pe, e_S, m, 1)
                            wait(pe, e_AT, m, c * LEVELS + LEVELS - 1)
                            wait(pe, e_u, m, c)
                            tok = slice(c * CH, (c + 1) * CH)
                            for h in range(2):
                                cols = slice(h * HALF, (h + 1) * HALF)
                                pe.matmul(OB[:, cols], AT[c][:], th[c][:, cols], start=True, stop=False)
                                pe.matmul(OB[:, cols], RE[0:M, SLOTS - 1, tok], S[c][:, cols], start=False, stop=False)
                                for j in range(4):
                                    b = 4 * h + j
                                    i = pe.matmul(OB[:, b * P:(b + 1) * P], acc[1 - p][:, b, tok], ident[:],
                                                  is_transpose=True, start=False, stop=(j == 3))
                            i.then_inc(e_o.sem, 1)

                        def state(c):
                            for h in range(2):
                                if c == 0:
                                    wait(pe, e_th, m, 2 + h)
                                    if h == 0:
                                        wait(pe, e_keTe, m)
                                else:
                                    wait(pe, e_S, m, h)
                                pe.matmul(WK[h][0:M, :], keT_sb[:, c, :], th[c][:, h * HALF:(h + 1) * HALF],
                                          start=True, stop=True).then_inc(e_su.sem, 1)

                        scores(0)
                        k_turned()
                        output(0)
                        state(0)
                        scores(1)
                        output(1)
                        state(1)
                    if front:
                        if not first:
                            wait(pe, e_pr, m, 4)
                        for half in range(2):
                            for b in range(NB):
                                if half == 0 and b % 4 == 0:
                                    wait(pe, e_silu, g, b // 4)
                                w = w_rk_sb if half == 0 else w_mg_sb
                                i = pe.matmul(PR[:, half * T:(half + 1) * T], w[:, b, :], shT[:, b, :],
                                              start=(b == 0), stop=(b == NB - 1))
                        i.then_inc(e_proj.sem, 1)

                pipeline(pe, step)

            @block.scalar
            def _(act):
                act.wait_ge(s_w, 16 * N_W)
                act.wait_ge(s_c, 2)
                act.wait_ge(s_slr, D * GRID // (CPG * D))
                nc.scalar.activation(th[0][:], th[1][:], ACT.Sign).then_inc(s_ss, 1)

                def step(g, p, front, mid, back):
                    m, b = g - 1, g - 2

                    def x_out(f):
                        if not front:
                            return
                        wait(act, e_xtr, g, f)
                        if f == 0 and not (isinstance(g, int) and g < 2):
                            wait(act, e_conv, g - 2, NB * W - 1)
                            wait(act, e_res, g - 2, NB - 1)
                            wait(act, e_t, g - 2)
                        if f == 0 and not (isinstance(g, int) and g < 1):
                            wait(act, e_hist, g - 1)
                        nc.scalar.activation(xT[p][:, 2 * f:2 * f + 2, HIST:HIST + T],
                                             TX[:].rearrange("p (b t) -> p b t", b=2), ACT.Copy).then_inc(e_xev.sem, 1)

                    if mid:
                        wait(act, e_proj, m)
                        if not (isinstance(m, int) and m == 0):
                            wait(act, e_RE, m - 1)
                            wait(act, e_rkp, m - 1)
                            wait(act, e_kn, m - 1)
                            wait(act, e_l2, m - 1)
                            wait(act, e_d, m - 1)
                        nc.scalar.activation(kk[:], PR[M:P, 0:T], ACT.Copy).then_inc(e_pr.sem, 1)
                        nc.scalar.activation(xs[:], PR[0:M, T:2 * T], ACT.Identity, bias=mb_sb[0:M, 0:1])\
                            .then_inc(e_pr.sem, 1)
                        nc.scalar.activation(gen[:], PR[M:P, T:2 * T], ACT.Exp, scale=-1.0, bias=mb_sb[M:P, 1:2])\
                            .then_inc(e_pr.sem, 1)
                        nc.scalar.activation(rr[0:M, :], PR[0:M, 0:T], ACT.Copy, scale=R_SCALE).then_inc(e_pr.sem, 1)
                        nc.scalar.activation(rr[M:P, :], PR[0:M, 0:T], ACT.Copy, scale=R_SCALE).then_inc(e_pr.sem, 1)
                        wait(act, e_pr, m, 1)
                        if not (isinstance(m, int) and m == 0):
                            wait(act, e_lg, m - 1)
                        nc.scalar.activation(xa[:], xs[:], ACT.Abs).then_inc(e_xa.sem, 1)
                        wait(act, e_xa, m)
                        nc.scalar.activation(ge[:], xa[:], ACT.Exp, scale=-1.0).then_inc(e_ge.sem, 1)
                    if back:
                        for c in range(CPG):
                            wait(act, e_nm, b, c)
                            if not (isinstance(b, int) and b == 0):
                                wait(act, e_sc8, b - 1, 0)
                            nc.scalar.activation(sg[:, c, :], y[p][:, c, :], ACT.Square, bias=nm[p][:, c:c + 1],
                                                 accum_out=ssm[:, c:c + 1]).then_inc(e_sq.sem, 1)
                    x_out(0)
                    x_out(1)
                    if mid:
                        wait(act, e_n1, m)
                        nc.scalar.activation(nl[:], nl[:], ACT.Ln).then_inc(e_n2.sem, 1)
                    x_out(2)
                    x_out(3)
                    if mid:
                        wait(act, e_sc, m)
                        nc.scalar.activation(lsel[:], gl[:], ACT.Ln).then_inc(e_ls.sem, 1)
                        wait(act, e_b, m)
                        nc.scalar.activation(bb[M:P, :], bb[0:M, :], ACT.Copy).then_inc(e_bd.sem, 1)
                    if front:
                        wait(act, e_t, g)
                        if mid and not (isinstance(g, int) and g < 2):
                            wait(act, e_c2, g - 2, 3)
                        nc.scalar.activation(tS[p][:], GA[:, 0:T], ACT.Copy).then_inc(e_tev.sem, 1)
                    if mid:
                        wait(act, e_ex, m)
                        nc.scalar.activation(kg[:], nl[:], ACT.Exp, bias=ln_fix[0:M, :]).then_inc(e_kg.sem, 1)
                        wait(act, e_kn, m)
                        nc.scalar.activation(kn[M:P, :], kn[0:M, :], ACT.Copy).then_inc(e_kd.sem, 1)
                        wait(act, e_X, m)
                        if not (isinstance(m, int) and m == 0):
                            wait(act, e_KE, m - 1)
                            wait(act, e_S, m - 1, 3)
                        nc.scalar.activation(E[:, 0:4, :], X[:, 0:4, :], ACT.Exp).then_inc(e_E.sem, 1)
                        nc.scalar.activation(E[0:M, 4, :], bb[0:M, :], ACT.Exp).then_inc(e_E.sem, 1)
                        nc.scalar.activation(E[M:P, 4, :], X[M:P, 4, :], ACT.Exp).then_inc(e_E.sem, 1)
                        for i in range(4):
                            c, h = i // 2, i % 2
                            wait(act, e_c2, m, i)
                            if not (isinstance(m, int) and m == 0):
                                wait(act, e_su, m - 1, 2 * c + 1)
                            nc.scalar.activation(th[c][:, h * HALF:(h + 1) * HALF], WK[h][:], ACT.Tanh, scale=0.5)\
                                .then_inc(e_th.sem, 1)
                    if front:
                        for h in range(2):
                            bs = slice(h * NB // 2, (h + 1) * NB // 2)
                            wait(act, e_conv, g, NB * W // 2 * (h + 1) - 1)
                            if not (isinstance(g, int) and g == 0):
                                wait(act, e_proj, g - 1)
                                wait(act, e_res, g - 1, NB - 1)
                            nc.scalar.activation(shT[:, bs, :], acc[p][:, bs, :], ACT.Silu).then_inc(e_silu.sem, 1)
                    if back:
                        for c in range(CPG):
                            wait(act, e_xf, b, c)
                            wait(act, e_sq, b, c)
                            nc.scalar.activation(sg[:, c, :], xf[c][:], ACT.Sign).then_inc(e_sg.sem, 1)
                    if mid:
                        wait(act, e_keT, m)
                        nc.scalar.activation(keT_sb[:], GA[:, T:T + CPG * M].rearrange("p (c m) -> p c m", c=CPG),
                                             ACT.Copy).then_inc(e_keTe.sem, 1)
                        for c in range(CPG):
                            wait(act, e_o, m, c)
                            if c == 0 and not (isinstance(m, int) and m < 2):
                                act.wait_ge(d_yst[1 - p], dma_at(m - 2, 1 - p))
                                wait(act, e_q, m - 2, 1)
                                wait(act, e_sq, m - 2, 1)
                            if c == 0 and not (isinstance(m, int) and m < 1):
                                wait(act, e_nm, m - 1, 1)
                            nc.scalar.activation(y[1 - p][:, c, :], OB[:], ACT.Identity,
                                                 accum_out=ysum[:, c:c + 1]).then_inc(e_y.sem, 1)

                pipeline(act, step)

            @block.vector
            def _(dve):
                v = nc.vector
                for q in range(D * GRID // (CPG * D)):
                    n = CPG * D // GRID
                    dve.wait_ge(s_sl[q % 2], 16 * (q // 2 + 1))
                    v.tensor_reduce(th[1][:, q * n:(q + 1) * n],
                                    sl_tmp[q % 2][:].rearrange("p c (d g) -> p (c d) g", g=GRID), AX_X, ALU.add)\
                        .then_inc(s_slr, 1)
                dve.wait_ge(s_w, 16 * N_W)
                dve.wait_ge(s_c, 2)
                v.tensor_scalar(mb_sb[:, 1:2], mb_sb[:, 0:1], -1.0, None, ALU.mult).then_inc(s_cv, 1)

                chain = [0]
                s_chain = s_setup

                def link(ins):
                    chain[0] += 1
                    ins.then_inc(s_chain, 1)
                    dve.wait_ge(s_chain, chain[0])

                bt = y[0][:].rearrange("p c d -> p (c d)")
                link(v.memset(b1_split[:], 0.0))
                for row, parts in ((0, 1), (32, 2), (64, 3)):
                    rest = qb[row:row + 1, :]
                    part = sg[row:row + 1, 0, :]
                    for k in range(parts):
                        if k:
                            link(v.tensor_tensor(rest, rest, part, ALU.subtract))
                        link(v.tensor_copy(part if k < parts - 1 else b1_split[row:row + 1, :], rest))
                dve.wait_ge(s_ss, 1)
                link(v.tensor_tensor(gam[:], gam[:], th[0][:], ALU.mult))
                link(v.tensor_tensor(bet[:], bet[:], th[0][:], ALU.mult))
                link(v.memset(S[0][:], 0.0))
                link(v.memset(xT[0][:, :, 0:HIST], 0.0))

                def step(g, p, front, mid, back):
                    m, b = g - 1, g - 2
                    not_first_m = not (isinstance(m, int) and m == 0)
                    todo = []

                    if back:
                        def affine(c):
                            wait(dve, e_y, b, c)
                            wait(dve, e_nm, b, c)
                            if c == 1:
                                wait(dve, e_xf, b, 0)
                            elif not (isinstance(b, int) and b == 0):
                                wait(dve, e_xf, b - 1, 1)
                            v.scalar_tensor_tensor(qb[:], y[p][:, c, :], nm[p][:, c:c + 1], gam[:], ALU.add, ALU.mult)\
                                .then_inc(e_q.sem, 1)
                            wait(dve, e_q, b, c)
                            wait(dve, e_st, b, 8)
                            if not (isinstance(b, int) and b == 0):
                                wait(dve, e_sg, b - 1, c)
                            v.scalar_tensor_tensor(xf[c][:], qb[:], st[:, 5, c:c + 1], bet[:], ALU.mult, ALU.add)\
                                .then_inc(e_xf.sem, 1)

                    def conv_round(h, i):
                        for j in range(NB // 2):
                            blk = h * (NB // 2) + j
                            n = (h * W + i) * (NB // 2) + j
                            src = xT[p][:, blk, i:i + T]
                            wt = cw_sb[:, blk, i:i + 1]
                            if i == 0:
                                if j == 0:
                                    wait(dve, e_xev, g, 2 * h + 1)
                                    wait(dve, e_hist, g)
                                    if not (isinstance(g, int) and g < 2):
                                        wait(dve, e_o, g - 2, 1)
                                v.tensor_scalar(acc[p][:, blk, :], src, wt, cb_sb[:, blk:blk + 1], ALU.mult, ALU.add)\
                                    .then_inc(e_conv.sem, 1)
                            else:
                                wait(dve, e_conv, g, n - NB // 2)
                                v.scalar_tensor_tensor(acc[p][:, blk, :], src, wt, acc[p][:, blk, :], ALU.mult, ALU.add)\
                                    .then_inc(e_conv.sem, 1)

                    def history():
                        if not (isinstance(g, int) and g == 0):
                            wait(dve, e_xev, g - 1, 3)
                            if not (isinstance(g, int) and g < 2):
                                wait(dve, e_conv, g - 2, NB * W - 1)
                            k = keep[:, g:g + 1] if isinstance(g, int) else keep[:, bass.ds(g, 1)]
                            v.tensor_scalar(xT[p][:, :, 0:HIST], xT[1 - p][:, :, T:T + HIST], k, None, ALU.mult)\
                                .then_inc(e_hist.sem, 1)
                        else:
                            v.memset(xT[p][:, :, 0:HIST], 0.0).then_inc(e_hist.sem, 1)

                    if front:
                        history()
                    if mid:
                        wait(dve, e_gw, m)
                        v.reciprocal(grw[:], gw[:]).then_inc(e_grw.sem, 1)
                    if back:
                        affine(0)
                    if mid:
                        wait(dve, e_d, m)
                        if not_first_m:
                            wait(dve, e_tl, m - 1)
                        v.reciprocal(tau[:], gen[:]).then_inc(e_tau.sem, 1)
                        wait(dve, e_gl, m)
                        v.tensor_scalar(grw[:], gl[:], ATANH[4], None, ALU.mult).then_inc(e_gq.sem, 1)
                        for k in (3, 2, 1):
                            wait(dve, e_gq, m, 3 - k)
                            v.scalar_tensor_tensor(grw[:], grw[:], ATANH[k], gl[:], ALU.add, ALU.mult)\
                                .then_inc(e_gq.sem, 1)
                        wait(dve, e_gq, m, 3)
                        v.scalar_tensor_tensor(grw[:], grw[:], ATANH[0], gw1[:], ALU.add, ALU.mult).then_inc(e_lg.sem, 1)
                        wait(dve, e_lg, m)
                        v.scalar_tensor_tensor(sel[:], xs[:], 0.0, grw[:], ALU.max, ALU.add).then_inc(e_sel.sem, 1)
                        wait(dve, e_sel, m)
                        v.tensor_scalar(gl[:], sel[:], SEL_MIN, None, ALU.max).then_inc(e_sc.sem, 1)
                        wait(dve, e_ssq, m)
                        v.tensor_scalar(nl[:], GA[0:M, T:2 * T], SS_SCALE, 1e-24 * SS_SCALE, ALU.mult, ALU.max)\
                            .then_inc(e_n1.sem, 1)
                    if back:
                        affine(1)
                    if mid:
                        wait(dve, e_gn, m)
                        if not_first_m:
                            wait(dve, e_X, m - 1)
                            wait(dve, e_E, m - 1, 1)
                            wait(dve, e_bd, m - 1)
                        for c in range(CPG):
                            tok = slice(c * CH, (c + 1) * CH)
                            i = v.tensor_tensor_scan(bb[0:M, tok], ones[0:M, 0:CH], gn[:, tok], 0.0, ALU.mult, ALU.subtract)
                        i.then_inc(e_b.sem, 1)
                    if front:
                        conv_round(0, 0)
                    if mid:
                        wait(dve, e_ls, m)
                        v.tensor_tensor(lsel[:], lsel[:], xs[:], ALU.min).then_inc(e_l2.sem, 1)
                    if front:
                        conv_round(0, 1)
                        conv_round(0, 2)
                    if mid:
                        wait(dve, e_tl, m)
                        wait(dve, e_n2, m)
                        v.scalar_tensor_tensor(nl[:], nl[:], -0.5, tl[:], ALU.mult, ALU.add).then_inc(e_ex.sem, 1)
                    if front:
                        conv_round(0, 3)
                        conv_round(1, 0)
                        conv_round(1, 1)
                    if mid:
                        wait(dve, e_E, m, 1)
                        k = keep[0:M, m:m + 1] if isinstance(m, int) else keep[0:M, bass.ds(m, 1)]
                        v.tensor_scalar(E[0:M, 4, 0:CH], E[0:M, 4, 0:CH], k, None, ALU.mult).then_inc(e_Ek.sem, 1)
                        wait(dve, e_E, m, 2)
                        wait(dve, e_Ek, m)
                        if not_first_m:
                            wait(dve, e_o, m - 1, 1)
                            wait(dve, e_A, m - 1, 1)
                        v.tensor_tensor(RE[:], E[:], rr[:].unsqueeze(1).to_broadcast([P, SLOTS, T]), ALU.mult)\
                            .then_inc(e_RE.sem, 1)
                    if front:
                        conv_round(1, 2)
                        conv_round(1, 3)

                    def masked(c):
                        wait(dve, e_A, m, c)
                        if c == 1:
                            wait(dve, e_AT, m, LEVELS - 1)
                        elif not_first_m:
                            wait(dve, e_AT, m - 1, 2 * LEVELS - 1)
                        v.tensor_tensor(Wm[:], AB[:, 0:NLV].rearrange("p (l t) -> p l t", l=LEVELS), mask[:], ALU.mult)\
                            .then_inc(e_Wm.sem, 1)
                        if not_first_m:
                            wait(dve, e_o, m - 1, c)
                        v.tensor_scalar(AT[c][:], ident[:], AB[:, NLV:NLV + 1], None, ALU.mult).then_inc(e_at0.sem, 1)

                    def gate(c):
                        wait(dve, e_th, m, 2 * c + 1)
                        v.scalar_tensor_tensor(th[c][:], th[c][:], 1.0, xin[1 - p][:, c, :], ALU.add, ALU.mult)\
                            .then_inc(e_u.sem, 1)

                    def decay(c):
                        for h in range(2):
                            cols = slice(h * HALF, (h + 1) * HALF)
                            last = c * CH + CH - 1
                            wait(dve, e_su, m, 2 * c + h)
                            if c == 0:
                                if not_first_m:
                                    wait(dve, e_o, m - 1, 1)
                                    wait(dve, e_S, m - 1, 2 + h)
                            else:
                                wait(dve, e_o, m, 0)
                                wait(dve, e_S, m, h)
                            v.scalar_tensor_tensor(S[1 - c][:, cols], S[c][:, cols], E[0:M, 4, last:last + 1],
                                                   WK[h][0:M, :], ALU.mult, ALU.add).then_inc(e_S.sem, 1)

                    def residual(lo, hi):
                        for blk in range(lo, hi):
                            wait(dve, e_silu, g, blk // 4)
                            v.scalar_tensor_tensor(acc[p][:, blk, :], shT[:, blk, :], rw_sb[:, blk:blk + 1],
                                                   xT[p][:, blk, HIST:HIST + T], ALU.mult, ALU.add)\
                                .then_inc(e_res.sem, 1)

                    if mid:
                        gate(0)
                        masked(0)
                        gate(1)
                    if front:
                        residual(0, 4)
                    if mid:
                        decay(0)
                        masked(1)
                    if front:
                        residual(4, 8)
                    if mid:
                        decay(1)
                    if back:
                        for c in range(CPG):
                            wait(dve, e_sg, b, c)
                        k = [0]

                        def then(ins):
                            ins.then_inc(e_sc8.sem, 1)
                            wait(dve, e_sc8, b, k[0])
                            k[0] += 1

                        then(v.tensor_reduce(ts[:], sg[:].rearrange("p c (t j) -> p c t j", j=DS), AX_X, ALU.add))
                        then(v.tensor_reduce(cl[:], ts[:].rearrange("p c (n t) -> p c n t", t=TPC), AX_X, ALU.add))
                        then(v.scalar_tensor_tensor(cl[:], cl[:], 4096.0,
                                                    c_cluster[:].unsqueeze(1).to_broadcast([P, CPG, NCL]),
                                                    ALU.mult, ALU.add))
                        then(v.scalar_tensor_tensor(key[:], ts[:], 8.0,
                                                    c_tile[:].unsqueeze(1).to_broadcast([P, CPG, NT]),
                                                    ALU.mult, ALU.add))
                        k4 = key[:].rearrange("p c (n t) -> p c n t", t=TPC)
                        then(v.tensor_tensor(k4, k4, cl[:].unsqueeze(3).to_broadcast([P, CPG, NCL, TPC]), ALU.add))
                        then(v.tensor_reduce(kmax[:], key[:], AX_X, ALU.max))
                        for c in range(CPG):
                            i = v.scalar_tensor_tensor(ts[:, c, :], key[:, c, :], kmax[:, c:c + 1], iota_t[:],
                                                       ALU.is_equal, ALU.mult)
                        then(i)
                        b2 = b * CPG
                        dst = idx_all[:, b2:b2 + CPG] if isinstance(b, int) else idx_all[:, bass.ds(b2, CPG)]
                        then(v.tensor_reduce(dst, ts[:], AX_X, ALU.add))

                pipeline(dve, step)

            @block.gpsimd
            def _(pool):
                q = nc.gpsimd
                q.memset(ident[:], 0.0).then_inc(s_pc, 1)
                q.memset(ones[:], 1.0)
                q.memset(ones_bf[:], 1.0)
                q.memset(minus_half[:], -0.5)
                for k, value in ((TWO, 2.0), (MINUS_1_D, -1.0 / D), (ONE_D, 1.0 / D), (EPS, LN_EPS)):
                    q.memset(consts[:, k:k + 1], value)
                q.memset(ln_fix[:], 10.0 * 0.6931471805599453)
                q.memset(mask[:], 1.0)
                q.memset(X[:], 0.0)
                q.memset(keep[:], 1.0).then_inc(s_pc, 1)
                pool.wait_ge(s_pc, 2)
                q.memset(keep[:].rearrange("p (b g) -> p b g", b=B)[:, :, 0:1], 0.0)
                q.affine_select(out=ident[:], in_=ident[:], compare_op=ALU.not_equal, fill=1.0, base=0,
                                pattern=[[-1, P]], channel_multiplier=1).then_inc(s_pc, 1)
                for l in range(LEVELS):
                    h = 2 ** l
                    mv = mask[:, l, :].rearrange("p (n h) -> p n h", h=h)
                    q.affine_select(out=mv, in_=mv, compare_op=ALU.is_ge, fill=0.0, base=0,
                                    pattern=[[-2 * h, 64 // h], [0, h]], channel_multiplier=1).then_inc(s_pc, 1)
                    pool.wait_ge(s_pc, 4 + 2 * l)
                    q.affine_select(out=mv, in_=mv, compare_op=ALU.is_ge, fill=0.0, base=h - 1,
                                    pattern=[[2 * h, 64 // h], [0, h]], channel_multiplier=-1).then_inc(s_pc, 1)
                q.iota(iota_t[:], pattern=[[1, NT]], base=0, channel_multiplier=0, allow_small_or_imprecise_dtypes=True)
                q.iota(c_tile[:].rearrange("p (n t) -> p n t", t=TPC), pattern=[[0, NCL], [-1, TPC]], base=TPC - 1,
                       channel_multiplier=0, allow_small_or_imprecise_dtypes=True)
                q.iota(c_cluster[:], pattern=[[-512, NCL]], base=512 * (NCL - 1), channel_multiplier=0,
                       allow_small_or_imprecise_dtypes=True).then_inc(s_c, 2)

                def step(g, p, front, mid, back):
                    m, b = g - 1, g - 2
                    later_m = not (isinstance(m, int) and m == 0)
                    if mid:
                        wait(pool, e_pr, m, 0)
                        if later_m:
                            wait(pool, e_ssq, m - 1)
                        q.tensor_tensor(ksq[:], kk[:], kk[:], ALU.mult).then_inc(e_ks.sem, 1)
                        wait(pool, e_pr, m, 2)
                        q.tensor_tensor(gen[:], gen[:], ones[0:M, :], ALU.add).then_inc(e_d.sem, 1)
                        wait(pool, e_ge, m)
                        q.tensor_tensor(gw[:], ge[:], const(TWO, M, T), ALU.add).then_inc(e_gw.sem, 1)
                        wait(pool, e_grw, m)
                        q.tensor_tensor(gw1[:], grw[:], ge[:], ALU.mult).then_inc(e_gw1.sem, 1)
                        wait(pool, e_gw1, m)
                        q.tensor_tensor(gl[:], gw1[:], gw1[:], ALU.mult).then_inc(e_gl.sem, 1)
                    if back:
                        k = [0]

                        def then(ins):
                            ins.then_inc(e_st.sem, 1)
                            wait(pool, e_st, b, k[0])
                            k[0] += 1

                        wait(pool, e_sq, b, 1)
                        if not (isinstance(b, int) and b == 0):
                            wait(pool, e_xf, b - 1, 1)
                        then(q.tensor_tensor(st[:, 0, :], ssm[:], const(ONE_D, P, CPG), ALU.mult))
                        then(q.tensor_tensor(st[:, 0, :], st[:, 0, :], const(EPS, P, CPG), ALU.add))
                        then(q.tensor_tensor(st[:, 1, :], st[:, 0, :], minus_half[:], ALU.pow))
                        then(q.tensor_tensor(st[:, 2, :], st[:, 1, :], st[:, 1, :], ALU.mult))
                        then(q.tensor_tensor(st[:, 3, :], st[:, 2, :], ssm[:], ALU.mult))
                        then(q.tensor_tensor(st[:, 4, :], st[:, 3, :], const(ONE_D, P, CPG), ALU.mult))
                        then(q.tensor_tensor(st[:, 4, :], st[:, 4, :], const(EPS, P, CPG), ALU.add))
                        then(q.tensor_tensor(st[:, 4, :], st[:, 4, :], minus_half[:], ALU.pow))
                        then(q.tensor_tensor(st[:, 5, :], st[:, 4, :], st[:, 1, :], ALU.mult))
                        for dst, src in ((nm_all, nm[p][:]), (r1_all, st[:, 1, :]), (r12_all, st[:, 5, :]), (ss_all, st[:, 3, :])):
                            col = slice(b * CPG, (b + 1) * CPG) if isinstance(b, int) else bass.ds(b * CPG, CPG)
                            q.tensor_copy(dst[:, col], src).then_inc(e_keep.sem, 1)
                    if mid:
                        wait(pool, e_sel, m)
                        wait(pool, e_tau, m)
                        if later_m:
                            wait(pool, e_b, m - 1)
                        q.tensor_tensor(gn[:], sel[:], tau[:], ALU.mult).then_inc(e_gn.sem, 1)
                        wait(pool, e_l2, m)
                        if later_m:
                            wait(pool, e_ex, m - 1)
                        q.tensor_tensor(tl[:], tau[:], lsel[:], ALU.mult).then_inc(e_tl.sem, 1)
                        wait(pool, e_b, m)
                        if later_m:
                            wait(pool, e_E, m - 1, 2)
                        for l in (*range(0, LEVELS, 2), *range(1, LEVELS, 2)):
                            if l == 1:
                                wait(pool, e_bd, m)
                                wait(pool, e_Xl, m)
                            h, rows = 2 ** l, level_rows(l)
                            b_early, b_late = level_halves(bb[rows, :], h)
                            x_early, x_late = level_halves(X[rows, l // 2, :], h)
                            ref = b_early[:, :, h - 1:h].to_broadcast([M, T // (2 * h), h])
                            i = q.tensor_tensor(x_late, b_late, ref, ALU.subtract)
                            if l:
                                i = q.tensor_tensor(x_early, ref, b_early, ALU.subtract)
                            if l == LEVELS - 1:
                                i.then_inc(e_Xl.sem, 1)
                        bend = bb[M:P, :].rearrange("p (c t) -> p c t", c=CPG)
                        q.tensor_tensor(X[M:P, 4, :].rearrange("p (c t) -> p c t", c=CPG),
                                        bend[:, :, CH - 1:CH].to_broadcast([M, CPG, CH]), bend, ALU.subtract)\
                            .then_inc(e_X.sem, 1)
                        wait(pool, e_X, m)
                        wait(pool, e_kg, m)
                        if later_m:
                            wait(pool, e_KE, m - 1)
                        q.tensor_tensor(kn[0:M, :], kk[:], kg[:], ALU.mult).then_inc(e_kn.sem, 1)
                        wait(pool, e_kn, m)
                        wait(pool, e_pr, m, 4)
                        if later_m:
                            wait(pool, e_A, m - 1, 1)
                            wait(pool, e_keT, m - 1)
                        q.tensor_tensor(rkp[:], rr[0:M, :], kn[0:M, :], ALU.mult).then_inc(e_rkp.sem, 1)
                        wait(pool, e_kd, m)
                        wait(pool, e_Ek, m)
                        wait(pool, e_E, m, 2)
                        q.tensor_tensor(KE[:], E[:], kn[:].unsqueeze(1).to_broadcast([P, SLOTS, T]), ALU.mult)\
                            .then_inc(e_KE.sem, 1)
                        for c in range(CPG):
                            wait(pool, e_Wm, m, c)
                            wait(pool, e_at0, m, c)
                            for l in range(LEVELS):
                                late = level_halves(AT[c][:], 2 ** l)[1]
                                if l:
                                    wait(pool, e_AT, m, c * LEVELS + l - 1)
                                q.tensor_tensor(late, late, Wm[:, l, :].rearrange("p (n h) -> p n h", h=2 ** l), ALU.add)\
                                    .then_inc(e_AT.sem, 1)
                        for c in range(CPG):
                            wait(pool, e_y, m, c)
                            if c == 0 and not (isinstance(m, int) and m < 2):
                                wait(pool, e_keep, m - 2, 3)
                                wait(pool, e_q, m - 2, 1)
                            q.tensor_tensor(nm[1 - p][:, c:c + 1], ysum[:, c:c + 1], const(MINUS_1_D, P, 1), ALU.mult)\
                                .then_inc(e_nm.sem, 1)

                pipeline(pool, step)

        with ExitStack() as ctx:
            def sb(name, shape, dt=F32):
                return ctx.enter_context(nc.sbuf_tensor(name, shape, dt))

            def psum(name, shape, dt=F32):
                return ctx.enter_context(nc.psum_tensor(name, shape, dt))

            def sem(name):
                return ctx.enter_context(nc.semaphore(name))

            BT = 8
            NBT = NC // BT
            assert NC % 16 == 0
            TC = 2 * DS * GRID
            assert TC == HALF
            gidx_f = sb("gidx_f", [P, NC])
            gidx = sb("gidx", [P, NC], U32)
            iota_g = sb("iota_g", [P, GRID])
            y_sl = sb("y_sl", [P, NC, DS])
            oh = sb("oh", [P, NC, NT], BF16)
            ohT = sb("ohT", [NT, NC, P], BF16)
            pen = sb("pen", [P, NC, NT])
            pick = sb("pick", [P, NC, NT])
            t1 = sb("t1", [NT, 2 * DS])
            t1s = sb("t1s", [NT, 3, 2 * DS], BF16)
            t2 = sb("t2", [NT, TC])
            t2s = sb("t2s", [NT, 3, TC], BF16)
            t3 = sb("t3", [NT, 4])
            t3s = sb("t3s", [NT, 3, 4], BF16)
            gb = sb("gb", [P, NC, 2 * DS])
            x1s = sb("x1s", [P, NC, DS])
            xfs = sb("xfs", [P, NC, DS])
            mm = sb("mm", [P, 2, NC])
            ext = sb("ext", [P, 2, NT])
            rng3 = sb("rng3", [P, NC, 4])
            rng = sb("rng", [P, NC])
            gcell = sb("gcell", [P, NC, DS])
            tmp = sb("tmp", [P, NC, DS])
            ohg = sb("ohg", [P, 2, DS, GRID])
            pr = sb("pr", [P, 2, TC])
            bsv = sb("bsv", [P, BT, 2, DS])
            dl = sb("dl", [P, BT, DS])
            w_a = sb("w_a", [P, BT, DS])
            sm = sb("sm", [P, 8, BT])
            coef = sb("coef", [P, 2, 2, BT])
            outs = sb("outs", [P, NC, DS])
            mh8 = sb("mh8", [P, BT])
            ident_bf = sb("ident_bf", [P, P], BF16)
            rows = [sb(f"rows{i}", [P, BT, D]) for i in range(2)]

            Z = [psum(f"Z{i}", [P, HALF]) for i in range(4)]
            OT = [psum(f"OT{i}", [NT, 8, P], BF16) for i in range(2)]
            QA = psum("QA", [P, HALF])
            QB = psum("QB", [P, HALF])

            p_tab, p_i, p_gi, p_gat = sem("p_tab"), sem("p_i"), sem("p_gi"), sem("p_gat")
            p_oh, p_ohT, p_ohTe, p_t1, p_g1, p_g1e = (sem(n) for n in ("p_oh", "p_ohT", "p_ohTe", "p_t1", "p_g1", "p_g1e"))
            p_v, p_ext, p_extT, p_t3, p_r3, p_u = (sem(n) for n in ("p_v", "p_ext", "p_extT", "p_t3", "p_r3", "p_u"))
            p_z, p_zf, p_b, p_coef, p_pw, p_ve = (sem(n) for n in ("p_z", "p_zf", "p_b", "p_coef", "p_pw", "p_ve"))
            p_row, p_sc, p_bb, p_g = (sem(n) for n in ("p_row", "p_sc", "p_bb", "p_g"))
            p_ld = [[sem(f"p_ld{p}{h}") for h in range(2)] for p in range(2)]
            p_st = [sem(f"p_st{p}") for p in range(2)]
            VB = 14

            y_b = y_dram.rearrange("(q n p) d -> q p n d", n=BT, p=P)
            out_b = out.rearrange("b l d -> (b l) d").rearrange("(q n p) d -> q p n d", n=BT, p=P)
            block = ctx.enter_context(nc.Block())

            @block.sync
            def _(sp):
                sp.dma_start(t1[:, 0:DS], gamma.rearrange("(t j) -> t j", j=DS)).then_inc(p_tab, 16)
                sp.dma_start(t1[:, DS:2 * DS], beta.rearrange("(t j) -> t j", j=DS)).then_inc(p_tab, 16)
                sp.dma_start(t2[:, 0:TC // 2], bases.rearrange("t j g -> t (j g)")).then_inc(p_tab, 16)
                sp.dma_start(t2[:, TC // 2:TC], slopes.rearrange("t j g -> t (j g)")).then_inc(p_tab, 16)
                sp.dma_start(t3[:, 2:3], oscale).then_inc(p_tab, 16)

                def load(q, p):
                    src = y_b[q] if isinstance(q, int) else y_b[bass.ds(q, 1)].rearrange("q p n d -> (q p) n d")
                    for h in range(2):
                        hs = slice(h * BT // 2, (h + 1) * BT // 2)
                        sp.dma_start(rows[p][:, hs, :], src[:, hs, :]).then_inc(p_ld[p][h], 16)

                def store(q, p):
                    dst = out_b[q] if isinstance(q, int) else out_b[bass.ds(q, 1)].rearrange("q p n d -> (q p) n d")
                    for h in range(2):
                        hs = slice(h * BT // 2, (h + 1) * BT // 2)
                        sp.wait_ge(p_row, q * BT + (h + 1) * BT // 2)
                        sp.dma_start(dst[:, hs, :], rows[p][:, hs, :]).then_inc(p_st[p], 16)

                load(0, 0)
                load(1, 1)
                with sp.Fori(0, NBT // 2 - 1) as pair:
                    for p in range(2):
                        store(pair * 2 + p, p)
                        sp.wait_ge(p_st[p], pair * 32 + 32)
                        load(pair * 2 + p + 2, p)
                for p in range(2):
                    store(NBT - 2 + p, p)
                for p in range(2):
                    sp.wait_ge(p_st[p], 16 * NBT)

            @block.gpsimd
            def _(pool):
                q = nc.gpsimd
                q.iota(gidx_f[:], pattern=[[P * NT, NC]], base=0, channel_multiplier=NT,
                       allow_small_or_imprecise_dtypes=True).then_inc(p_i, 1)
                q.iota(iota_g[:], pattern=[[1, GRID]], base=0, channel_multiplier=0,
                       allow_small_or_imprecise_dtypes=True).then_inc(p_i, 1)
                q.memset(mh8[:], -0.5).then_inc(p_i, 1)
                pool.wait_ge(p_gi, 1)
                for n in range(NC):
                    q.indirect_dma_start(y_sl[:, n, :], None, y_slices,
                                         bass.IndirectOffsetOnAxis(ap=gidx[:, n:n + 1], axis=0)).then_inc(p_gat, 16)

                def batch(k):
                    pool.wait_ge(p_ve, k + 1)
                    q.tensor_tensor(sm[:, 6, :], sm[:, 5, :], mh8[:], ALU.pow).then_inc(p_pw, 1)

                pool.wait_ge(p_i, 3)
                with pool.Fori(0, NBT) as k:
                    batch(k)
                pool.wait_ge(p_b, VB * NBT)
                for p in range(2):
                    pool.wait_ge(p_st[p], 16 * NBT)
                for n in range(NC):
                    q.indirect_dma_start(out_slices, bass.IndirectOffsetOnAxis(ap=gidx[:, n:n + 1], axis=0),
                                         outs[:, n, :], None).then_inc(p_sc, 16)
                pool.wait_ge(p_sc, 16 * NC)

            @block.tensor
            def _(pe):
                pe.wait_ge(p_oh, 2)
                for f in range(NC // 8):
                    if f >= 2:
                        pe.wait_ge(p_ohTe, f - 1)
                    for j in range(8):
                        i = pe.transpose(OT[f % 2][:, j, :], oh[:, f * 8 + j, :], ident_bf[:])
                    i.then_inc(p_ohT, 1)
                pe.wait_ge(p_ohTe, NC // 8)
                pe.wait_ge(p_t1, 1)
                for f in range(NC // 16):
                    for j in range(16):
                        for k in range(3):
                            i = pe.matmul(Z[f % 4][:, j * 32:(j + 1) * 32], ohT[:, f * 16 + j, :], t1s[:, k, :],
                                          start=(k == 0), stop=(k == 2))
                    i.then_inc(p_g1, 1)
                pe.wait_ge(p_ext, 1)
                for k in range(2):
                    i = pe.transpose(QA[0:NT, k * P:(k + 1) * P], ext[:, k, :], ident[:])
                i.then_inc(p_extT, 1)
                pe.wait_ge(p_t3, 1)
                for n in range(NC):
                    for k in range(3):
                        i = pe.matmul(QB[:, n * 4:(n + 1) * 4], ohT[:, n, :], t3s[:, k, :], start=(k == 0), stop=(k == 2))
                i.then_inc(p_r3, 1)
                pe.wait_ge(p_g1e, NC // 16)

                def tables(n, j):
                    if not isinstance(n, int):
                        pe.wait_ge(p_zf, n - 3)
                    elif n >= 4:
                        pe.wait_ge(p_zf, n - 3)
                    lhs = ohT[:, n, :] if isinstance(n, int) else ohT[:, bass.ds(n, 1), :].rearrange("t n p -> t (n p)")
                    for k in range(3):
                        i = pe.matmul(Z[j % 4][:], lhs, t2s[:, k, :], start=(k == 0), stop=(k == 2))
                    i.then_inc(p_z, 1)

                for j in range(4):
                    tables(j, j)
                with pe.Fori(1, NC // 4) as four:
                    for j in range(4):
                        tables(four * 4 + j, j)

            @block.scalar
            def _(act):
                for f in range(NC // 8):
                    act.wait_ge(p_ohT, f + 1)
                    nc.scalar.activation(ohT[:, f * 8:(f + 1) * 8, :], OT[f % 2][:], ACT.Copy).then_inc(p_ohTe, 1)
                for f in range(NC // 16):
                    act.wait_ge(p_g1, f + 1)
                    nc.scalar.activation(gb[:, f * 16:(f + 1) * 16, :],
                                         Z[f % 4][:].rearrange("p (n j) -> p n j", n=16), ACT.Copy).then_inc(p_g1e, 1)

                def scale_rows(k, p):
                    act.wait_ge(p_coef, k + 1)
                    for h in range(2):
                        act.wait_ge(p_ld[p][h], (k - p) * 8 + 16)
                        for n in range(h * BT // 2, (h + 1) * BT // 2):
                            nc.scalar.activation(rows[p][:, n, :], rows[p][:, n, :], ACT.Identity,
                                                 scale=coef[:, p, 0, n:n + 1], bias=coef[:, p, 1, n:n + 1])\
                                .then_inc(p_row, 1)

                with act.Fori(0, NBT // 2) as pair:
                    for p in range(2):
                        scale_rows(pair * 2 + p, p)

            @block.vector
            def _(dve):
                v = nc.vector
                count = [0]

                def link(ins):
                    count[0] += 1
                    ins.then_inc(p_v, 1)
                    dve.wait_ge(p_v, count[0])

                dve.wait_ge(p_i, 1)
                v.tensor_tensor(gidx[:], gidx_f[:], idx_all[:], ALU.add).then_inc(p_gi, 1)
                v.tensor_copy(ident_bf[:], ident[:]).then_inc(p_oh, 1)
                v.tensor_tensor(oh[:], iota_t[:].unsqueeze(1).to_broadcast([P, NC, NT]),
                                idx_all[:].unsqueeze(2).to_broadcast([P, NC, NT]), ALU.is_equal).then_inc(p_oh, 1)
                dve.wait_ge(p_tab, 16 * 5)

                def split(dst, src):
                    for k in range(3):
                        link(v.tensor_copy(dst[:, k, :], src))
                        if k < 2:
                            link(v.tensor_tensor(src, src, dst[:, k, :], ALU.subtract))

                split(t1s, t1[:])
                v.memset(t3[:, 3:4], 0.0).then_inc(p_t1, 1)
                split(t2s, t2[:])
                dve.wait_ge(p_oh, 2)
                link(v.tensor_scalar(pen[:], oh[:], BIG, -BIG, ALU.mult, ALU.add))

                def per_tile(a):
                    return a.unsqueeze(2).to_broadcast([P, NC, DS])

                dve.wait_ge(p_gat, 16 * NC)
                dve.wait_ge(p_g1e, NC // 16)
                link(v.tensor_tensor(xfs[:], y_sl[:], per_tile(nm_all[:]), ALU.add))
                link(v.tensor_tensor(x1s[:], xfs[:], per_tile(r1_all[:]), ALU.mult))
                link(v.tensor_tensor(xfs[:], xfs[:], per_tile(r12_all[:]), ALU.mult))
                link(v.tensor_tensor(xfs[:], xfs[:], gb[:, :, 0:DS], ALU.mult))
                link(v.tensor_tensor(xfs[:], xfs[:], gb[:, :, DS:2 * DS], ALU.add))
                link(v.tensor_reduce(mm[:, 0, :], xfs[:], AX_X, ALU.max))
                link(v.tensor_reduce(mm[:, 1, :], xfs[:], AX_X, ALU.min))
                link(v.tensor_scalar(mm[:, 1, :], mm[:, 1, :], -1.0, None, ALU.mult))
                for k in range(2):
                    link(v.tensor_tensor(pick[:], oh[:], mm[:, k, :].unsqueeze(2).to_broadcast([P, NC, NT]), ALU.mult))
                    link(v.tensor_tensor(pick[:], pick[:], pen[:], ALU.add))
                    link(v.tensor_reduce(ext[:, k, :], pick[:].rearrange("p n t -> p t n"), AX_X, ALU.max))
                v.memset(sm[:], 0.0).then_inc(p_ext, 1)
                dve.wait_ge(p_extT, 1)
                link(v.tensor_reduce(t3[:, 0:2], QA[0:NT, 0:2 * P].rearrange("t (k p) -> t k p", k=2), AX_X, ALU.max))
                split(t3s, t3[:])
                v.memset(sm[:], 0.0).then_inc(p_t3, 1)
                dve.wait_ge(p_r3, 1)
                link(v.tensor_copy(rng3[:], QB[:, 0:NC * 4].rearrange("p (n k) -> p n k", k=4)))
                link(v.scalar_tensor_tensor(rng[:], rng3[:, :, 0], 0.0, rng3[:, :, 1], ALU.add, ALU.add))
                link(v.tensor_scalar(rng[:], rng[:], 1e-8, None, ALU.add))
                link(v.reciprocal(rng[:], rng[:]))
                link(v.tensor_tensor(xfs[:], xfs[:], per_tile(rng3[:, :, 1]), ALU.add))
                link(v.tensor_tensor(xfs[:], xfs[:], per_tile(rng[:]), ALU.mult))
                link(v.tensor_scalar(xfs[:], xfs[:], 0.0, 1.0 - 1e-6, ALU.max, ALU.min))
                link(v.tensor_scalar(xfs[:], xfs[:], float(GRID), None, ALU.mult))
                link(v.tensor_scalar(gcell[:], xfs[:], MAGIC, None, ALU.add))
                link(v.tensor_scalar(gcell[:], gcell[:], -MAGIC, None, ALU.add))
                link(v.tensor_tensor(tmp[:], gcell[:], xfs[:], ALU.is_gt))
                link(v.tensor_tensor(gcell[:], gcell[:], tmp[:], ALU.subtract))
                link(v.tensor_tensor(xfs[:], xfs[:], gcell[:], ALU.subtract))
                dve.wait_ge(p_i, 3)

                def batch(k, p):
                    n0 = k * BT
                    at = bass.ds(n0, BT)
                    for j in range(BT):
                        n = n0 + j
                        gc = gcell[:, bass.ds(n, 1), :].rearrange("p n j -> p (n j)").unsqueeze(2)\
                            .to_broadcast([P, DS, GRID])
                        pj = pr[:, j % 2, :].rearrange("p (k j g) -> p k j g", k=2, g=GRID)
                        v.tensor_tensor(ohg[:, j % 2, :, :], iota_g[:].unsqueeze(1).to_broadcast([P, DS, GRID]), gc,
                                        ALU.is_equal).then_inc(p_g, 1)
                        dve.wait_ge(p_z, n + 1)
                        dve.wait_ge(p_g, n + 1)
                        v.tensor_tensor(pj, Z[j % 4][:].rearrange("p (k j g) -> p k j g", k=2, g=GRID),
                                        ohg[:, j % 2, :, :].unsqueeze(1).to_broadcast([P, 2, DS, GRID]), ALU.mult)\
                            .then_inc(p_zf, 1)
                        dve.wait_ge(p_zf, n + 1)
                        v.tensor_reduce(bsv[:, j, :, :], pj, AX_X, ALU.add).then_inc(p_bb, 1)
                    c = [0]

                    def then(ins):
                        ins.then_inc(p_b, 1)
                        c[0] += 1
                        dve.wait_ge(p_b, k * VB + c[0])

                    def by_tile(a):
                        return a.unsqueeze(2).to_broadcast([P, BT, DS])

                    dve.wait_ge(p_bb, (k + 1) * BT)
                    x_at = x1s[:, at, :]
                    then(v.tensor_tensor(dl[:], bsv[:, :, 1, :], xfs[:, at, :], ALU.mult))
                    then(v.tensor_tensor(dl[:], dl[:], bsv[:, :, 0, :], ALU.add))
                    then(v.tensor_tensor(dl[:], dl[:], rng3[:, at, 2:3].to_broadcast([P, BT, DS]), ALU.mult))
                    then(v.tensor_reduce(sm[:, 0, :], dl[:], AX_X, ALU.add))
                    then(v.scalar_tensor_tensor(w_a[:], x_at, 4.0, dl[:], ALU.mult, ALU.add))
                    then(v.tensor_tensor(w_a[:], w_a[:], dl[:], ALU.mult))
                    then(v.tensor_reduce(sm[:, 1, :], w_a[:], AX_X, ALU.add))
                    then(v.tensor_scalar(sm[:, 0, :], sm[:, 0, :], 1.0 / D, None, ALU.mult))
                    then(v.scalar_tensor_tensor(sm[:, 1, :], ss_all[:, at], 4.0, sm[:, 1, :], ALU.mult, ALU.add))
                    then(v.tensor_tensor(sm[:, 2, :], sm[:, 0, :], sm[:, 0, :], ALU.mult))
                    then(v.scalar_tensor_tensor(sm[:, 1, :], sm[:, 1, :], 1.0 / D, sm[:, 2, :], ALU.mult, ALU.subtract))
                    v.tensor_scalar(sm[:, 5, :], sm[:, 1, :], LN_EPS, None, ALU.add).then_inc(p_ve, 1)
                    then(v.scalar_tensor_tensor(w_a[:], x_at, 2.0, dl[:], ALU.mult, ALU.add))
                    then(v.tensor_tensor(w_a[:], w_a[:], by_tile(sm[:, 0, :]), ALU.subtract))
                    dve.wait_ge(p_pw, k + 1)
                    v.tensor_tensor(outs[:, at, :], w_a[:], by_tile(sm[:, 6, :]), ALU.mult)
                    if not (isinstance(k, int) and k < 2):
                        dve.wait_ge(p_row, (k - 1) * BT)
                    v.scalar_tensor_tensor(coef[:, p, 0, :], r1_all[:, at], 2.0, sm[:, 6, :], ALU.mult, ALU.mult)
                    v.scalar_tensor_tensor(sm[:, 3, :], r1_all[:, at], 2.0, nm_all[:, at], ALU.mult, ALU.mult).then_inc(p_u, 1)
                    dve.wait_ge(p_u, 3 * k + 1)
                    v.tensor_tensor(sm[:, 4, :], sm[:, 3, :], sm[:, 0, :], ALU.subtract).then_inc(p_u, 1)
                    dve.wait_ge(p_u, 3 * k + 2)
                    v.tensor_tensor(coef[:, p, 1, :], sm[:, 4, :], sm[:, 6, :], ALU.mult).then_inc(p_coef, 1)
                    v.tensor_copy(sm[:, 7, :], sm[:, 6, :]).then_inc(p_u, 1)
                    then(v.tensor_copy(w_a[:, :, 0], sm[:, 3, :]))

                batch(0, 0)
                batch(1, 1)
                with dve.Fori(1, NBT // 2) as pair:
                    for p in range(2):
                        batch(pair * 2 + p, p)


def kernel(**inputs):
    import numpy as np
    import concourse.bacc as bacc
    from concourse.bass_utils import run_bass_kernel_spmd

    def arr(name):
        return np.asarray(inputs[name])

    def by_block(w):
        return np.ascontiguousarray(w.T.reshape(-1, 128, w.shape[0]).transpose(1, 0, 2))

    def column(v):
        return np.ascontiguousarray(v.reshape(-1, 128).T)

    x = np.ascontiguousarray(arr("L0_attn_hidden_states"))
    slopes = np.ascontiguousarray(arr("L0_ffn_spline_slopes"))
    conv_w = arr("L0_attn_conv_w")
    host = dict(
        x=x,
        w_rk=by_block(arr("L0_attn_in_proj_w")),
        w_mg=by_block(arr("L0_attn_mem_gate_w")),
        w0=by_block(arr("L0_attn_ch_gate_w0")),
        w1=np.ascontiguousarray(arr("L0_attn_ch_gate_w1").T),
        conv_w=np.ascontiguousarray(conv_w.reshape(-1, 128, conv_w.shape[1]).transpose(1, 0, 2)),
        conv_b=column(arr("L0_attn_conv_b")),
        gate_b1=np.ascontiguousarray(arr("L0_attn_ch_gate_b1")[None, :]),
        mem_b=np.ascontiguousarray(arr("L0_attn_mem_gate_b")[:, None]),
        res_w=column(arr("L0_attn_residual_weight")),
        gamma=np.ascontiguousarray(arr("L0_ffn_ln_gamma")),
        beta=np.ascontiguousarray(arr("L0_ffn_ln_beta")),
        bases=np.ascontiguousarray(arr("L0_ffn_spline_bases")),
        slopes=slopes,
        oscale=np.ascontiguousarray(arr("L0_ffn_output_scale")[:, None]),
    )
    nc = bacc.Bacc("TRN2", target_bir_lowering=False, num_devices=1)
    args = {k: nc.dram_tensor(f"in_{k}", v.shape, mybir.dt.from_np(v.dtype), kind="ExternalInput").ap()
            for k, v in host.items()}
    out = nc.dram_tensor("out", x.shape, F32, kind="ExternalOutput").ap()
    build(nc, out=out, **args)
    r = run_bass_kernel_spmd(nc, [{f"in_{k}": v for k, v in host.items()}], core_ids=[0])
    return r.results[0]["out"]
```

```python
from contextlib import ExitStack

import concourse.bass as bass
from concourse import mybir

ALU = mybir.AluOpType
ACT = mybir.ActivationFunctionType
F32 = mybir.dt.float32
BF16 = mybir.dt.bfloat16
U32 = mybir.dt.uint32
AX_X = mybir.AxisListType.X

P = 128
CH = 128
CPG = 2
T = CH * CPG
LEVELS = 7
HIST = 3
SLOTS = 5
SEL_MIN = 2.0 ** -60
SS_SCALE = 2.0 ** 20
BIG = 1e30
ATANH = (2.0000000078699283, 0.6666631600410559, 0.40024852291048835, 0.27961426376095516, 0.2817466568891232)
MAGIC = float(2 ** 23)
LN_EPS = 1e-5


class Event:

    def __init__(self, sem, per_group):
        self.sem, self.per_group = sem, per_group

    def at(self, g, i=0):
        return g * self.per_group + (i + 1)


def build(nc, x, w_rk, w_mg, w0, w1, conv_w, conv_b, gate_b1, mem_b, res_w, gamma, beta, bases, slopes, oscale, out):
    B, L, D = x.shape
    M = 64
    R = w0.shape[2]
    W = conv_w.shape[2]
    NB = D // P
    NG = B * L // T
    NC = B * L // CH
    NT = bases.shape[0]
    DS = D // NT
    GRID = bases.shape[2]
    NCL = 8
    TPC = NT // NCL
    HALF = 512
    NLV = LEVELS * (CH // 2)
    assert W == HIST + 1 and R == P and D == 2 * HALF and NG % 2 == 0 and NG >= 4
    R_SCALE = 0.5 / float(M) ** 0.5

    x_g = x.rearrange("b l d -> (b l) d").rearrange("(g c p) d -> g p c d", c=CPG, p=P)
    out_g = out.rearrange("b l d -> (b l) d").rearrange("(g c p) d -> g p c d", c=CPG, p=P)
    y_dram = nc.dram_tensor("y_scratch", (B * L, D), F32, kind="Internal").ap()
    y_g = y_dram.rearrange("(g c p) d -> g p c d", c=CPG, p=P)
    y_slices = y_dram.rearrange("n (t j) -> (n t) j", j=DS)
    out_slices = out.rearrange("b l d -> (b l) d").rearrange("n (t j) -> (n t) j", j=DS)

    with ExitStack() as whole:
        def sbw(name, shape, dt=F32):
            return whole.enter_context(nc.sbuf_tensor(name, shape, dt))

        ident = sbw("ident", [P, P])
        iota_t = sbw("iota_t", [P, NT])
        minus_half = sbw("minus_half", [P, CPG])
        nm_all = sbw("nm_all", [P, NC])
        r1_all = sbw("r1_all", [P, NC])
        r12_all = sbw("r12_all", [P, NC])
        ss_all = sbw("ss_all", [P, NC])
        idx_all = sbw("idx_all", [P, NC])
        with ExitStack() as ctx:
            def sb(name, shape, dt=F32):
                return ctx.enter_context(nc.sbuf_tensor(name, shape, dt))

            def psum(name, shape, dt=F32):
                return ctx.enter_context(nc.psum_tensor(name, shape, dt))

            def sem(name):
                return ctx.enter_context(nc.semaphore(name))

            def ev(name, per_group):
                return Event(sem(name), per_group)

            w_rk_sb = sb("w_rk_sb", [P, NB, P])
            w_mg_sb = sb("w_mg_sb", [P, NB, P])
            w0_sb = sb("w0_sb", [P, NB, R])
            w1_sb = sb("w1_sb", [P, D])
            cw_sb = sb("cw_sb", [P, NB, W])
            cb_sb = sb("cb_sb", [P, NB])
            rw_sb = sb("rw_sb", [P, NB])
            mb_sb = sb("mb_sb", [P, 2])
            b1_split = sb("b1_split", [96, D], BF16)
            gam = sb("gam", [P, D])
            bet = sb("bet", [P, D])
            ones = sb("ones", [P, T])
            ones_bf = sb("ones_bf", [96, P], BF16)
            mask = sb("mask", [P, LEVELS, CH // 2])
            keep = sb("keep", [P, NG])
            ln_fix = sb("ln_fix", [P, 1])
            two = sb("two", [P, 1])
            MINUS_1_D, ONE_D, EPS = range(3)
            consts = sb("consts", [P, 3])
            c_tile = sb("c_tile", [P, NT])
            c_cluster = sb("c_cluster", [P, NCL])

            xin = [sb(f"xin{i}", [P, CPG, D]) for i in range(2)]
            xT = [sb(f"xT{i}", [P, NB, HIST + T]) for i in range(2)]
            acc = sb("acc", [P, NB, T])
            zT = [sb(f"zT{i}", [P, NB, T]) for i in range(2)]
            shT = sb("shT", [P, NB, T])
            tS = [sb(f"tS{i}", [P, T]) for i in range(2)]
            rr = sb("rr", [P, T])
            kk = sb("kk", [M, T])
            xs = sb("xs", [M, T])
            xa = sb("xa", [M, T])
            ge = sb("ge", [M, T])
            gl = sb("gl", [M, T])
            gw1 = sb("gw1", [M, T])
            grw = sb("grw", [M, T])
            sel = sb("sel", [M, T])
            lsel = sb("lsel", [M, T])
            gen = sb("gen", [M, T])
            tau = sb("tau", [M, T])
            gn = sb("gn", [M, T])
            tl = sb("tl", [M, T])
            ksq = sb("ksq", [M, T])
            nl = sb("nl", [M, T])
            kg = sb("kg", [M, T])
            kn = sb("kn", [P, T])
            bb = sb("bb", [P, T])
            rkp = [sb(f"rkp{i}", [M, T]) for i in range(2)]
            dec = [sb(f"dec{i}", [M, CPG]) for i in range(2)]
            X = sb("X", [P, SLOTS, T])
            E = sb("E", [P, SLOTS, T])
            RE = [sb(f"RE{i}", [P, SLOTS, T]) for i in range(2)]
            KE = [sb(f"KE{i}", [P, SLOTS, T]) for i in range(2)]
            keT_sb = sb("keT_sb", [P, CPG, M])
            Wm = sb("Wm", [P, LEVELS, CH // 2])
            AT = [sb(f"AT{i}", [P, CH]) for i in range(2)]
            th = [[sb(f"th{i}{c}", [P, D]) for c in range(CPG)] for i in range(2)]
            S = [sb(f"S{i}", [M, D]) for i in range(2)]
            y = [sb(f"y{i}", [P, CPG, D]) for i in range(2)]
            xf = [sb(f"xf{i}", [P, D]) for i in range(2)]
            sg = sb("sg", [P, CPG, D], BF16)
            ysum = sb("ysum", [P, CPG])
            nm = [sb(f"nm{i}", [P, CPG]) for i in range(2)]
            ssm = sb("ssm", [P, CPG])
            st = sb("st", [P, 6, CPG])
            ts = sb("ts", [P, CPG, NT])
            cl = sb("cl", [P, CPG, NCL])
            key = sb("key", [P, CPG, NT])
            kmax = sb("kmax", [P, CPG])
            tidx = sb("tidx", [P, CPG])

            TX = psum("TX", [P, HALF])
            PR = psum("PR", [P, HALF])
            GA = psum("GA", [P, HALF])
            AB = psum("AB", [P, HALF])
            WK = [psum(f"WK{i}", [P, HALF]) for i in range(2)]
            OB = psum("OB", [P, 2 * HALF])

            s_w = sem("s_w")
            s_sl = [sem(f"s_sl{i}") for i in range(2)]
            s_slr = sem("s_slr")
            s_c = sem("s_c")
            s_cv = sem("s_cv")
            s_ss = sem("s_ss")
            s_setup = sem("s_setup")
            s_pc = sem("s_pc")
            d_xin = [sem(f"d_xin{i}") for i in range(2)]
            d_yst = [sem(f"d_yst{i}") for i in range(2)]
            e_xtr, e_xev, e_hist = ev("e_xtr", 4), ev("e_xev", 4), ev("e_hist", 1)
            e_t, e_tev = ev("e_t", 1), ev("e_tev", 1)
            e_conv, e_silu, e_proj, e_res = ev("e_conv", NB * W), ev("e_silu", 2), ev("e_proj", 1), ev("e_res", NB)
            e_pr = ev("e_pr", 5)
            e_xa, e_ge, e_gz, e_gl, e_gw1, e_grw = (ev(n, 1) for n in ("e_xa", "e_ge", "e_gz", "e_gl", "e_gw1", "e_grw"))
            e_lg, e_sel, e_sc, e_ls, e_l2 = (ev(n, 1) for n in ("e_lg", "e_sel", "e_sc", "e_ls", "e_l2"))
            e_d, e_tau, e_gn, e_tl, e_b, e_bd = (ev(n, 1) for n in ("e_d", "e_tau", "e_gn", "e_tl", "e_b", "e_bd"))
            e_ks, e_ssq, e_n1, e_n2, e_ex, e_kg = (ev(n, 1) for n in ("e_ks", "e_ssq", "e_n1", "e_n2", "e_ex", "e_kg"))
            e_kn, e_kd, e_X, e_Ek, e_RE, e_KE, e_rkp = (
                ev(n, 1) for n in ("e_kn", "e_kd", "e_X", "e_Ek", "e_RE", "e_KE", "e_rkp"))
            e_E, e_gq = ev("e_E", 3), ev("e_gq", 4)
            e_keT, e_keTe = ev("e_keT", 1), ev("e_keTe", 1)
            e_c2, e_th, e_u = ev("e_c2", 4), ev("e_th", 4), ev("e_u", 2)
            e_Ah, e_Xl = ev("e_Ah", 2), ev("e_Xl", 1)
            e_A, e_Wm, e_at0, e_AT = ev("e_A", 2), ev("e_Wm", 2), ev("e_at0", 2), ev("e_AT", 2 * LEVELS)
            e_o, e_su, e_S, e_y = ev("e_o", 2), ev("e_su", 4), ev("e_S", 4), ev("e_y", 2)
            e_nm, e_sq, e_st = ev("e_nm", 2), ev("e_sq", 2), ev("e_st", 9)
            e_q, e_xf, e_sg = ev("e_q", 2), ev("e_xf", 2), ev("e_sg", 2)
            e_dec = ev("e_dec", 1)
            e_sc8, e_keep = ev("e_sc8", 8), ev("e_keep", 4)

            def wait(eng, e, g, i=0):
                eng.wait_ge(e.sem, e.at(g, i))

            def const(k, rows, n):
                return consts[0:rows, k:k + 1].to_broadcast([rows, n])

            def dma_at(g, p):
                return (g - p) * 8 + 16

            def level_halves(v, h):
                b = v.rearrange("p (n s h) -> p n s h", s=2, h=h)
                return b[:, :, 0, :], b[:, :, 1, :]

            def level_rows(l):
                return slice(0, M) if l % 2 == 0 else slice(M, P)

            def pipeline(eng, step):
                step(0, 0, True, False, False, False)
                step(1, 1, True, True, False, False)
                step(2, 0, True, True, True, False)
                step(3, 1, True, True, True, True)
                with eng.Fori(2, NG // 2) as pair:
                    step(pair * 2, 0, True, True, True, True)
                    step(pair * 2 + 1, 1, True, True, True, True)
                step(NG, 0, False, True, True, True)
                step(NG + 1, 1, False, False, True, True)
                step(NG + 2, 0, False, False, False, True)

            block = ctx.enter_context(nc.Block())

            N_W = 13
            SLQ = 4
            sl_tmp = [xin[i] for i in range(2)]

            @block.sync
            def _(sp):
                for dst, src in (
                    (w_rk_sb[:], w_rk), (w_mg_sb[:], w_mg), (w0_sb[:], w0), (w1_sb[:], w1),
                    (cw_sb[:], conv_w), (cb_sb[:], conv_b), (rw_sb[:], res_w), (mb_sb[:, 0:1], mem_b),
                    (gam[:], gamma.partition_broadcast(P)), (bet[:], beta.partition_broadcast(P)),
                    (xf[0][0:1, :], gate_b1), (xf[0][32:33, :], gate_b1), (xf[0][64:65, :], gate_b1),
                ):
                    sp.dma_start(dst, src).then_inc(s_w, 16)
                sl = slopes.rearrange("t j g -> (t j g)").rearrange("(q n) -> q n", n=CPG * D)
                for q in range(D * GRID // (CPG * D)):
                    if q >= 2:
                        sp.wait_ge(s_slr, q - 1)
                    sp.dma_start(sl_tmp[q % 2][:].rearrange("p c d -> p (c d)"),
                                 sl[q].partition_broadcast(P)).then_inc(s_sl[q % 2], 16)
                sp.wait_ge(s_slr, D * GRID // (CPG * D))

                def step(g, p, front, gates, rec, back):
                    if front:
                        if not (isinstance(g, int) and g < 2):
                            wait(sp, e_xtr, g - 2, 3)
                            wait(sp, e_u, g - 2, 1)
                        sp.dma_start(xin[p][:], x_g[bass.ds(g, 1)].rearrange("g p c d -> (g p) c d")
                                     if not isinstance(g, int) else x_g[g]).then_inc(d_xin[p], 16)
                    if back:
                        b = g - 3
                        wait(sp, e_y, b, 1)
                        dst = y_g[b] if isinstance(b, int) else y_g[bass.ds(b, 1)].rearrange("g p c d -> (g p) c d")
                        sp.dma_start(dst, y[1 - p][:]).then_inc(d_yst[1 - p], 16)

                pipeline(sp, step)
                for p in range(2):
                    sp.wait_ge(d_yst[p], NG // 2 * 16)

            @block.tensor
            def _(pe):
                pe.wait_ge(s_w, 16 * N_W)
                pe.wait_ge(s_c, 2)
                pe.wait_ge(s_cv, 1)

                def step(g, p, front, gates, rec, back):
                    m, r = g - 1, g - 2

                    def before(k, n):
                        return not (isinstance(k, int) and k < n)

                    def fill(f):
                        if f == 0:
                            pe.wait_ge(d_xin[p], dma_at(g, p))
                        if f > 0:
                            wait(pe, e_xev, g, f - 1)
                        elif before(g, 1):
                            wait(pe, e_xev, g - 1, 3)
                        for k in range(4):
                            b, c = 2 * f + k // 2, k % 2
                            i = pe.transpose(TX[:, (b % 2) * T + c * P:(b % 2) * T + (c + 1) * P],
                                             xin[p][:, c, b * P:(b + 1) * P], ident[:])
                        i.then_inc(e_xtr.sem, 1)

                    def t_blocks(f):
                        wait(pe, e_xev, g, f)
                        if f == 0 and gates:
                            wait(pe, e_pr, m, 4)
                        for b in (2 * f, 2 * f + 1):
                            i = pe.matmul(PR[:, 0:T], w0_sb[:, b, :], xT[p][:, b, HIST:HIST + T],
                                          start=(b == 0), stop=(b == NB - 1))
                        if f == 3:
                            i.then_inc(e_t.sem, 1)

                    def gate_product(i):
                        c, h = i // 2, i % 2
                        if i == 0:
                            wait(pe, e_tev, m)
                        if i >= 2:
                            wait(pe, e_th, m, i - 2)
                        elif before(m, 2):
                            wait(pe, e_S, m - 2, i + 2)
                        cols = slice(h * HALF, (h + 1) * HALF)
                        pe.matmul(WK[h][:], tS[1 - p][:, c * P:(c + 1) * P], w1_sb[:, cols], start=True, stop=False)
                        pe.matmul(WK[h][:], ones_bf[:], b1_split[:, cols], start=False, stop=True).then_inc(e_c2.sem, 1)

                    def squares_sum():
                        wait(pe, e_ks, m)
                        if rec:
                            wait(pe, e_keTe, r)
                        pe.matmul(GA[:, T:2 * T], ones[0:M, 0:P], ksq[:], start=True, stop=True).then_inc(e_ssq.sem, 1)

                    def k_turned():
                        wait(pe, e_RE, r)
                        wait(pe, e_KE, r)
                        wait(pe, e_rkp, r)
                        wait(pe, e_n1, r)
                        if before(r, 1):
                            wait(pe, e_at0, r - 1, 1)
                        for c in range(CPG):
                            if c == 0:
                                scores(0)
                            i = pe.transpose(GA[:, T + c * M:T + (c + 1) * M],
                                             KE[p][M:P, SLOTS - 1, c * CH:(c + 1) * CH], ident[M:P, M:P])
                        i.then_inc(e_keT.sem, 1)

                    def scores(c):
                        if c:
                            wait(pe, e_at0, r, c - 1)
                        tok = slice(c * CH, (c + 1) * CH)
                        for l in (*range(1, LEVELS, 2), *range(0, LEVELS, 2)):
                            rows = level_rows(l)
                            if l == 0:
                                wait(pe, e_Ah, r, c)
                            later = level_halves(RE[p][rows, l // 2, tok], 2 ** l)[1]
                            i = pe.matmul(AB[:, l * 64:(l + 1) * 64], KE[p][rows, l // 2, tok], later,
                                          start=True, stop=True)
                            if l == LEVELS - 2:
                                i.then_inc(e_Ah.sem, 1)
                        pe.matmul(AB[:, NLV:NLV + 2], rkp[p][:, tok], ones[0:M, 0:2], start=True, stop=True)\
                          .then_inc(e_A.sem, 1)

                    def output(c):
                        if c == 0:
                            wait(pe, e_res, r, NB - 1)
                            if before(r, 1):
                                wait(pe, e_y, r - 1, 1)
                                wait(pe, e_S, r - 1, 3)
                        else:
                            wait(pe, e_y, r, 0)
                            wait(pe, e_S, r, 1)
                        wait(pe, e_AT, r, c * LEVELS + LEVELS - 1)
                        wait(pe, e_u, r, c)
                        tok = slice(c * CH, (c + 1) * CH)
                        for h in range(2):
                            cols = slice(h * HALF, (h + 1) * HALF)
                            pe.matmul(OB[:, cols], AT[c][:], th[p][c][:, cols], start=True, stop=False)
                            pe.matmul(OB[:, cols], RE[p][0:M, SLOTS - 1, tok], S[c][:, cols], start=False, stop=False)
                            for j in range(4):
                                b = 4 * h + j
                                i = pe.matmul(OB[:, b * P:(b + 1) * P], zT[p][:, b, tok], ident[:],
                                              is_transpose=True, start=False, stop=(j == 3))
                        i.then_inc(e_o.sem, 1)

                    def state(c):
                        for h in range(2):
                            if c == 0:
                                if gates:
                                    wait(pe, e_th, m, 2 + h)
                                elif before(r, 1):
                                    wait(pe, e_S, r - 1, 2 + h)
                                if h == 0:
                                    wait(pe, e_keTe, r)
                            else:
                                wait(pe, e_S, r, h)
                            pe.matmul(WK[h][0:M, :], keT_sb[:, c, :], th[p][c][:, h * HALF:(h + 1) * HALF],
                                      start=True, stop=True).then_inc(e_su.sem, 1)

                    if gates:
                        gate_product(0)
                        gate_product(1)
                    if rec:
                        k_turned()
                    if gates:
                        gate_product(2)
                        gate_product(3)
                        squares_sum()
                    if front:
                        fill(0)
                    if rec:
                        scores(1)
                    if front:
                        fill(1)
                        t_blocks(0)
                        fill(2)
                        t_blocks(1)
                    if rec:
                        output(0)
                        state(0)
                    if front:
                        fill(3)
                        t_blocks(2)
                        t_blocks(3)
                    if rec:
                        output(1)
                        state(1)
                    if front:
                        wait(pe, e_tev, g)
                        for half in range(2):
                            for b in range(NB):
                                if half == 0 and b % 4 == 0:
                                    wait(pe, e_silu, g, b // 4)
                                w = w_rk_sb if half == 0 else w_mg_sb
                                i = pe.matmul(PR[:, half * T:(half + 1) * T], w[:, b, :], shT[:, b, :],
                                              start=(b == 0), stop=(b == NB - 1))
                        i.then_inc(e_proj.sem, 1)

                pipeline(pe, step)

            @block.scalar
            def _(act):
                act.wait_ge(s_w, 16 * N_W)
                act.wait_ge(s_c, 2)
                act.wait_ge(s_slr, D * GRID // (CPG * D))
                nc.scalar.activation(th[0][0][:], th[0][1][:], ACT.Sign).then_inc(s_ss, 1)

                def step(g, p, front, gates, rec, back):
                    m, r, b = g - 1, g - 2, g - 3

                    def before(k, n):
                        return not (isinstance(k, int) and k < n)

                    def x_out(f):
                        wait(act, e_xtr, g, f)
                        if f == 0 and before(g, 2):
                            wait(act, e_conv, g - 2, NB * W - 1)
                            wait(act, e_res, g - 2, NB - 1)
                            wait(act, e_t, g - 2)
                        if f == 0 and before(g, 1):
                            wait(act, e_hist, g - 1)
                        nc.scalar.activation(xT[p][:, 2 * f:2 * f + 2, HIST:HIST + T],
                                             TX[:].rearrange("p (b t) -> p b t", b=2), ACT.Copy).then_inc(e_xev.sem, 1)

                    def tanh(i):
                        c, h = i // 2, i % 2
                        wait(act, e_c2, m, i)
                        if before(m, 2):
                            wait(act, e_su, m - 2, 2 * c + 1)
                        nc.scalar.activation(th[1 - p][c][:, h * HALF:(h + 1) * HALF], WK[h][:], ACT.Tanh, scale=0.5)\
                            .then_inc(e_th.sem, 1)

                    def y_out(c):
                        wait(act, e_o, r, c)
                        if c == 0 and before(r, 2):
                            act.wait_ge(d_yst[p], dma_at(r - 2, p))
                            wait(act, e_q, r - 2, 1)
                            wait(act, e_sq, r - 2, 1)
                        if c == 0 and before(r, 1):
                            wait(act, e_nm, r - 1, 1)
                        nc.scalar.activation(y[p][:, c, :], OB[:], ACT.Identity,
                                             accum_out=ysum[:, c:c + 1]).then_inc(e_y.sem, 1)

                    if gates:
                        wait(act, e_proj, m)
                        if before(m, 1):
                            wait(act, e_RE, m - 1)
                            wait(act, e_rkp, m - 1)
                            wait(act, e_kn, m - 1)
                            wait(act, e_l2, m - 1)
                            wait(act, e_tau, m - 1)
                        nc.scalar.activation(kk[:], PR[M:P, 0:T], ACT.Copy).then_inc(e_pr.sem, 1)
                        nc.scalar.activation(xs[:], PR[0:M, T:2 * T], ACT.Identity, bias=mb_sb[0:M, 0:1])\
                            .then_inc(e_pr.sem, 1)
                        tanh(0)
                        nc.scalar.activation(rr[0:M, :], PR[0:M, 0:T], ACT.Copy, scale=R_SCALE).then_inc(e_pr.sem, 1)
                        nc.scalar.activation(rr[M:P, :], PR[0:M, 0:T], ACT.Copy, scale=R_SCALE).then_inc(e_pr.sem, 1)
                        wait(act, e_pr, m, 1)
                        if before(m, 1):
                            wait(act, e_lg, m - 1)
                        nc.scalar.activation(xa[:], xs[:], ACT.Abs).then_inc(e_xa.sem, 1)
                        tanh(1)
                    if rec:
                        wait(act, e_keT, r)
                        if before(r, 1):
                            wait(act, e_su, r - 1, 3)
                        nc.scalar.activation(keT_sb[:], GA[:, T:T + CPG * M].rearrange("p (c m) -> p c m", c=CPG),
                                             ACT.Copy).then_inc(e_keTe.sem, 1)
                    if gates:
                        tanh(2)
                        tanh(3)
                        nc.scalar.activation(gen[:], PR[M:P, T:2 * T], ACT.Exp, scale=-1.0, bias=mb_sb[M:P, 1:2])\
                            .then_inc(e_pr.sem, 1)
                        wait(act, e_xa, m)
                        nc.scalar.activation(ge[:], xa[:], ACT.Exp, scale=-1.0).then_inc(e_ge.sem, 1)
                        wait(act, e_ge, m)
                        nc.scalar.activation(grw[:], ge[:], ACT.Ln, bias=two[0:M, :]).then_inc(e_gz.sem, 1)
                        wait(act, e_gz, m)
                        nc.scalar.activation(grw[:], grw[:], ACT.Exp, scale=-1.0).then_inc(e_grw.sem, 1)
                    if back:
                        for c in range(CPG):
                            wait(act, e_nm, b, c)
                            if before(b, 1):
                                wait(act, e_sc8, b - 1, 0)
                            nc.scalar.activation(sg[:, c, :], y[1 - p][:, c, :], ACT.Square, bias=nm[1 - p][:, c:c + 1],
                                                 accum_out=ssm[:, c:c + 1]).then_inc(e_sq.sem, 1)
                    if front:
                        x_out(0)
                        x_out(1)
                    if gates:
                        wait(act, e_n1, m)
                        nc.scalar.activation(nl[:], nl[:], ACT.Ln).then_inc(e_n2.sem, 1)
                    if front:
                        x_out(2)
                    if gates:
                        wait(act, e_sc, m)
                        nc.scalar.activation(lsel[:], gl[:], ACT.Ln).then_inc(e_ls.sem, 1)
                        wait(act, e_b, m)
                        nc.scalar.activation(bb[M:P, :], bb[0:M, :], ACT.Copy).then_inc(e_bd.sem, 1)
                    if rec:
                        y_out(0)
                    if front:
                        x_out(3)
                        wait(act, e_t, g)
                        if before(g, 2):
                            wait(act, e_c2, g - 2, 3)
                        nc.scalar.activation(tS[p][:], PR[:, 0:T], ACT.Copy).then_inc(e_tev.sem, 1)
                    if gates:
                        wait(act, e_ex, m)
                        nc.scalar.activation(kg[:], nl[:], ACT.Exp, bias=ln_fix[0:M, :]).then_inc(e_kg.sem, 1)
                        wait(act, e_kn, m)
                        nc.scalar.activation(kn[M:P, :], kn[0:M, :], ACT.Copy).then_inc(e_kd.sem, 1)
                    if rec:
                        y_out(1)
                    if gates:
                        wait(act, e_X, m)
                        if before(m, 1):
                            wait(act, e_KE, m - 1)
                            wait(act, e_dec, m - 1)
                        nc.scalar.activation(E[:, 0:4, :], X[:, 0:4, :], ACT.Exp).then_inc(e_E.sem, 1)
                        nc.scalar.activation(E[0:M, 4, :], bb[0:M, :], ACT.Exp).then_inc(e_E.sem, 1)
                        nc.scalar.activation(E[M:P, 4, :], X[M:P, 4, :], ACT.Exp).then_inc(e_E.sem, 1)
                    if front:
                        for h in range(2):
                            bs = slice(h * NB // 2, (h + 1) * NB // 2)
                            wait(act, e_conv, g, NB * W // 2 * (h + 1) - 1)
                            if before(g, 1):
                                wait(act, e_proj, g - 1)
                                wait(act, e_res, g - 1, NB - 1)
                            nc.scalar.activation(shT[:, bs, :], acc[:, bs, :], ACT.Silu).then_inc(e_silu.sem, 1)
                    if back:
                        for c in range(CPG):
                            wait(act, e_xf, b, c)
                            wait(act, e_sq, b, c)
                            nc.scalar.activation(sg[:, c, :], xf[c][:], ACT.Sign).then_inc(e_sg.sem, 1)

                pipeline(act, step)

            @block.vector
            def _(dve):
                v = nc.vector
                for q in range(D * GRID // (CPG * D)):
                    n = CPG * D // GRID
                    dve.wait_ge(s_sl[q % 2], 16 * (q // 2 + 1))
                    v.tensor_reduce(th[0][1][:, q * n:(q + 1) * n],
                                    sl_tmp[q % 2][:].rearrange("p c (d g) -> p (c d) g", g=GRID), AX_X, ALU.add)\
                        .then_inc(s_slr, 1)
                dve.wait_ge(s_w, 16 * N_W)
                dve.wait_ge(s_c, 2)
                v.tensor_scalar(mb_sb[:, 1:2], mb_sb[:, 0:1], -1.0, None, ALU.mult).then_inc(s_cv, 1)

                chain = [0]
                s_chain = s_setup

                def link(ins):
                    chain[0] += 1
                    ins.then_inc(s_chain, 1)
                    dve.wait_ge(s_chain, chain[0])

                link(v.memset(b1_split[:], 0.0))
                for row, parts in ((0, 1), (32, 2), (64, 3)):
                    rest = xf[0][row:row + 1, :]
                    part = sg[row:row + 1, 0, :]
                    for k in range(parts):
                        if k:
                            link(v.tensor_tensor(rest, rest, part, ALU.subtract))
                        link(v.tensor_copy(part if k < parts - 1 else b1_split[row:row + 1, :], rest))
                dve.wait_ge(s_ss, 1)
                link(v.tensor_tensor(gam[:], gam[:], th[0][0][:], ALU.mult))
                link(v.tensor_tensor(bet[:], bet[:], th[0][0][:], ALU.mult))
                link(v.memset(S[0][:], 0.0))
                link(v.memset(xT[0][:, :, 0:HIST], 0.0))

                def step(g, p, front, gates, rec, back):
                    m, r, b = g - 1, g - 2, g - 3

                    def before(k, n):
                        return not (isinstance(k, int) and k < n)

                    if back:
                        def affine(c):
                            wait(dve, e_y, b, c)
                            wait(dve, e_nm, b, c)
                            if before(b, 1):
                                wait(dve, e_sg, b - 1, c)
                            v.scalar_tensor_tensor(xf[c][:], y[1 - p][:, c, :], nm[1 - p][:, c:c + 1], gam[:],
                                                   ALU.add, ALU.mult).then_inc(e_q.sem, 1)
                            wait(dve, e_q, b, c)
                            wait(dve, e_st, b, 8)
                            v.scalar_tensor_tensor(xf[c][:], xf[c][:], st[:, 5, c:c + 1], bet[:], ALU.mult, ALU.add)\
                                .then_inc(e_xf.sem, 1)

                    def conv_round(h, i):
                        for j in range(NB // 2):
                            blk = h * (NB // 2) + j
                            n = (h * W + i) * (NB // 2) + j
                            src = xT[p][:, blk, i:i + T]
                            wt = cw_sb[:, blk, i:i + 1]
                            if i == 0:
                                if j == 0:
                                    wait(dve, e_xev, g, 2 * h + 1)
                                    wait(dve, e_hist, g)
                                    if before(g, 1):
                                        wait(dve, e_silu, g - 1, h)
                                v.tensor_scalar(acc[:, blk, :], src, wt, cb_sb[:, blk:blk + 1], ALU.mult, ALU.add)\
                                    .then_inc(e_conv.sem, 1)
                            else:
                                wait(dve, e_conv, g, n - NB // 2)
                                v.scalar_tensor_tensor(acc[:, blk, :], src, wt, acc[:, blk, :], ALU.mult, ALU.add)\
                                    .then_inc(e_conv.sem, 1)

                    def history():
                        if not (isinstance(g, int) and g == 0):
                            wait(dve, e_xev, g - 1, 3)
                            if not (isinstance(g, int) and g < 2):
                                wait(dve, e_conv, g - 2, NB * W - 1)
                            k = keep[:, g:g + 1] if isinstance(g, int) else keep[:, bass.ds(g, 1)]
                            v.tensor_scalar(xT[p][:, :, 0:HIST], xT[1 - p][:, :, T:T + HIST], k, None, ALU.mult)\
                                .then_inc(e_hist.sem, 1)
                        else:
                            v.memset(xT[p][:, :, 0:HIST], 0.0).then_inc(e_hist.sem, 1)

                    def masked(c):
                        wait(dve, e_A, r, c)
                        if c == 1:
                            wait(dve, e_AT, r, LEVELS - 1)
                        elif before(r, 1):
                            wait(dve, e_AT, r - 1, 2 * LEVELS - 1)
                        v.tensor_tensor(Wm[:], AB[:, 0:NLV].rearrange("p (l t) -> p l t", l=LEVELS), mask[:], ALU.mult)\
                            .then_inc(e_Wm.sem, 1)
                        if before(r, 1):
                            wait(dve, e_o, r - 1, c)
                        v.tensor_scalar(AT[c][:], ident[:], AB[:, NLV:NLV + 1], None, ALU.mult).then_inc(e_at0.sem, 1)

                    def gate(c):
                        wait(dve, e_th, m, 2 * c + 1)
                        v.scalar_tensor_tensor(th[1 - p][c][:], th[1 - p][c][:], 1.0, xin[1 - p][:, c, :],
                                               ALU.add, ALU.mult).then_inc(e_u.sem, 1)

                    def decay(c):
                        for h in range(2):
                            cols = slice(h * HALF, (h + 1) * HALF)
                            wait(dve, e_su, r, 2 * c + h)
                            if c == 0:
                                wait(dve, e_dec, r)
                                if before(r, 1):
                                    wait(dve, e_o, r - 1, 1)
                                    wait(dve, e_S, r - 1, 2 + h)
                            else:
                                wait(dve, e_o, r, 0)
                                wait(dve, e_S, r, h)
                            v.scalar_tensor_tensor(S[1 - c][:, cols], S[c][:, cols], dec[p][:, c:c + 1],
                                                   WK[h][0:M, :], ALU.mult, ALU.add).then_inc(e_S.sem, 1)

                    def residual(lo, hi):
                        for blk in range(lo, hi):
                            wait(dve, e_silu, g, blk // 4)
                            if rec and blk == 0:
                                wait(dve, e_o, r, 1)
                            v.scalar_tensor_tensor(zT[p][:, blk, :], shT[:, blk, :], rw_sb[:, blk:blk + 1],
                                                   xT[p][:, blk, HIST:HIST + T], ALU.mult, ALU.add)\
                                .then_inc(e_res.sem, 1)

                    if front:
                        history()
                    if gates:
                        gate(0)
                    if rec:
                        masked(0)
                    if gates:
                        gate(1)
                        wait(dve, e_d, m)
                        if before(m, 1):
                            wait(dve, e_tl, m - 1)
                        v.reciprocal(tau[:], gen[:]).then_inc(e_tau.sem, 1)
                        wait(dve, e_ssq, m)
                        if before(m, 1):
                            wait(dve, e_kg, m - 1)
                        v.tensor_scalar(nl[:], GA[0:M, T:2 * T], SS_SCALE, 1e-24 * SS_SCALE, ALU.mult, ALU.max)\
                            .then_inc(e_n1.sem, 1)
                    if rec:
                        masked(1)
                    if gates:
                        wait(dve, e_gl, m)
                        v.tensor_scalar(grw[:], gl[:], ATANH[4], None, ALU.mult).then_inc(e_gq.sem, 1)
                        for k in (3, 2, 1):
                            wait(dve, e_gq, m, 3 - k)
                            v.scalar_tensor_tensor(grw[:], grw[:], ATANH[k], gl[:], ALU.add, ALU.mult)\
                                .then_inc(e_gq.sem, 1)
                        wait(dve, e_gq, m, 3)
                        v.scalar_tensor_tensor(grw[:], grw[:], ATANH[0], gw1[:], ALU.add, ALU.mult).then_inc(e_lg.sem, 1)
                        wait(dve, e_lg, m)
                        v.scalar_tensor_tensor(sel[:], xs[:], 0.0, grw[:], ALU.max, ALU.add).then_inc(e_sel.sem, 1)
                        wait(dve, e_sel, m)
                        v.tensor_scalar(gl[:], sel[:], SEL_MIN, None, ALU.max).then_inc(e_sc.sem, 1)
                    if back:
                        affine(0)
                    if gates:
                        wait(dve, e_gn, m)
                        if before(m, 1):
                            wait(dve, e_X, m - 1)
                            wait(dve, e_E, m - 1, 1)
                            wait(dve, e_bd, m - 1)
                        for c in range(CPG):
                            tok = slice(c * CH, (c + 1) * CH)
                            i = v.tensor_tensor_scan(bb[0:M, tok], ones[0:M, 0:CH], gn[:, tok], 0.0, ALU.mult, ALU.subtract)
                        i.then_inc(e_b.sem, 1)
                    if front:
                        conv_round(0, 0)
                    if gates:
                        wait(dve, e_ls, m)
                        v.tensor_tensor(lsel[:], lsel[:], xs[:], ALU.min).then_inc(e_l2.sem, 1)
                    if front:
                        conv_round(0, 1)
                        conv_round(0, 2)
                    if gates:
                        wait(dve, e_tl, m)
                        wait(dve, e_n2, m)
                        v.scalar_tensor_tensor(nl[:], nl[:], -0.5, tl[:], ALU.mult, ALU.add).then_inc(e_ex.sem, 1)
                    if rec:
                        decay(0)
                    if front:
                        conv_round(0, 3)
                        conv_round(1, 0)
                        conv_round(1, 1)
                    if gates:
                        wait(dve, e_E, m, 1)
                        k = keep[0:M, m:m + 1] if isinstance(m, int) else keep[0:M, bass.ds(m, 1)]
                        v.tensor_scalar(E[0:M, 4, 0:CH], E[0:M, 4, 0:CH], k, None, ALU.mult).then_inc(e_Ek.sem, 1)
                        wait(dve, e_E, m, 2)
                        wait(dve, e_Ek, m)
                        if before(m, 2):
                            wait(dve, e_o, m - 2, 1)
                            wait(dve, e_A, m - 2, 1)
                            wait(dve, e_S, m - 2, 3)
                        v.tensor_copy(dec[1 - p][:], E[0:M, 4, :].rearrange("m (c t) -> m c t", c=CPG)[:, :, CH - 1])\
                            .then_inc(e_dec.sem, 1)
                        v.tensor_tensor(RE[1 - p][:], E[:], rr[:].unsqueeze(1).to_broadcast([P, SLOTS, T]), ALU.mult)\
                            .then_inc(e_RE.sem, 1)
                    if front:
                        conv_round(1, 2)
                        conv_round(1, 3)
                    if rec:
                        decay(1)
                    if back:
                        affine(1)
                    if front:
                        residual(0, 8)
                    if back:
                        for c in range(CPG):
                            wait(dve, e_sg, b, c)
                        k = [0]

                        def then(ins):
                            ins.then_inc(e_sc8.sem, 1)
                            wait(dve, e_sc8, b, k[0])
                            k[0] += 1

                        then(v.tensor_reduce(ts[:], sg[:].rearrange("p c (t j) -> p c t j", j=DS), AX_X, ALU.add))
                        then(v.tensor_reduce(cl[:], ts[:].rearrange("p c (n t) -> p c n t", t=TPC), AX_X, ALU.add))
                        then(v.scalar_tensor_tensor(cl[:], cl[:], 4096.0,
                                                    c_cluster[:].unsqueeze(1).to_broadcast([P, CPG, NCL]),
                                                    ALU.mult, ALU.add))
                        then(v.scalar_tensor_tensor(key[:], ts[:], 8.0,
                                                    c_tile[:].unsqueeze(1).to_broadcast([P, CPG, NT]),
                                                    ALU.mult, ALU.add))
                        k4 = key[:].rearrange("p c (n t) -> p c n t", t=TPC)
                        then(v.tensor_tensor(k4, k4, cl[:].unsqueeze(3).to_broadcast([P, CPG, NCL, TPC]), ALU.add))
                        then(v.tensor_reduce(kmax[:], key[:], AX_X, ALU.max))
                        for c in range(CPG):
                            i = v.scalar_tensor_tensor(ts[:, c, :], key[:, c, :], kmax[:, c:c + 1], iota_t[:],
                                                       ALU.is_equal, ALU.mult)
                        then(i)
                        b2 = b * CPG
                        dst = idx_all[:, b2:b2 + CPG] if isinstance(b, int) else idx_all[:, bass.ds(b2, CPG)]
                        then(v.tensor_reduce(dst, ts[:], AX_X, ALU.add))

                pipeline(dve, step)

            @block.gpsimd
            def _(pool):
                q = nc.gpsimd
                q.memset(ident[:], 0.0).then_inc(s_pc, 1)
                q.memset(ones[:], 1.0)
                q.memset(ones_bf[:], 1.0)
                q.memset(minus_half[:], -0.5)
                for k, value in ((MINUS_1_D, -1.0 / D), (ONE_D, 1.0 / D), (EPS, LN_EPS)):
                    q.memset(consts[:, k:k + 1], value)
                q.memset(two[:], 2.0)
                q.memset(ln_fix[:], 10.0 * 0.6931471805599453)
                q.memset(mask[:], 1.0)
                q.memset(X[:], 0.0)
                q.memset(keep[:], 1.0).then_inc(s_pc, 1)
                pool.wait_ge(s_pc, 2)
                q.memset(keep[:].rearrange("p (b g) -> p b g", b=B)[:, :, 0:1], 0.0)
                q.affine_select(out=ident[:], in_=ident[:], compare_op=ALU.not_equal, fill=1.0, base=0,
                                pattern=[[-1, P]], channel_multiplier=1).then_inc(s_pc, 1)
                for l in range(LEVELS):
                    h = 2 ** l
                    mv = mask[:, l, :].rearrange("p (n h) -> p n h", h=h)
                    q.affine_select(out=mv, in_=mv, compare_op=ALU.is_ge, fill=0.0, base=0,
                                    pattern=[[-2 * h, 64 // h], [0, h]], channel_multiplier=1).then_inc(s_pc, 1)
                    pool.wait_ge(s_pc, 4 + 2 * l)
                    q.affine_select(out=mv, in_=mv, compare_op=ALU.is_ge, fill=0.0, base=h - 1,
                                    pattern=[[2 * h, 64 // h], [0, h]], channel_multiplier=-1).then_inc(s_pc, 1)
                q.iota(iota_t[:], pattern=[[1, NT]], base=0, channel_multiplier=0, allow_small_or_imprecise_dtypes=True)
                q.iota(c_tile[:].rearrange("p (n t) -> p n t", t=TPC), pattern=[[0, NCL], [-1, TPC]], base=TPC - 1,
                       channel_multiplier=0, allow_small_or_imprecise_dtypes=True)
                q.iota(c_cluster[:], pattern=[[-512, NCL]], base=512 * (NCL - 1), channel_multiplier=0,
                       allow_small_or_imprecise_dtypes=True).then_inc(s_c, 2)

                def step(g, p, front, gates, rec, back):
                    m, r, b = g - 1, g - 2, g - 3

                    def before(k, n):
                        return not (isinstance(k, int) and k < n)

                    def assemble(c):
                        wait(pool, e_Wm, r, c)
                        wait(pool, e_at0, r, c)
                        for l in range(LEVELS):
                            late = level_halves(AT[c][:], 2 ** l)[1]
                            if l:
                                wait(pool, e_AT, r, c * LEVELS + l - 1)
                            q.tensor_tensor(late, late, Wm[:, l, :].rearrange("p (n h) -> p n h", h=2 ** l), ALU.add)\
                                .then_inc(e_AT.sem, 1)

                    def mean(c):
                        wait(pool, e_y, r, c)
                        if c == 0 and before(r, 2):
                            wait(pool, e_keep, r - 2, 3)
                            wait(pool, e_q, r - 2, 1)
                        q.tensor_tensor(nm[p][:, c:c + 1], ysum[:, c:c + 1], const(MINUS_1_D, P, 1), ALU.mult)\
                            .then_inc(e_nm.sem, 1)

                    if gates:
                        wait(pool, e_pr, m, 0)
                        if before(m, 1):
                            wait(pool, e_ssq, m - 1)
                        q.tensor_tensor(ksq[:], kk[:], kk[:], ALU.mult).then_inc(e_ks.sem, 1)
                        wait(pool, e_pr, m, 4)
                        q.tensor_tensor(gen[:], gen[:], ones[0:M, :], ALU.add).then_inc(e_d.sem, 1)
                        wait(pool, e_grw, m)
                        q.tensor_tensor(gw1[:], grw[:], ge[:], ALU.mult).then_inc(e_gw1.sem, 1)
                        wait(pool, e_gw1, m)
                        q.tensor_tensor(gl[:], gw1[:], gw1[:], ALU.mult).then_inc(e_gl.sem, 1)
                    if rec:
                        assemble(0)
                    if back:
                        k = [0]

                        def then(ins):
                            ins.then_inc(e_st.sem, 1)
                            wait(pool, e_st, b, k[0])
                            k[0] += 1

                        wait(pool, e_sq, b, 1)
                        if not (isinstance(b, int) and b == 0):
                            wait(pool, e_xf, b - 1, 1)
                        then(q.tensor_tensor(st[:, 0, :], ssm[:], const(ONE_D, P, CPG), ALU.mult))
                        then(q.tensor_tensor(st[:, 0, :], st[:, 0, :], const(EPS, P, CPG), ALU.add))
                        then(q.tensor_tensor(st[:, 1, :], st[:, 0, :], minus_half[:], ALU.pow))
                        then(q.tensor_tensor(st[:, 2, :], st[:, 1, :], st[:, 1, :], ALU.mult))
                        then(q.tensor_tensor(st[:, 3, :], st[:, 2, :], ssm[:], ALU.mult))
                        then(q.tensor_tensor(st[:, 4, :], st[:, 3, :], const(ONE_D, P, CPG), ALU.mult))
                        then(q.tensor_tensor(st[:, 4, :], st[:, 4, :], const(EPS, P, CPG), ALU.add))
                        then(q.tensor_tensor(st[:, 4, :], st[:, 4, :], minus_half[:], ALU.pow))
                        then(q.tensor_tensor(st[:, 5, :], st[:, 4, :], st[:, 1, :], ALU.mult))
                        for dst, src in ((nm_all, nm[1 - p][:]), (r1_all, st[:, 1, :]), (r12_all, st[:, 5, :]), (ss_all, st[:, 3, :])):
                            col = slice(b * CPG, (b + 1) * CPG) if isinstance(b, int) else bass.ds(b * CPG, CPG)
                            q.tensor_copy(dst[:, col], src).then_inc(e_keep.sem, 1)
                    if gates:
                        wait(pool, e_sel, m)
                        wait(pool, e_tau, m)
                        if before(m, 1):
                            wait(pool, e_b, m - 1)
                        q.tensor_tensor(gn[:], sel[:], tau[:], ALU.mult).then_inc(e_gn.sem, 1)
                    if rec:
                        assemble(1)
                    if gates:
                        wait(pool, e_l2, m)
                        if before(m, 1):
                            wait(pool, e_ex, m - 1)
                        q.tensor_tensor(tl[:], tau[:], lsel[:], ALU.mult).then_inc(e_tl.sem, 1)
                        wait(pool, e_b, m)
                        if before(m, 1):
                            wait(pool, e_E, m - 1, 2)
                        for l in (*range(0, LEVELS, 2), *range(1, LEVELS, 2)):
                            if l == 1:
                                wait(pool, e_bd, m)
                                wait(pool, e_Xl, m)
                            h, rows = 2 ** l, level_rows(l)
                            b_early, b_late = level_halves(bb[rows, :], h)
                            x_early, x_late = level_halves(X[rows, l // 2, :], h)
                            ref = b_early[:, :, h - 1:h].to_broadcast([M, T // (2 * h), h])
                            i = q.tensor_tensor(x_late, b_late, ref, ALU.subtract)
                            if l:
                                i = q.tensor_tensor(x_early, ref, b_early, ALU.subtract)
                            if l == LEVELS - 1:
                                i.then_inc(e_Xl.sem, 1)
                        bend = bb[M:P, :].rearrange("p (c t) -> p c t", c=CPG)
                        q.tensor_tensor(X[M:P, 4, :].rearrange("p (c t) -> p c t", c=CPG),
                                        bend[:, :, CH - 1:CH].to_broadcast([M, CPG, CH]), bend, ALU.subtract)\
                            .then_inc(e_X.sem, 1)
                        wait(pool, e_X, m)
                        wait(pool, e_kg, m)
                        if before(m, 1):
                            wait(pool, e_KE, m - 1)
                        q.tensor_tensor(kn[0:M, :], kk[:], kg[:], ALU.mult).then_inc(e_kn.sem, 1)
                        wait(pool, e_kn, m)
                        wait(pool, e_pr, m, 4)
                        if before(m, 2):
                            wait(pool, e_A, m - 2, 1)
                            wait(pool, e_keT, m - 2)
                        q.tensor_tensor(rkp[1 - p][:], rr[0:M, :], kn[0:M, :], ALU.mult).then_inc(e_rkp.sem, 1)
                    if rec:
                        mean(0)
                        mean(1)
                    if gates:
                        wait(pool, e_kd, m)
                        wait(pool, e_Ek, m)
                        wait(pool, e_E, m, 2)
                        q.tensor_tensor(KE[1 - p][:], E[:], kn[:].unsqueeze(1).to_broadcast([P, SLOTS, T]), ALU.mult)\
                            .then_inc(e_KE.sem, 1)

                pipeline(pool, step)

        with ExitStack() as ctx:
            def sb(name, shape, dt=F32):
                return ctx.enter_context(nc.sbuf_tensor(name, shape, dt))

            def psum(name, shape, dt=F32):
                return ctx.enter_context(nc.psum_tensor(name, shape, dt))

            def sem(name):
                return ctx.enter_context(nc.semaphore(name))

            BT = 8
            NBT = NC // BT
            assert NC % 16 == 0
            TC = 2 * DS * GRID
            assert TC == HALF
            gidx_f = sb("gidx_f", [P, NC])
            gidx = sb("gidx", [P, NC], U32)
            iota_g = sb("iota_g", [P, GRID])
            y_sl = sb("y_sl", [P, NC, DS])
            oh = sb("oh", [P, NC, NT], BF16)
            ohT = sb("ohT", [NT, NC, P], BF16)
            pen = sb("pen", [P, NC, NT])
            pick = sb("pick", [P, NC, NT])
            t1 = sb("t1", [NT, 2 * DS])
            t1s = sb("t1s", [NT, 3, 2 * DS], BF16)
            t2 = sb("t2", [NT, TC])
            t2s = sb("t2s", [NT, 3, TC], BF16)
            t3 = sb("t3", [NT, 4])
            t3s = sb("t3s", [NT, 3, 4], BF16)
            gb = sb("gb", [P, NC, 2 * DS])
            x1s = sb("x1s", [P, NC, DS])
            xfs = sb("xfs", [P, NC, DS])
            mm = sb("mm", [P, 2, NC])
            ext = sb("ext", [P, 2, NT])
            rng3 = sb("rng3", [P, NC, 4])
            rng = sb("rng", [P, NC])
            gcell = sb("gcell", [P, NC, DS])
            tmp = sb("tmp", [P, NC, DS])
            ohg = sb("ohg", [P, 2, DS, GRID])
            pr = sb("pr", [P, 2, TC])
            bsv = sb("bsv", [P, BT, 2, DS])
            dl = sb("dl", [P, BT, DS])
            w_a = sb("w_a", [P, BT, DS])
            sm = sb("sm", [P, 8, BT])
            coef = sb("coef", [P, 2, 2, BT])
            outs = sb("outs", [P, NC, DS])
            mh8 = sb("mh8", [P, BT])
            ident_bf = sb("ident_bf", [P, P], BF16)
            rows = [sb(f"rows{i}", [P, BT, D]) for i in range(2)]

            Z = [psum(f"Z{i}", [P, HALF]) for i in range(4)]
            OT = [psum(f"OT{i}", [NT, 8, P], BF16) for i in range(2)]
            QA = psum("QA", [P, HALF])
            QB = psum("QB", [P, HALF])

            p_tab, p_i, p_gi, p_gat = sem("p_tab"), sem("p_i"), sem("p_gi"), sem("p_gat")
            p_oh, p_ohT, p_ohTe, p_t1, p_g1, p_g1e = (sem(n) for n in ("p_oh", "p_ohT", "p_ohTe", "p_t1", "p_g1", "p_g1e"))
            p_v, p_ext, p_extT, p_t3, p_r3, p_u = (sem(n) for n in ("p_v", "p_ext", "p_extT", "p_t3", "p_r3", "p_u"))
            p_z, p_zf, p_b, p_coef, p_pw, p_ve = (sem(n) for n in ("p_z", "p_zf", "p_b", "p_coef", "p_pw", "p_ve"))
            p_row, p_sc, p_bb, p_g = (sem(n) for n in ("p_row", "p_sc", "p_bb", "p_g"))
            p_ld = [[sem(f"p_ld{p}{h}") for h in range(2)] for p in range(2)]
            p_st = [sem(f"p_st{p}") for p in range(2)]
            VB = 14

            y_b = y_dram.rearrange("(q n p) d -> q p n d", n=BT, p=P)
            out_b = out.rearrange("b l d -> (b l) d").rearrange("(q n p) d -> q p n d", n=BT, p=P)
            block = ctx.enter_context(nc.Block())

            @block.sync
            def _(sp):
                sp.dma_start(t1[:, 0:DS], gamma.rearrange("(t j) -> t j", j=DS)).then_inc(p_tab, 16)
                sp.dma_start(t1[:, DS:2 * DS], beta.rearrange("(t j) -> t j", j=DS)).then_inc(p_tab, 16)
                sp.dma_start(t2[:, 0:TC // 2], bases.rearrange("t j g -> t (j g)")).then_inc(p_tab, 16)
                sp.dma_start(t2[:, TC // 2:TC], slopes.rearrange("t j g -> t (j g)")).then_inc(p_tab, 16)
                sp.dma_start(t3[:, 2:3], oscale).then_inc(p_tab, 16)

                def load(q, p):
                    src = y_b[q] if isinstance(q, int) else y_b[bass.ds(q, 1)].rearrange("q p n d -> (q p) n d")
                    for h in range(2):
                        hs = slice(h * BT // 2, (h + 1) * BT // 2)
                        sp.dma_start(rows[p][:, hs, :], src[:, hs, :]).then_inc(p_ld[p][h], 16)

                def store(q, p):
                    dst = out_b[q] if isinstance(q, int) else out_b[bass.ds(q, 1)].rearrange("q p n d -> (q p) n d")
                    for h in range(2):
                        hs = slice(h * BT // 2, (h + 1) * BT // 2)
                        sp.wait_ge(p_row, q * BT + (h + 1) * BT // 2)
                        sp.dma_start(dst[:, hs, :], rows[p][:, hs, :]).then_inc(p_st[p], 16)

                load(0, 0)
                load(1, 1)
                with sp.Fori(0, NBT // 2 - 1) as pair:
                    for p in range(2):
                        store(pair * 2 + p, p)
                        sp.wait_ge(p_st[p], pair * 32 + 32)
                        load(pair * 2 + p + 2, p)
                for p in range(2):
                    store(NBT - 2 + p, p)
                for p in range(2):
                    sp.wait_ge(p_st[p], 16 * NBT)

            @block.gpsimd
            def _(pool):
                q = nc.gpsimd
                q.iota(gidx_f[:], pattern=[[P * NT, NC]], base=0, channel_multiplier=NT,
                       allow_small_or_imprecise_dtypes=True).then_inc(p_i, 1)
                q.iota(iota_g[:], pattern=[[1, GRID]], base=0, channel_multiplier=0,
                       allow_small_or_imprecise_dtypes=True).then_inc(p_i, 1)
                q.memset(mh8[:], -0.5).then_inc(p_i, 1)
                pool.wait_ge(p_gi, 1)
                for n in range(NC):
                    q.indirect_dma_start(y_sl[:, n, :], None, y_slices,
                                         bass.IndirectOffsetOnAxis(ap=gidx[:, n:n + 1], axis=0)).then_inc(p_gat, 16)

                def batch(k):
                    pool.wait_ge(p_ve, k + 1)
                    q.tensor_tensor(sm[:, 6, :], sm[:, 5, :], mh8[:], ALU.pow).then_inc(p_pw, 1)

                pool.wait_ge(p_i, 3)
                with pool.Fori(0, NBT) as k:
                    batch(k)
                pool.wait_ge(p_b, VB * NBT)
                for p in range(2):
                    pool.wait_ge(p_st[p], 16 * NBT)
                for n in range(NC):
                    q.indirect_dma_start(out_slices, bass.IndirectOffsetOnAxis(ap=gidx[:, n:n + 1], axis=0),
                                         outs[:, n, :], None).then_inc(p_sc, 16)
                pool.wait_ge(p_sc, 16 * NC)

            @block.tensor
            def _(pe):
                pe.wait_ge(p_oh, 2)
                for f in range(NC // 8):
                    if f >= 2:
                        pe.wait_ge(p_ohTe, f - 1)
                    for j in range(8):
                        i = pe.transpose(OT[f % 2][:, j, :], oh[:, f * 8 + j, :], ident_bf[:])
                    i.then_inc(p_ohT, 1)
                pe.wait_ge(p_ohTe, NC // 8)
                pe.wait_ge(p_t1, 1)
                for f in range(NC // 16):
                    for j in range(16):
                        for k in range(3):
                            i = pe.matmul(Z[f % 4][:, j * 32:(j + 1) * 32], ohT[:, f * 16 + j, :], t1s[:, k, :],
                                          start=(k == 0), stop=(k == 2))
                    i.then_inc(p_g1, 1)
                pe.wait_ge(p_ext, 1)
                for k in range(2):
                    i = pe.transpose(QA[0:NT, k * P:(k + 1) * P], ext[:, k, :], ident[:])
                i.then_inc(p_extT, 1)
                pe.wait_ge(p_t3, 1)
                for n in range(NC):
                    for k in range(3):
                        i = pe.matmul(QB[:, n * 4:(n + 1) * 4], ohT[:, n, :], t3s[:, k, :], start=(k == 0), stop=(k == 2))
                i.then_inc(p_r3, 1)
                pe.wait_ge(p_g1e, NC // 16)

                def tables(n, j):
                    if not isinstance(n, int):
                        pe.wait_ge(p_zf, n - 3)
                    elif n >= 4:
                        pe.wait_ge(p_zf, n - 3)
                    lhs = ohT[:, n, :] if isinstance(n, int) else ohT[:, bass.ds(n, 1), :].rearrange("t n p -> t (n p)")
                    for k in range(3):
                        i = pe.matmul(Z[j % 4][:], lhs, t2s[:, k, :], start=(k == 0), stop=(k == 2))
                    i.then_inc(p_z, 1)

                for j in range(4):
                    tables(j, j)
                with pe.Fori(1, NC // 4) as four:
                    for j in range(4):
                        tables(four * 4 + j, j)

            @block.scalar
            def _(act):
                for f in range(NC // 8):
                    act.wait_ge(p_ohT, f + 1)
                    nc.scalar.activation(ohT[:, f * 8:(f + 1) * 8, :], OT[f % 2][:], ACT.Copy).then_inc(p_ohTe, 1)
                for f in range(NC // 16):
                    act.wait_ge(p_g1, f + 1)
                    nc.scalar.activation(gb[:, f * 16:(f + 1) * 16, :],
                                         Z[f % 4][:].rearrange("p (n j) -> p n j", n=16), ACT.Copy).then_inc(p_g1e, 1)

                def scale_rows(k, p):
                    act.wait_ge(p_coef, k + 1)
                    for h in range(2):
                        act.wait_ge(p_ld[p][h], (k - p) * 8 + 16)
                        for n in range(h * BT // 2, (h + 1) * BT // 2):
                            nc.scalar.activation(rows[p][:, n, :], rows[p][:, n, :], ACT.Identity,
                                                 scale=coef[:, p, 0, n:n + 1], bias=coef[:, p, 1, n:n + 1])\
                                .then_inc(p_row, 1)

                with act.Fori(0, NBT // 2) as pair:
                    for p in range(2):
                        scale_rows(pair * 2 + p, p)

            @block.vector
            def _(dve):
                v = nc.vector
                count = [0]

                def link(ins):
                    count[0] += 1
                    ins.then_inc(p_v, 1)
                    dve.wait_ge(p_v, count[0])

                dve.wait_ge(p_i, 1)
                v.tensor_tensor(gidx[:], gidx_f[:], idx_all[:], ALU.add).then_inc(p_gi, 1)
                v.tensor_copy(ident_bf[:], ident[:]).then_inc(p_oh, 1)
                v.tensor_tensor(oh[:], iota_t[:].unsqueeze(1).to_broadcast([P, NC, NT]),
                                idx_all[:].unsqueeze(2).to_broadcast([P, NC, NT]), ALU.is_equal).then_inc(p_oh, 1)
                dve.wait_ge(p_tab, 16 * 5)

                def split(dst, src):
                    for k in range(3):
                        link(v.tensor_copy(dst[:, k, :], src))
                        if k < 2:
                            link(v.tensor_tensor(src, src, dst[:, k, :], ALU.subtract))

                split(t1s, t1[:])
                v.memset(t3[:, 3:4], 0.0).then_inc(p_t1, 1)
                split(t2s, t2[:])
                dve.wait_ge(p_oh, 2)
                link(v.tensor_scalar(pen[:], oh[:], BIG, -BIG, ALU.mult, ALU.add))

                def per_tile(a):
                    return a.unsqueeze(2).to_broadcast([P, NC, DS])

                dve.wait_ge(p_gat, 16 * NC)
                dve.wait_ge(p_g1e, NC // 16)
                link(v.tensor_tensor(xfs[:], y_sl[:], per_tile(nm_all[:]), ALU.add))
                link(v.tensor_tensor(x1s[:], xfs[:], per_tile(r1_all[:]), ALU.mult))
                link(v.tensor_tensor(xfs[:], xfs[:], per_tile(r12_all[:]), ALU.mult))
                link(v.tensor_tensor(xfs[:], xfs[:], gb[:, :, 0:DS], ALU.mult))
                link(v.tensor_tensor(xfs[:], xfs[:], gb[:, :, DS:2 * DS], ALU.add))
                link(v.tensor_reduce(mm[:, 0, :], xfs[:], AX_X, ALU.max))
                link(v.tensor_reduce(mm[:, 1, :], xfs[:], AX_X, ALU.min))
                link(v.tensor_scalar(mm[:, 1, :], mm[:, 1, :], -1.0, None, ALU.mult))
                for k in range(2):
                    link(v.tensor_tensor(pick[:], oh[:], mm[:, k, :].unsqueeze(2).to_broadcast([P, NC, NT]), ALU.mult))
                    link(v.tensor_tensor(pick[:], pick[:], pen[:], ALU.add))
                    link(v.tensor_reduce(ext[:, k, :], pick[:].rearrange("p n t -> p t n"), AX_X, ALU.max))
                v.memset(sm[:], 0.0).then_inc(p_ext, 1)
                dve.wait_ge(p_extT, 1)
                link(v.tensor_reduce(t3[:, 0:2], QA[0:NT, 0:2 * P].rearrange("t (k p) -> t k p", k=2), AX_X, ALU.max))
                split(t3s, t3[:])
                v.memset(sm[:], 0.0).then_inc(p_t3, 1)
                dve.wait_ge(p_r3, 1)
                link(v.tensor_copy(rng3[:], QB[:, 0:NC * 4].rearrange("p (n k) -> p n k", k=4)))
                link(v.scalar_tensor_tensor(rng[:], rng3[:, :, 0], 0.0, rng3[:, :, 1], ALU.add, ALU.add))
                link(v.tensor_scalar(rng[:], rng[:], 1e-8, None, ALU.add))
                link(v.reciprocal(rng[:], rng[:]))
                link(v.tensor_tensor(xfs[:], xfs[:], per_tile(rng3[:, :, 1]), ALU.add))
                link(v.tensor_tensor(xfs[:], xfs[:], per_tile(rng[:]), ALU.mult))
                link(v.tensor_scalar(xfs[:], xfs[:], 0.0, 1.0 - 1e-6, ALU.max, ALU.min))
                link(v.tensor_scalar(xfs[:], xfs[:], float(GRID), None, ALU.mult))
                link(v.tensor_scalar(gcell[:], xfs[:], MAGIC, None, ALU.add))
                link(v.tensor_scalar(gcell[:], gcell[:], -MAGIC, None, ALU.add))
                link(v.tensor_tensor(tmp[:], gcell[:], xfs[:], ALU.is_gt))
                link(v.tensor_tensor(gcell[:], gcell[:], tmp[:], ALU.subtract))
                link(v.tensor_tensor(xfs[:], xfs[:], gcell[:], ALU.subtract))
                dve.wait_ge(p_i, 3)

                def batch(k, p):
                    n0 = k * BT
                    at = bass.ds(n0, BT)
                    for j in range(BT):
                        n = n0 + j
                        gc = gcell[:, bass.ds(n, 1), :].rearrange("p n j -> p (n j)").unsqueeze(2)\
                            .to_broadcast([P, DS, GRID])
                        pj = pr[:, j % 2, :].rearrange("p (k j g) -> p k j g", k=2, g=GRID)
                        v.tensor_tensor(ohg[:, j % 2, :, :], iota_g[:].unsqueeze(1).to_broadcast([P, DS, GRID]), gc,
                                        ALU.is_equal).then_inc(p_g, 1)
                        dve.wait_ge(p_z, n + 1)
                        dve.wait_ge(p_g, n + 1)
                        v.tensor_tensor(pj, Z[j % 4][:].rearrange("p (k j g) -> p k j g", k=2, g=GRID),
                                        ohg[:, j % 2, :, :].unsqueeze(1).to_broadcast([P, 2, DS, GRID]), ALU.mult)\
                            .then_inc(p_zf, 1)
                        dve.wait_ge(p_zf, n + 1)
                        v.tensor_reduce(bsv[:, j, :, :], pj, AX_X, ALU.add).then_inc(p_bb, 1)
                    c = [0]

                    def then(ins):
                        ins.then_inc(p_b, 1)
                        c[0] += 1
                        dve.wait_ge(p_b, k * VB + c[0])

                    def by_tile(a):
                        return a.unsqueeze(2).to_broadcast([P, BT, DS])

                    dve.wait_ge(p_bb, (k + 1) * BT)
                    x_at = x1s[:, at, :]
                    then(v.tensor_tensor(dl[:], bsv[:, :, 1, :], xfs[:, at, :], ALU.mult))
                    then(v.tensor_tensor(dl[:], dl[:], bsv[:, :, 0, :], ALU.add))
                    then(v.tensor_tensor(dl[:], dl[:], rng3[:, at, 2:3].to_broadcast([P, BT, DS]), ALU.mult))
                    then(v.tensor_reduce(sm[:, 0, :], dl[:], AX_X, ALU.add))
                    then(v.scalar_tensor_tensor(w_a[:], x_at, 4.0, dl[:], ALU.mult, ALU.add))
                    then(v.tensor_tensor(w_a[:], w_a[:], dl[:], ALU.mult))
                    then(v.tensor_reduce(sm[:, 1, :], w_a[:], AX_X, ALU.add))
                    then(v.tensor_scalar(sm[:, 0, :], sm[:, 0, :], 1.0 / D, None, ALU.mult))
                    then(v.scalar_tensor_tensor(sm[:, 1, :], ss_all[:, at], 4.0, sm[:, 1, :], ALU.mult, ALU.add))
                    then(v.tensor_tensor(sm[:, 2, :], sm[:, 0, :], sm[:, 0, :], ALU.mult))
                    then(v.scalar_tensor_tensor(sm[:, 1, :], sm[:, 1, :], 1.0 / D, sm[:, 2, :], ALU.mult, ALU.subtract))
                    v.tensor_scalar(sm[:, 5, :], sm[:, 1, :], LN_EPS, None, ALU.add).then_inc(p_ve, 1)
                    then(v.scalar_tensor_tensor(w_a[:], x_at, 2.0, dl[:], ALU.mult, ALU.add))
                    then(v.tensor_tensor(w_a[:], w_a[:], by_tile(sm[:, 0, :]), ALU.subtract))
                    dve.wait_ge(p_pw, k + 1)
                    v.tensor_tensor(outs[:, at, :], w_a[:], by_tile(sm[:, 6, :]), ALU.mult)
                    if not (isinstance(k, int) and k < 2):
                        dve.wait_ge(p_row, (k - 1) * BT)
                    v.scalar_tensor_tensor(coef[:, p, 0, :], r1_all[:, at], 2.0, sm[:, 6, :], ALU.mult, ALU.mult)
                    v.scalar_tensor_tensor(sm[:, 3, :], r1_all[:, at], 2.0, nm_all[:, at], ALU.mult, ALU.mult).then_inc(p_u, 1)
                    dve.wait_ge(p_u, 3 * k + 1)
                    v.tensor_tensor(sm[:, 4, :], sm[:, 3, :], sm[:, 0, :], ALU.subtract).then_inc(p_u, 1)
                    dve.wait_ge(p_u, 3 * k + 2)
                    v.tensor_tensor(coef[:, p, 1, :], sm[:, 4, :], sm[:, 6, :], ALU.mult).then_inc(p_coef, 1)
                    v.tensor_copy(sm[:, 7, :], sm[:, 6, :]).then_inc(p_u, 1)
                    then(v.tensor_copy(w_a[:, :, 0], sm[:, 3, :]))

                batch(0, 0)
                batch(1, 1)
                with dve.Fori(1, NBT // 2) as pair:
                    for p in range(2):
                        batch(pair * 2 + p, p)


def kernel(**inputs):
    import numpy as np
    import concourse.bacc as bacc
    from concourse.bass_utils import run_bass_kernel_spmd

    def arr(name):
        return np.asarray(inputs[name])

    def by_block(w):
        return np.ascontiguousarray(w.T.reshape(-1, 128, w.shape[0]).transpose(1, 0, 2))

    def column(v):
        return np.ascontiguousarray(v.reshape(-1, 128).T)

    x = np.ascontiguousarray(arr("L0_attn_hidden_states"))
    slopes = np.ascontiguousarray(arr("L0_ffn_spline_slopes"))
    conv_w = arr("L0_attn_conv_w")
    host = dict(
        x=x,
        w_rk=by_block(arr("L0_attn_in_proj_w")),
        w_mg=by_block(arr("L0_attn_mem_gate_w")),
        w0=by_block(arr("L0_attn_ch_gate_w0")),
        w1=np.ascontiguousarray(arr("L0_attn_ch_gate_w1").T),
        conv_w=np.ascontiguousarray(conv_w.reshape(-1, 128, conv_w.shape[1]).transpose(1, 0, 2)),
        conv_b=column(arr("L0_attn_conv_b")),
        gate_b1=np.ascontiguousarray(arr("L0_attn_ch_gate_b1")[None, :]),
        mem_b=np.ascontiguousarray(arr("L0_attn_mem_gate_b")[:, None]),
        res_w=column(arr("L0_attn_residual_weight")),
        gamma=np.ascontiguousarray(arr("L0_ffn_ln_gamma")),
        beta=np.ascontiguousarray(arr("L0_ffn_ln_beta")),
        bases=np.ascontiguousarray(arr("L0_ffn_spline_bases")),
        slopes=slopes,
        oscale=np.ascontiguousarray(arr("L0_ffn_output_scale")[:, None]),
    )
    nc = bacc.Bacc("TRN2", target_bir_lowering=False, num_devices=1)
    args = {k: nc.dram_tensor(f"in_{k}", v.shape, mybir.dt.from_np(v.dtype), kind="ExternalInput").ap()
            for k, v in host.items()}
    out = nc.dram_tensor("out", x.shape, F32, kind="ExternalOutput").ap()
    build(nc, out=out, **args)
    r = run_bass_kernel_spmd(nc, [{f"in_{k}": v for k, v in host.items()}], core_ids=[0])
    return r.results[0]["out"]
```

```python
from contextlib import ExitStack

import concourse.bass as bass
from concourse import mybir

ALU = mybir.AluOpType
ACT = mybir.ActivationFunctionType
F32 = mybir.dt.float32
BF16 = mybir.dt.bfloat16
U32 = mybir.dt.uint32
AX_X = mybir.AxisListType.X

P = 128
CH = 128
CPG = 2
T = CH * CPG
LEVELS = 7
HIST = 3
SLOTS = 5
SEL_MIN = 2.0 ** -60
SS_SCALE = 2.0 ** 20
BIG = 1e30
ATANH = (2.0000000078699283, 0.6666631600410559, 0.40024852291048835, 0.27961426376095516, 0.2817466568891232)
MAGIC = float(2 ** 23)
LN_EPS = 1e-5
EXP_AND_LOG = 6
SILU_AND_TANH = 18


class Event:

    def __init__(self, sem, per_group):
        self.sem, self.per_group = sem, per_group

    def at(self, g, i=0):
        return g * self.per_group + (i + 1)


def build(nc, x, w_rk, w_mg, w0, w1, conv_w, conv_b, gate_b1, mem_b, res_w, gamma, beta, bases, slopes, oscale, out):
    B, L, D = x.shape
    M = 64
    R = w0.shape[2]
    W = conv_w.shape[2]
    NB = D // P
    NG = B * L // T
    NC = B * L // CH
    NT = bases.shape[0]
    DS = D // NT
    GRID = bases.shape[2]
    NCL = 8
    TPC = NT // NCL
    HALF = 512
    NLV = LEVELS * (CH // 2)
    assert W == HIST + 1 and R == P and D == 2 * HALF and NG % 2 == 0 and NG >= 4
    R_SCALE = 0.5 / float(M) ** 0.5

    x_g = x.rearrange("b l d -> (b l) d").rearrange("(g c p) d -> g p c d", c=CPG, p=P)
    out_g = out.rearrange("b l d -> (b l) d").rearrange("(g c p) d -> g p c d", c=CPG, p=P)
    y_dram = nc.dram_tensor("y_scratch", (B * L, D), F32, kind="Internal").ap()
    y_g = y_dram.rearrange("(g c p) d -> g p c d", c=CPG, p=P)
    y_slices = y_dram.rearrange("n (t j) -> (n t) j", j=DS)
    out_slices = out.rearrange("b l d -> (b l) d").rearrange("n (t j) -> (n t) j", j=DS)

    with ExitStack() as whole:
        def sbw(name, shape, dt=F32):
            return whole.enter_context(nc.sbuf_tensor(name, shape, dt))

        ident = sbw("ident", [P, P])
        iota_t = sbw("iota_t", [P, NT])
        minus_half = sbw("minus_half", [P, CPG])
        nm_all = sbw("nm_all", [P, NC])
        r1_all = sbw("r1_all", [P, NC])
        r12_all = sbw("r12_all", [P, NC])
        ss_all = sbw("ss_all", [P, NC])
        idx_all = sbw("idx_all", [P, NC])
        EARLY = NC - 3 * CPG
        gidx_f = sbw("gidx_f", [P, NC])
        gidx = sbw("gidx", [P, NC], U32)
        xin0 = sbw("xin0", [P, CPG, D])
        assert NC * DS <= D
        y_sl = xin0[:, 0, 0:NC * DS].rearrange("p (n j) -> p n j", j=DS)
        s_gat = whole.enter_context(nc.semaphore("s_gat"))
        with ExitStack() as ctx:
            def sb(name, shape, dt=F32):
                return ctx.enter_context(nc.sbuf_tensor(name, shape, dt))

            def psum(name, shape, dt=F32):
                return ctx.enter_context(nc.psum_tensor(name, shape, dt))

            def sem(name):
                return ctx.enter_context(nc.semaphore(name))

            def ev(name, per_group):
                return Event(sem(name), per_group)

            w_rk_sb = sb("w_rk_sb", [P, NB, P])
            w_mg_sb = sb("w_mg_sb", [P, NB, P])
            w0_sb = sb("w0_sb", [P, NB, R])
            w1_sb = sb("w1_sb", [P, D])
            cw_sb = sb("cw_sb", [P, NB, W])
            cb_sb = sb("cb_sb", [P, NB])
            rw_sb = sb("rw_sb", [P, NB])
            mb_sb = sb("mb_sb", [P, 1])
            b1_split = sb("b1_split", [96, D], BF16)
            gam = sb("gam", [P, D])
            bet = sb("bet", [P, D])
            ones = sb("ones", [P, T])
            ones_bf = sb("ones_bf", [96, P], BF16)
            mask = sb("mask", [P, LEVELS, CH // 2])
            keep = sb("keep", [P, NG])
            ln_fix = sb("ln_fix", [P, 1])
            two = sb("two", [P, 1])
            MINUS_1_D, ONE_D, EPS = range(3)
            consts = sb("consts", [P, 3])
            c_tile = sb("c_tile", [P, NT])
            c_cluster = sb("c_cluster", [P, NCL])

            xin = [xin0, sb("xin1", [P, CPG, D])]
            xT = [sb(f"xT{i}", [P, NB, HIST + T]) for i in range(2)]
            acc = sb("acc", [P, NB, T])
            zT = [sb(f"zT{i}", [P, NB, T]) for i in range(2)]
            shT = sb("shT", [P, NB, T])
            tS = [sb(f"tS{i}", [P, T]) for i in range(2)]
            rr = sb("rr", [P, T])
            kk = sb("kk", [M, T])
            xs = sb("xs", [P, T])
            xa = sb("xa", [P, T])
            ge = sb("ge", [P, T])
            gl = sb("gl", [P, T])
            gw1 = sb("gw1", [P, T])
            grw = sb("grw", [P, T])
            sel = sb("sel", [M, T])
            lsel = sb("lsel", [M, T])
            tau = sb("tau", [M, T])
            gn = sb("gn", [M, T])
            tl = sb("tl", [M, T])
            ksq = sb("ksq", [M, T])
            nl = sb("nl", [M, T])
            kn = sb("kn", [P, T])
            bb = sb("bb", [P, T])
            rkp = [sb(f"rkp{i}", [M, T]) for i in range(2)]
            dec = [sb(f"dec{i}", [M, CPG]) for i in range(2)]
            X = sb("X", [P, SLOTS, T])
            E = sb("E", [P, SLOTS, T])
            RE = [sb(f"RE{i}", [P, SLOTS, T]) for i in range(2)]
            KE = [sb(f"KE{i}", [P, SLOTS, T]) for i in range(2)]
            keT_sb = sb("keT_sb", [P, CPG, M])
            Wm = [sb(f"Wm{i}", [P, LEVELS, CH // 2]) for i in range(2)]
            AT = [sb(f"AT{i}", [P, CH]) for i in range(2)]
            th = [[sb(f"th{i}{c}", [P, D]) for c in range(CPG)] for i in range(2)]
            S = [sb(f"S{i}", [M, D]) for i in range(2)]
            y = [sb(f"y{i}", [P, CPG, D]) for i in range(2)]
            xf = [sb(f"xf{i}", [P, D]) for i in range(2)]
            sg = sb("sg", [P, CPG, D], BF16)
            ysum = sb("ysum", [P, CPG])
            nm = [sb(f"nm{i}", [P, CPG]) for i in range(2)]
            ssm = sb("ssm", [P, CPG])
            st = sb("st", [P, 6, CPG])
            ts = sb("ts", [P, CPG, NT])
            cl = sb("cl", [P, CPG, NCL])
            key = sb("key", [P, CPG, NT])
            kmax = sb("kmax", [P, CPG])
            tidx = sb("tidx", [P, CPG])

            TX = psum("TX", [P, HALF])
            PR = psum("PR", [P, HALF])
            GA = psum("GA", [P, HALF])
            AB = psum("AB", [P, HALF])
            WK = [psum(f"WK{i}", [P, HALF]) for i in range(2)]
            OB = psum("OB", [P, 2 * HALF])

            s_w = sem("s_w")
            s_sl = [sem(f"s_sl{i}") for i in range(2)]
            s_slr = sem("s_slr")
            s_c = sem("s_c")
            s_cv = sem("s_cv")
            s_ss = sem("s_ss")
            s_setup = sem("s_setup")
            s_pc = sem("s_pc")
            s_gi = sem("s_gi")
            d_xin = [sem(f"d_xin{i}") for i in range(2)]
            d_yst = [sem(f"d_yst{i}") for i in range(2)]
            e_xtr, e_xev, e_hist = ev("e_xtr", 4), ev("e_xev", 4), ev("e_hist", 1)
            e_t, e_tev = ev("e_t", 1), ev("e_tev", 1)
            e_tap0 = ev("e_tap0", NB)
            e_conv, e_silu, e_proj, e_res = ev("e_conv", NB * HIST), ev("e_silu", 2), ev("e_proj", 1), ev("e_res", NB // 2)
            e_resm, e_resp = ev("e_resm", 1), ev("e_resp", 1)
            e_pr = ev("e_pr", 4)
            e_xa, e_ge, e_gz, e_gl, e_gw1, e_grw = (ev(n, 1) for n in ("e_xa", "e_ge", "e_gz", "e_gl", "e_gw1", "e_grw"))
            e_lg, e_sel, e_sc, e_ls, e_l2 = (ev(n, 1) for n in ("e_lg", "e_sel", "e_sc", "e_ls", "e_l2"))
            e_lt, e_tau, e_gn, e_tl, e_b, e_bd = (ev(n, 1) for n in ("e_lt", "e_tau", "e_gn", "e_tl", "e_b", "e_bd"))
            e_ks, e_ssq, e_n1, e_n2, e_ex, e_kg = (ev(n, 1) for n in ("e_ks", "e_ssq", "e_n1", "e_n2", "e_ex", "e_kg"))
            e_kn, e_kd, e_X, e_Ek, e_RE, e_KE, e_rkp = (
                ev(n, 1) for n in ("e_kn", "e_kd", "e_X", "e_Ek", "e_RE", "e_KE", "e_rkp"))
            e_E, e_gq = ev("e_E", 3), ev("e_gq", 4)
            e_keT, e_keTe = ev("e_keT", 1), ev("e_keTe", 1)
            e_c2, e_th, e_u = ev("e_c2", 4), ev("e_th", 4), ev("e_u", 2)
            e_Ah, e_Xl = ev("e_Ah", 2), ev("e_Xl", 1)
            e_A, e_Wm, e_at0, e_AT = ev("e_A", 2), ev("e_Wm", 2), ev("e_at0", 2), ev("e_AT", 2 * LEVELS)
            e_o, e_su, e_S, e_y = ev("e_o", 2), ev("e_su", 4), ev("e_S", 4), ev("e_y", 2)
            e_nm, e_sq, e_st = ev("e_nm", 2), ev("e_sq", 2), ev("e_st", 9)
            e_q, e_xf, e_sg = ev("e_q", 2), ev("e_xf", 2), ev("e_sg", 2)
            e_dec = ev("e_dec", 1)
            e_sc8, e_keep = ev("e_sc8", 11), ev("e_keep", 4)

            def wait(eng, e, g, i=0):
                eng.wait_ge(e.sem, e.at(g, i))

            def const(k, rows, n):
                return consts[0:rows, k:k + 1].to_broadcast([rows, n])

            def dma_at(g, p):
                return (g - p) * 8 + 16

            def level_halves(v, h):
                b = v.rearrange("p (n s h) -> p n s h", s=2, h=h)
                return b[:, :, 0, :], b[:, :, 1, :]

            def level_rows(l):
                return slice(0, M) if l % 2 == 0 else slice(M, P)

            def pipeline(eng, step):
                step(0, 0, True, False, False, False)
                step(1, 1, True, True, False, False)
                step(2, 0, True, True, True, False)
                step(3, 1, True, True, True, True)
                with eng.Fori(2, NG // 2) as pair:
                    step(pair * 2, 0, True, True, True, True)
                    step(pair * 2 + 1, 1, True, True, True, True)
                step(NG, 0, False, True, True, True)
                step(NG + 1, 1, False, False, True, True)
                step(NG + 2, 0, False, False, False, True)

            block = ctx.enter_context(nc.Block())

            N_W = 13
            SLQ = 4
            sl_tmp = [xin[i] for i in range(2)]

            @block.sync
            def _(sp):
                for dst, src in (
                    (w_rk_sb[:], w_rk), (w_mg_sb[:], w_mg), (w0_sb[:], w0), (w1_sb[:], w1),
                    (cw_sb[:], conv_w), (cb_sb[:], conv_b), (rw_sb[:], res_w), (mb_sb[:], mem_b),
                    (gam[:], gamma.partition_broadcast(P)), (bet[:], beta.partition_broadcast(P)),
                    (xf[0][0:1, :], gate_b1), (xf[0][32:33, :], gate_b1), (xf[0][64:65, :], gate_b1),
                ):
                    sp.dma_start(dst, src).then_inc(s_w, 16)
                sl = slopes.rearrange("t j g -> (t j g)").rearrange("(q n) -> q n", n=CPG * D)
                for q in range(D * GRID // (CPG * D)):
                    if q >= 2:
                        sp.wait_ge(s_slr, q - 1)
                    sp.dma_start(sl_tmp[q % 2][:].rearrange("p c d -> p (c d)"),
                                 sl[q].partition_broadcast(P)).then_inc(s_sl[q % 2], 16)
                sp.wait_ge(s_slr, D * GRID // (CPG * D))

                def step(g, p, front, gates, rec, back):
                    if front:
                        if not (isinstance(g, int) and g < 2):
                            wait(sp, e_xtr, g - 2, 3)
                            wait(sp, e_u, g - 2, 1)
                        sp.dma_start(xin[p][:], x_g[bass.ds(g, 1)].rearrange("g p c d -> (g p) c d")
                                     if not isinstance(g, int) else x_g[g]).then_inc(d_xin[p], 16)
                    if back:
                        b = g - 3
                        wait(sp, e_y, b, 1)
                        dst = y_g[b] if isinstance(b, int) else y_g[bass.ds(b, 1)].rearrange("g p c d -> (g p) c d")
                        sp.dma_start(dst, y[1 - p][:]).then_inc(d_yst[1 - p], 16)

                pipeline(sp, step)
                for p in range(2):
                    sp.wait_ge(d_yst[p], NG // 2 * 16)

            @block.tensor
            def _(pe):
                pe.wait_ge(s_w, 16 * N_W)
                pe.wait_ge(s_c, 2)
                pe.wait_ge(s_cv, 1)

                def step(g, p, front, gates, rec, back):
                    m, r = g - 1, g - 2

                    def before(k, n):
                        return not (isinstance(k, int) and k < n)

                    def fill(f):
                        if f == 0:
                            pe.wait_ge(d_xin[p], dma_at(g, p))
                        if f > 0:
                            wait(pe, e_xev, g, f - 1)
                        elif before(g, 1):
                            wait(pe, e_xev, g - 1, 3)
                        for k in range(4):
                            b, c = 2 * f + k // 2, k % 2
                            i = pe.transpose(TX[:, (b % 2) * T + c * P:(b % 2) * T + (c + 1) * P],
                                             xin[p][:, c, b * P:(b + 1) * P], ident[:])
                        i.then_inc(e_xtr.sem, 1)

                    def t_blocks(f):
                        wait(pe, e_xev, g, f)
                        if f == 0 and gates:
                            wait(pe, e_pr, m, 3)
                        for b in (2 * f, 2 * f + 1):
                            i = pe.matmul(PR[:, 0:T], w0_sb[:, b, :], xT[p][:, b, HIST:HIST + T],
                                          start=(b == 0), stop=(b == NB - 1))
                        if f == 3:
                            i.then_inc(e_t.sem, 1)

                    def gate_product(i):
                        c, h = i // 2, i % 2
                        if i == 0:
                            wait(pe, e_tev, g)
                        if i >= 2:
                            wait(pe, e_th, g, i - 2)
                        elif rec:
                            wait(pe, e_S, r, i + 2)
                        elif gates:
                            wait(pe, e_th, m, i + 2)
                        cols = slice(h * HALF, (h + 1) * HALF)
                        pe.matmul(WK[h][:], tS[p][:, c * P:(c + 1) * P], w1_sb[:, cols], start=True, stop=False)
                        pe.matmul(WK[h][:], ones_bf[:], b1_split[:, cols], start=False, stop=True).then_inc(e_c2.sem, 1)

                    def squares_sum():
                        wait(pe, e_ks, m)
                        if rec:
                            wait(pe, e_keTe, r)
                        pe.matmul(GA[:, T:2 * T], ones[0:M, 0:P], ksq[:], start=True, stop=True).then_inc(e_ssq.sem, 1)

                    def k_turned():
                        wait(pe, e_RE, r)
                        wait(pe, e_KE, r)
                        wait(pe, e_rkp, r)
                        wait(pe, e_n1, r)
                        if before(r, 1):
                            wait(pe, e_at0, r - 1, 1)
                        for c in range(CPG):
                            if c == 0:
                                scores(0)
                            i = pe.transpose(GA[:, T + c * M:T + (c + 1) * M],
                                             KE[p][M:P, SLOTS - 1, c * CH:(c + 1) * CH], ident[M:P, M:P])
                        i.then_inc(e_keT.sem, 1)

                    def scores(c):
                        if c:
                            wait(pe, e_at0, r, c - 1)
                        tok = slice(c * CH, (c + 1) * CH)
                        for l in (*range(1, LEVELS, 2), *range(0, LEVELS, 2)):
                            rows = level_rows(l)
                            if l == 0:
                                wait(pe, e_Ah, r, c)
                            later = level_halves(RE[p][rows, l // 2, tok], 2 ** l)[1]
                            i = pe.matmul(AB[:, l * 64:(l + 1) * 64], KE[p][rows, l // 2, tok], later,
                                          start=True, stop=True)
                            if l == LEVELS - 2:
                                i.then_inc(e_Ah.sem, 1)
                        pe.matmul(AB[:, NLV:NLV + 2], rkp[p][:, tok], ones[0:M, 0:2], start=True, stop=True)\
                          .then_inc(e_A.sem, 1)

                    def output(c):
                        if c == 0:
                            wait(pe, e_res, r, NB // 2 - 1)
                            wait(pe, e_resp, r)
                            if before(r, 1):
                                wait(pe, e_y, r - 1, 1)
                                wait(pe, e_S, r - 1, 3)
                        else:
                            wait(pe, e_y, r, 0)
                            wait(pe, e_S, r, 1)
                        wait(pe, e_AT, r, c * LEVELS + LEVELS - 1)
                        wait(pe, e_u, r, c)
                        tok = slice(c * CH, (c + 1) * CH)
                        for h in range(2):
                            cols = slice(h * HALF, (h + 1) * HALF)
                            pe.matmul(OB[:, cols], AT[c][:], th[p][c][:, cols], start=True, stop=False)
                            pe.matmul(OB[:, cols], RE[p][0:M, SLOTS - 1, tok], S[c][:, cols], start=False, stop=False)
                            for j in range(4):
                                b = 4 * h + j
                                i = pe.matmul(OB[:, b * P:(b + 1) * P], zT[p][:, b, tok], ident[:],
                                              is_transpose=True, start=False, stop=(j == 3))
                        i.then_inc(e_o.sem, 1)

                    def state(c):
                        for h in range(2):
                            if c == 0:
                                if gates:
                                    wait(pe, e_th, m, 2 + h)
                                elif before(r, 1):
                                    wait(pe, e_S, r - 1, 2 + h)
                                if h == 0:
                                    wait(pe, e_keTe, r)
                            else:
                                wait(pe, e_S, r, h)
                            pe.matmul(WK[h][0:M, :], keT_sb[:, c, :], th[p][c][:, h * HALF:(h + 1) * HALF],
                                      start=True, stop=True).then_inc(e_su.sem, 1)

                    if front:
                        fill(0)
                    if rec:
                        k_turned()
                    if front:
                        fill(1)
                    if gates:
                        squares_sum()
                    if rec:
                        scores(1)
                    if front:
                        fill(2)
                        t_blocks(0)
                        fill(3)
                        t_blocks(1)
                        t_blocks(2)
                    if rec:
                        output(0)
                        state(0)
                    if front:
                        t_blocks(3)
                    if rec:
                        output(1)
                        state(1)
                    if front:
                        wait(pe, e_tev, g)
                        for half in range(2):
                            for b in range(NB):
                                if half == 0 and b % 4 == 0:
                                    wait(pe, e_silu, g, b // 4)
                                w = w_rk_sb if half == 0 else w_mg_sb
                                i = pe.matmul(PR[:, half * T:(half + 1) * T], w[:, b, :], shT[:, b, :],
                                              start=(b == 0), stop=(b == NB - 1))
                            if half == 0:
                                for k in range(4):
                                    gate_product(k)
                        i.then_inc(e_proj.sem, 1)

                pipeline(pe, step)

            @block.scalar
            def _(act):
                act.wait_ge(s_w, 16 * N_W)
                act.wait_ge(s_c, 2)

                def tables(which):
                    nc.scalar.add_instruction(mybir.InstLoadActFuncSet(name=nc.get_next_instruction_name(),
                                                                       act_func_set_id=which))

                act.wait_ge(s_slr, D * GRID // (CPG * D))
                nc.scalar.activation(th[0][0][:], th[0][1][:], ACT.Sign).then_inc(s_ss, 1)

                def step(g, p, front, gates, rec, back):
                    m, r, b = g - 1, g - 2, g - 3

                    def before(k, n):
                        return not (isinstance(k, int) and k < n)

                    def x_out(f):
                        wait(act, e_xtr, g, f)
                        if f == 0 and before(g, 2):
                            wait(act, e_conv, g - 2, NB * HIST - 1)
                            wait(act, e_res, g - 2, NB // 2 - 1)
                            wait(act, e_resp, g - 2)
                            wait(act, e_t, g - 2)
                        if f == 0 and before(g, 1):
                            wait(act, e_hist, g - 1)
                        nc.scalar.activation(xT[p][:, 2 * f:2 * f + 2, HIST:HIST + T],
                                             TX[:].rearrange("p (b t) -> p b t", b=2), ACT.Copy).then_inc(e_xev.sem, 1)

                    def tanh(i):
                        c, h = i // 2, i % 2
                        wait(act, e_c2, g, i)
                        if rec:
                            wait(act, e_su, r, 2 * c + 1)
                        nc.scalar.activation(th[p][c][:, h * HALF:(h + 1) * HALF], WK[h][:], ACT.Tanh, scale=0.5)\
                            .then_inc(e_th.sem, 1)

                    def y_out(c):
                        wait(act, e_o, r, c)
                        if c == 0 and before(r, 2):
                            act.wait_ge(d_yst[p], dma_at(r - 2, p))
                            wait(act, e_q, r - 2, 1)
                            wait(act, e_sq, r - 2, 1)
                        if c == 0 and before(r, 1):
                            wait(act, e_nm, r - 1, 1)
                        nc.scalar.activation(y[p][:, c, :], OB[:], ACT.Identity,
                                             accum_out=ysum[:, c:c + 1]).then_inc(e_y.sem, 1)

                    def tap0(h):
                        wait(act, e_hist, g)
                        wait(act, e_xev, g, 2 * h + 1)
                        if before(g, 1):
                            wait(act, e_silu, g - 1, h)
                        for blk in range(h * NB // 2, (h + 1) * NB // 2):
                            nc.scalar.activation(acc[:, blk, :], xT[p][:, blk, 0:T], ACT.Identity,
                                                 scale=cw_sb[:, blk, 0:1], bias=cb_sb[:, blk:blk + 1])\
                                .then_inc(e_tap0.sem, 1)

                    if gates:
                        wait(act, e_proj, m)
                        if before(m, 1):
                            wait(act, e_RE, m - 1)
                            wait(act, e_rkp, m - 1)
                            wait(act, e_kn, m - 1)
                            wait(act, e_l2, m - 1)
                            wait(act, e_lt, m - 1)
                        nc.scalar.activation(kk[:], PR[M:P, 0:T], ACT.Copy).then_inc(e_pr.sem, 1)
                        nc.scalar.activation(xs[:], PR[:, T:2 * T], ACT.Identity, bias=mb_sb[:])\
                            .then_inc(e_pr.sem, 1)
                    if front:
                        x_out(0)
                    if gates:
                        wait(act, e_pr, m, 1)
                        if before(m, 1):
                            wait(act, e_lg, m - 1)
                        nc.scalar.activation(xa[:], xs[:], ACT.Abs).then_inc(e_xa.sem, 1)
                        tables(EXP_AND_LOG)
                        wait(act, e_xa, m)
                        nc.scalar.activation(ge[:], xa[:], ACT.Exp, scale=-1.0).then_inc(e_ge.sem, 1)
                        wait(act, e_ge, m)
                        nc.scalar.activation(grw[:], ge[:], ACT.Ln, bias=two[:]).then_inc(e_gz.sem, 1)
                        wait(act, e_gz, m)
                        nc.scalar.activation(grw[:], grw[:], ACT.Exp, scale=-1.0).then_inc(e_grw.sem, 1)
                    if rec:
                        wait(act, e_keT, r)
                        if before(r, 1):
                            wait(act, e_su, r - 1, 3)
                        nc.scalar.activation(keT_sb[:], GA[:, T:T + CPG * M].rearrange("p (c m) -> p c m", c=CPG),
                                             ACT.Copy).then_inc(e_keTe.sem, 1)
                    if front:
                        x_out(1)
                    if gates:
                        nc.scalar.activation(rr[0:M, :], PR[0:M, 0:T], ACT.Copy, scale=R_SCALE).then_inc(e_pr.sem, 1)
                        nc.scalar.activation(rr[M:P, :], PR[0:M, 0:T], ACT.Copy, scale=R_SCALE).then_inc(e_pr.sem, 1)
                    if front:
                        tap0(0)
                    if gates:
                        wait(act, e_lt, m)
                        if before(m, 1):
                            wait(act, e_tl, m - 1)
                        nc.scalar.activation(tau[:], xs[M:P, :], ACT.Exp).then_inc(e_tau.sem, 1)
                    if front:
                        x_out(2)
                    if gates:
                        wait(act, e_n1, m)
                        nc.scalar.activation(nl[:], nl[:], ACT.Ln).then_inc(e_n2.sem, 1)
                        wait(act, e_sc, m)
                        nc.scalar.activation(lsel[:], gl[0:M, :], ACT.Ln).then_inc(e_ls.sem, 1)
                    if front:
                        x_out(3)
                        tap0(1)
                    if gates:
                        wait(act, e_b, m)
                        nc.scalar.activation(bb[M:P, :], bb[0:M, :], ACT.Copy).then_inc(e_bd.sem, 1)
                    if back:
                        for c in range(CPG):
                            wait(act, e_nm, b, c)
                            if before(b, 1):
                                wait(act, e_sc8, b - 1, 3)
                            nc.scalar.activation(sg[:, c, :], y[1 - p][:, c, :], ACT.Square, bias=nm[1 - p][:, c:c + 1],
                                                 accum_out=ssm[:, c:c + 1]).then_inc(e_sq.sem, 1)
                    if rec:
                        y_out(0)
                    if front:
                        wait(act, e_t, g)
                        if before(g, 2):
                            wait(act, e_c2, g - 2, 3)
                        nc.scalar.activation(tS[p][:], PR[:, 0:T], ACT.Copy).then_inc(e_tev.sem, 1)
                    if gates:
                        wait(act, e_ex, m)
                        nc.scalar.activation(nl[:], nl[:], ACT.Exp, bias=ln_fix[0:M, :]).then_inc(e_kg.sem, 1)
                        wait(act, e_kn, m)
                        nc.scalar.activation(kn[M:P, :], kn[0:M, :], ACT.Copy).then_inc(e_kd.sem, 1)
                        wait(act, e_X, m)
                        if before(m, 1):
                            wait(act, e_KE, m - 1)
                            wait(act, e_dec, m - 1)
                        nc.scalar.activation(E[:, 0:4, :], X[:, 0:4, :], ACT.Exp).then_inc(e_E.sem, 1)
                        nc.scalar.activation(E[0:M, 4, :], bb[0:M, :], ACT.Exp).then_inc(e_E.sem, 1)
                        nc.scalar.activation(E[M:P, 4, :], X[M:P, 4, :], ACT.Exp).then_inc(e_E.sem, 1)
                    if front:
                        tables(SILU_AND_TANH)

                    def silu(h):
                        bs = slice(h * NB // 2, (h + 1) * NB // 2)
                        wait(act, e_conv, g, NB * HIST // 2 * (h + 1) - 1)
                        if before(g, 1):
                            wait(act, e_proj, g - 1)
                            wait(act, e_res, g - 1, NB // 2 - 1)
                            wait(act, e_resm, g - 1)
                        nc.scalar.activation(shT[:, bs, :], acc[:, bs, :], ACT.Silu).then_inc(e_silu.sem, 1)

                    def sign(c):
                        wait(act, e_xf, b, c)
                        wait(act, e_sq, b, c)
                        nc.scalar.activation(sg[:, c, :], xf[c][:], ACT.Sign).then_inc(e_sg.sem, 1)

                    if front:
                        silu(0)
                    if rec:
                        y_out(1)
                    if front:
                        silu(1)
                    if back:
                        sign(0)
                    if front:
                        tanh(0)
                        tanh(1)
                    if back:
                        sign(1)
                    if front:
                        tanh(2)
                        tanh(3)

                pipeline(act, step)

            @block.vector
            def _(dve):
                v = nc.vector
                for q in range(D * GRID // (CPG * D)):
                    n = CPG * D // GRID
                    dve.wait_ge(s_sl[q % 2], 16 * (q // 2 + 1))
                    v.tensor_reduce(th[0][1][:, q * n:(q + 1) * n],
                                    sl_tmp[q % 2][:].rearrange("p c (d g) -> p (c d) g", g=GRID), AX_X, ALU.add)\
                        .then_inc(s_slr, 1)
                dve.wait_ge(s_w, 16 * N_W)
                dve.wait_ge(s_c, 2)
                chain = [0]
                s_chain = s_setup

                def link(ins):
                    chain[0] += 1
                    ins.then_inc(s_chain, 1)
                    dve.wait_ge(s_chain, chain[0])

                link(v.memset(b1_split[:], 0.0))
                for row, parts in ((0, 1), (32, 2), (64, 3)):
                    rest = xf[0][row:row + 1, :]
                    part = sg[row:row + 1, 0, :]
                    for k in range(parts):
                        if k:
                            link(v.tensor_tensor(rest, rest, part, ALU.subtract))
                        link(v.tensor_copy(part if k < parts - 1 else b1_split[row:row + 1, :], rest))
                dve.wait_ge(s_ss, 1)
                link(v.tensor_tensor(gam[:], gam[:], th[0][0][:], ALU.mult))
                link(v.tensor_tensor(bet[:], bet[:], th[0][0][:], ALU.mult))
                link(v.memset(S[0][:], 0.0))
                v.memset(xT[0][:, :, 0:HIST], 0.0).then_inc(s_cv, 1)
                dve.wait_ge(s_cv, 1)

                def step(g, p, front, gates, rec, back):
                    m, r, b = g - 1, g - 2, g - 3

                    def before(k, n):
                        return not (isinstance(k, int) and k < n)

                    if back:
                        def affine(c):
                            wait(dve, e_y, b, c)
                            wait(dve, e_nm, b, c)
                            if before(b, 1):
                                wait(dve, e_sg, b - 1, c)
                            v.scalar_tensor_tensor(xf[c][:], y[1 - p][:, c, :], nm[1 - p][:, c:c + 1], gam[:],
                                                   ALU.add, ALU.mult).then_inc(e_q.sem, 1)
                            wait(dve, e_q, b, c)
                            wait(dve, e_st, b, 8)
                            v.scalar_tensor_tensor(xf[c][:], xf[c][:], st[:, 5, c:c + 1], bet[:], ALU.mult, ALU.add)\
                                .then_inc(e_xf.sem, 1)

                    def conv_round(h, i):
                        for j in range(NB // 2):
                            blk = h * (NB // 2) + j
                            n = (h * HIST + i - 1) * (NB // 2) + j
                            if i > 1:
                                wait(dve, e_conv, g, n - NB // 2)
                            else:
                                wait(dve, e_tap0, g, blk)
                            v.scalar_tensor_tensor(acc[:, blk, :], xT[p][:, blk, i:i + T], cw_sb[:, blk, i:i + 1],
                                                   acc[:, blk, :], ALU.mult, ALU.add).then_inc(e_conv.sem, 1)

                    def history():
                        if not (isinstance(g, int) and g == 0):
                            wait(dve, e_xev, g - 1, 3)
                            if not (isinstance(g, int) and g < 2):
                                wait(dve, e_conv, g - 2, NB * HIST - 1)
                            k = keep[:, g:g + 1] if isinstance(g, int) else keep[:, bass.ds(g, 1)]
                            v.tensor_scalar(xT[p][:, :, 0:HIST], xT[1 - p][:, :, T:T + HIST], k, None, ALU.mult)\
                                .then_inc(e_hist.sem, 1)
                        else:
                            v.memset(xT[p][:, :, 0:HIST], 0.0).then_inc(e_hist.sem, 1)

                    def masked(c):
                        wait(dve, e_A, r, c)
                        if before(r, 1):
                            wait(dve, e_AT, r - 1, (c + 1) * LEVELS - 1)
                        v.tensor_tensor(Wm[c][:], AB[:, 0:NLV].rearrange("p (l t) -> p l t", l=LEVELS), mask[:], ALU.mult)\
                            .then_inc(e_Wm.sem, 1)
                        if before(r, 1):
                            wait(dve, e_o, r - 1, c)
                        v.tensor_scalar(AT[c][:], ident[:], AB[:, NLV:NLV + 1], None, ALU.mult).then_inc(e_at0.sem, 1)

                    def gate(c):
                        wait(dve, e_th, m, 2 * c + 1)
                        v.scalar_tensor_tensor(th[1 - p][c][:], th[1 - p][c][:], 1.0, xin[1 - p][:, c, :],
                                               ALU.add, ALU.mult).then_inc(e_u.sem, 1)

                    def decay(c):
                        for h in range(2):
                            cols = slice(h * HALF, (h + 1) * HALF)
                            wait(dve, e_su, r, 2 * c + h)
                            if c == 0:
                                wait(dve, e_dec, r)
                                if before(r, 1):
                                    wait(dve, e_o, r - 1, 1)
                                    wait(dve, e_S, r - 1, 2 + h)
                            else:
                                wait(dve, e_o, r, 0)
                                wait(dve, e_S, r, h)
                            v.scalar_tensor_tensor(S[1 - c][:, cols], S[c][:, cols], dec[p][:, c:c + 1],
                                                   WK[h][0:M, :], ALU.mult, ALU.add).then_inc(e_S.sem, 1)

                    def residual(lo, hi):
                        for blk in range(lo, hi):
                            wait(dve, e_silu, g, blk // 4)
                            if rec and blk == 0:
                                wait(dve, e_o, r, 1)
                            v.scalar_tensor_tensor(zT[p][:, blk, :], shT[:, blk, :], rw_sb[:, blk:blk + 1],
                                                   xT[p][:, blk, HIST:HIST + T], ALU.mult, ALU.add)\
                                .then_inc(e_res.sem, 1)

                    if front:
                        history()
                    if isinstance(g, int) and g == NG:
                        wait(dve, e_sc8, g - 4, 10)
                        v.tensor_tensor(gidx[:, 0:EARLY], gidx_f[:, 0:EARLY], idx_all[:, 0:EARLY], ALU.add)\
                            .then_inc(s_gi, 1)
                    if gates:
                        gate(0)
                    if rec:
                        masked(0)
                    if gates:
                        gate(1)
                        wait(dve, e_ssq, m)
                        if before(m, 1):
                            wait(dve, e_kn, m - 1)
                        v.tensor_scalar(nl[:], GA[0:M, T:2 * T], SS_SCALE, 1e-24 * SS_SCALE, ALU.mult, ALU.max)\
                            .then_inc(e_n1.sem, 1)
                    if gates:
                        wait(dve, e_gl, m)
                        v.tensor_scalar(grw[:], gl[:], ATANH[4], None, ALU.mult).then_inc(e_gq.sem, 1)
                        for k in (3, 2, 1):
                            wait(dve, e_gq, m, 3 - k)
                            v.scalar_tensor_tensor(grw[:], grw[:], ATANH[k], gl[:], ALU.add, ALU.mult)\
                                .then_inc(e_gq.sem, 1)
                        wait(dve, e_gq, m, 3)
                        v.scalar_tensor_tensor(grw[:], grw[:], ATANH[0], gw1[:], ALU.add, ALU.mult).then_inc(e_lg.sem, 1)
                        wait(dve, e_lg, m)
                        if before(m, 1):
                            wait(dve, e_tau, m - 1)
                        v.scalar_tensor_tensor(xs[M:P, :], xs[M:P, :], 0.0, grw[M:P, :], ALU.min, ALU.subtract)\
                            .then_inc(e_lt.sem, 1)
                        v.scalar_tensor_tensor(sel[:], xs[0:M, :], 0.0, grw[0:M, :], ALU.max, ALU.add)\
                            .then_inc(e_sel.sem, 1)
                        wait(dve, e_sel, m)
                        v.tensor_scalar(gl[0:M, :], sel[:], SEL_MIN, None, ALU.max).then_inc(e_sc.sem, 1)
                    if rec:
                        masked(1)
                    if front:
                        conv_round(0, 1)
                    if gates:
                        wait(dve, e_gn, m)
                        if before(m, 1):
                            wait(dve, e_X, m - 1)
                            wait(dve, e_E, m - 1, 1)
                            wait(dve, e_bd, m - 1)
                        for c in range(CPG):
                            tok = slice(c * CH, (c + 1) * CH)
                            i = v.tensor_tensor_scan(bb[0:M, tok], ones[0:M, 0:CH], gn[:, tok], 0.0, ALU.mult, ALU.subtract)
                        i.then_inc(e_b.sem, 1)
                    if front:
                        conv_round(0, 2)
                    if gates:
                        wait(dve, e_ls, m)
                        v.tensor_tensor(lsel[:], lsel[:], xs[0:M, :], ALU.min).then_inc(e_l2.sem, 1)
                    if front:
                        conv_round(0, 3)
                    if gates:
                        wait(dve, e_tl, m)
                        wait(dve, e_n2, m)
                        v.scalar_tensor_tensor(nl[:], nl[:], -0.5, tl[:], ALU.mult, ALU.add).then_inc(e_ex.sem, 1)
                    if front:
                        conv_round(1, 1)
                    if rec:
                        decay(0)
                    if front:
                        conv_round(1, 2)
                        conv_round(1, 3)
                    if gates:
                        wait(dve, e_E, m, 1)
                        k = keep[0:M, m:m + 1] if isinstance(m, int) else keep[0:M, bass.ds(m, 1)]
                        v.tensor_scalar(E[0:M, 4, 0:CH], E[0:M, 4, 0:CH], k, None, ALU.mult).then_inc(e_Ek.sem, 1)
                        wait(dve, e_E, m, 2)
                        wait(dve, e_Ek, m)
                        if before(m, 2):
                            wait(dve, e_o, m - 2, 1)
                            wait(dve, e_A, m - 2, 1)
                            wait(dve, e_S, m - 2, 3)
                        v.tensor_copy(dec[1 - p][:], E[0:M, 4, :].rearrange("m (c t) -> m c t", c=CPG)[:, :, CH - 1])\
                            .then_inc(e_dec.sem, 1)
                        v.tensor_tensor(RE[1 - p][:], E[:], rr[:].unsqueeze(1).to_broadcast([P, SLOTS, T]), ALU.mult)\
                            .then_inc(e_RE.sem, 1)
                    if rec:
                        decay(1)
                    if back:
                        affine(0)
                        affine(1)
                    if front:
                        residual(0, NB // 2)
                    if back:
                        for c in range(CPG):
                            wait(dve, e_sg, b, c)
                        k = [0]

                        def then(ins):
                            ins.then_inc(e_sc8.sem, 1)
                            wait(dve, e_sc8, b, k[0])
                            k[0] += 1

                        sg4 = sg[:].rearrange("p c (t j) -> p c t j", j=DS)
                        for half in (8, 4, 2):
                            then(v.tensor_tensor(sg4[:, :, :, 0:half], sg4[:, :, :, 0:half], sg4[:, :, :, half:2 * half],
                                                 ALU.add))
                        then(v.tensor_tensor(ts[:], sg4[:, :, :, 0], sg4[:, :, :, 1], ALU.add))
                        then(v.tensor_reduce(cl[:], ts[:].rearrange("p c (n t) -> p c n t", t=TPC), AX_X, ALU.add))
                        then(v.scalar_tensor_tensor(cl[:], cl[:], 4096.0,
                                                    c_cluster[:].unsqueeze(1).to_broadcast([P, CPG, NCL]),
                                                    ALU.mult, ALU.add))
                        then(v.scalar_tensor_tensor(key[:], ts[:], 8.0,
                                                    c_tile[:].unsqueeze(1).to_broadcast([P, CPG, NT]),
                                                    ALU.mult, ALU.add))
                        k4 = key[:].rearrange("p c (n t) -> p c n t", t=TPC)
                        then(v.tensor_tensor(k4, k4, cl[:].unsqueeze(3).to_broadcast([P, CPG, NCL, TPC]), ALU.add))
                        then(v.tensor_reduce(kmax[:], key[:], AX_X, ALU.max))
                        for c in range(CPG):
                            i = v.scalar_tensor_tensor(ts[:, c, :], key[:, c, :], kmax[:, c:c + 1], iota_t[:],
                                                       ALU.is_equal, ALU.mult)
                        then(i)
                        b2 = b * CPG
                        dst = idx_all[:, b2:b2 + CPG] if isinstance(b, int) else idx_all[:, bass.ds(b2, CPG)]
                        then(v.tensor_reduce(dst, ts[:], AX_X, ALU.add))

                pipeline(dve, step)

            @block.gpsimd
            def _(pool):
                q = nc.gpsimd
                q.memset(ident[:], 0.0).then_inc(s_pc, 1)
                q.memset(ones[:], 1.0)
                q.memset(ones_bf[:], 1.0)
                q.memset(minus_half[:], -0.5)
                for k, value in ((MINUS_1_D, -1.0 / D), (ONE_D, 1.0 / D), (EPS, LN_EPS)):
                    q.memset(consts[:, k:k + 1], value)
                q.memset(two[:], 2.0)
                q.memset(ln_fix[:], 10.0 * 0.6931471805599453)
                q.memset(mask[:], 1.0)
                q.memset(X[:], 0.0)
                q.memset(keep[:], 1.0).then_inc(s_pc, 1)
                pool.wait_ge(s_pc, 2)
                q.memset(keep[:].rearrange("p (b g) -> p b g", b=B)[:, :, 0:1], 0.0)
                q.affine_select(out=ident[:], in_=ident[:], compare_op=ALU.not_equal, fill=1.0, base=0,
                                pattern=[[-1, P]], channel_multiplier=1).then_inc(s_pc, 1)
                for l in range(LEVELS):
                    h = 2 ** l
                    mv = mask[:, l, :].rearrange("p (n h) -> p n h", h=h)
                    q.affine_select(out=mv, in_=mv, compare_op=ALU.is_ge, fill=0.0, base=0,
                                    pattern=[[-2 * h, 64 // h], [0, h]], channel_multiplier=1).then_inc(s_pc, 1)
                    pool.wait_ge(s_pc, 4 + 2 * l)
                    q.affine_select(out=mv, in_=mv, compare_op=ALU.is_ge, fill=0.0, base=h - 1,
                                    pattern=[[2 * h, 64 // h], [0, h]], channel_multiplier=-1).then_inc(s_pc, 1)
                q.iota(gidx_f[:], pattern=[[P * NT, NC]], base=0, channel_multiplier=NT,
                       allow_small_or_imprecise_dtypes=True)
                q.iota(iota_t[:], pattern=[[1, NT]], base=0, channel_multiplier=0, allow_small_or_imprecise_dtypes=True)
                q.iota(c_tile[:].rearrange("p (n t) -> p n t", t=TPC), pattern=[[0, NCL], [-1, TPC]], base=TPC - 1,
                       channel_multiplier=0, allow_small_or_imprecise_dtypes=True)
                q.iota(c_cluster[:], pattern=[[-512, NCL]], base=512 * (NCL - 1), channel_multiplier=0,
                       allow_small_or_imprecise_dtypes=True).then_inc(s_c, 2)

                def step(g, p, front, gates, rec, back):
                    m, r, b = g - 1, g - 2, g - 3

                    def before(k, n):
                        return not (isinstance(k, int) and k < n)

                    def gather(part):
                        if part == 0:
                            pool.wait_ge(s_gi, 1)
                            wait(pool, e_u, NG - 2, 1)
                            pool.wait_ge(d_yst[0], dma_at(NG - 4, 0))
                            pool.wait_ge(d_yst[1], dma_at(NG - 5, 1))
                        cuts = (0, EARLY // 4, EARLY * 2 // 3, EARLY)
                        for n in range(cuts[part], cuts[part + 1]):
                            q.indirect_dma_start(y_sl[:, n, :], None, y_slices[0:EARLY * P * NT],
                                                 bass.IndirectOffsetOnAxis(ap=gidx[:, n:n + 1], axis=0))\
                                .then_inc(s_gat, 16)

                    def assemble(c):
                        wait(pool, e_Wm, r, c)
                        wait(pool, e_at0, r, c)
                        for l in range(LEVELS):
                            late = level_halves(AT[c][:], 2 ** l)[1]
                            if l:
                                wait(pool, e_AT, r, c * LEVELS + l - 1)
                            q.tensor_tensor(late, late, Wm[c][:, l, :].rearrange("p (n h) -> p n h", h=2 ** l), ALU.add)\
                                .then_inc(e_AT.sem, 1)

                    def mean(c):
                        wait(pool, e_y, r, c)
                        if c == 0 and before(r, 2):
                            wait(pool, e_keep, r - 2, 3)
                            wait(pool, e_q, r - 2, 1)
                        q.tensor_tensor(nm[p][:, c:c + 1], ysum[:, c:c + 1], const(MINUS_1_D, P, 1), ALU.mult)\
                            .then_inc(e_nm.sem, 1)

                    if gates:
                        wait(pool, e_pr, m, 0)
                        if before(m, 1):
                            wait(pool, e_ssq, m - 1)
                        q.tensor_tensor(ksq[:], kk[:], kk[:], ALU.mult).then_inc(e_ks.sem, 1)
                        wait(pool, e_grw, m)
                        q.tensor_tensor(gw1[:], grw[:], ge[:], ALU.mult).then_inc(e_gw1.sem, 1)
                        wait(pool, e_gw1, m)
                        q.tensor_tensor(gl[:], gw1[:], gw1[:], ALU.mult).then_inc(e_gl.sem, 1)
                    if rec:
                        assemble(0)
                    if gates:
                        wait(pool, e_sel, m)
                        wait(pool, e_tau, m)
                        if before(m, 1):
                            wait(pool, e_b, m - 1)
                        q.tensor_tensor(gn[:], sel[:], tau[:], ALU.mult).then_inc(e_gn.sem, 1)
                    if rec:
                        assemble(1)
                    if gates:
                        wait(pool, e_l2, m)
                        if before(m, 1):
                            wait(pool, e_ex, m - 1)
                        q.tensor_tensor(tl[:], tau[:], lsel[:], ALU.mult).then_inc(e_tl.sem, 1)
                        wait(pool, e_b, m)
                        if before(m, 1):
                            wait(pool, e_E, m - 1, 2)
                        for l in (*range(0, LEVELS, 2), *range(1, LEVELS, 2)):
                            if l == 1:
                                wait(pool, e_bd, m)
                                wait(pool, e_Xl, m)
                            h, rows = 2 ** l, level_rows(l)
                            b_early, b_late = level_halves(bb[rows, :], h)
                            x_early, x_late = level_halves(X[rows, l // 2, :], h)
                            ref = b_early[:, :, h - 1:h].to_broadcast([M, T // (2 * h), h])
                            i = q.tensor_tensor(x_late, b_late, ref, ALU.subtract)
                            if l:
                                i = q.tensor_tensor(x_early, ref, b_early, ALU.subtract)
                            if l == LEVELS - 1:
                                i.then_inc(e_Xl.sem, 1)
                        bend = bb[M:P, :].rearrange("p (c t) -> p c t", c=CPG)
                        q.tensor_tensor(X[M:P, 4, :].rearrange("p (c t) -> p c t", c=CPG),
                                        bend[:, :, CH - 1:CH].to_broadcast([M, CPG, CH]), bend, ALU.subtract)\
                            .then_inc(e_X.sem, 1)
                        wait(pool, e_X, m)
                        wait(pool, e_kg, m)
                        if before(m, 1):
                            wait(pool, e_KE, m - 1)
                        q.tensor_tensor(kn[0:M, :], kk[:], nl[:], ALU.mult).then_inc(e_kn.sem, 1)
                        wait(pool, e_kn, m)
                        wait(pool, e_pr, m, 3)
                        if before(m, 2):
                            wait(pool, e_A, m - 2, 1)
                            wait(pool, e_keT, m - 2)
                        q.tensor_tensor(rkp[1 - p][:], rr[0:M, :], kn[0:M, :], ALU.mult).then_inc(e_rkp.sem, 1)
                    if back:
                        k = [0]

                        def then(ins):
                            ins.then_inc(e_st.sem, 1)
                            wait(pool, e_st, b, k[0])
                            k[0] += 1

                        wait(pool, e_sq, b, 1)
                        if not (isinstance(b, int) and b == 0):
                            wait(pool, e_xf, b - 1, 1)
                        then(q.tensor_tensor(st[:, 0, :], ssm[:], const(ONE_D, P, CPG), ALU.mult))
                        then(q.tensor_tensor(st[:, 0, :], st[:, 0, :], const(EPS, P, CPG), ALU.add))
                        then(q.tensor_tensor(st[:, 1, :], st[:, 0, :], minus_half[:], ALU.pow))
                        then(q.tensor_tensor(st[:, 2, :], st[:, 1, :], st[:, 1, :], ALU.mult))
                        then(q.tensor_tensor(st[:, 3, :], st[:, 2, :], ssm[:], ALU.mult))
                        then(q.tensor_tensor(st[:, 4, :], st[:, 3, :], const(ONE_D, P, CPG), ALU.mult))
                        then(q.tensor_tensor(st[:, 4, :], st[:, 4, :], const(EPS, P, CPG), ALU.add))
                        then(q.tensor_tensor(st[:, 4, :], st[:, 4, :], minus_half[:], ALU.pow))
                        then(q.tensor_tensor(st[:, 5, :], st[:, 4, :], st[:, 1, :], ALU.mult))
                        for dst, src in ((nm_all, nm[1 - p][:]), (r1_all, st[:, 1, :]), (r12_all, st[:, 5, :]), (ss_all, st[:, 3, :])):
                            col = slice(b * CPG, (b + 1) * CPG) if isinstance(b, int) else bass.ds(b * CPG, CPG)
                            q.tensor_copy(dst[:, col], src).then_inc(e_keep.sem, 1)
                    if rec:
                        mean(0)
                    if gates:
                        wait(pool, e_kd, m)
                        wait(pool, e_Ek, m)
                        wait(pool, e_E, m, 2)
                        q.tensor_tensor(KE[1 - p][:], E[:], kn[:].unsqueeze(1).to_broadcast([P, SLOTS, T]), ALU.mult)\
                            .then_inc(e_KE.sem, 1)
                    if rec:
                        mean(1)
                    if isinstance(g, int) and g >= NG:
                        gather(g - NG)
                    if front:
                        wait(pool, e_silu, g, 1)
                        if rec:
                            wait(pool, e_o, r, 1)
                        z = zT[p][:, NB // 2:NB, :]
                        q.tensor_tensor(z, shT[:, NB // 2:NB, :],
                                        rw_sb[:, NB // 2:NB].unsqueeze(2).to_broadcast([P, NB // 2, T]), ALU.mult)\
                            .then_inc(e_resm.sem, 1)
                        wait(pool, e_resm, g)
                        q.tensor_tensor(z, z, xT[p][:, NB // 2:NB, HIST:HIST + T], ALU.add).then_inc(e_resp.sem, 1)

                pipeline(pool, step)

        with ExitStack() as ctx:
            def sb(name, shape, dt=F32):
                return ctx.enter_context(nc.sbuf_tensor(name, shape, dt))

            def psum(name, shape, dt=F32):
                return ctx.enter_context(nc.psum_tensor(name, shape, dt))

            def sem(name):
                return ctx.enter_context(nc.semaphore(name))

            BT = 8
            NBT = NC // BT
            assert NC % 16 == 0
            TC = 2 * DS * GRID
            assert TC == HALF
            iota_g = sb("iota_g", [P, GRID])
            oh = sb("oh", [P, NC, NT], BF16)
            ohT = sb("ohT", [NT, NC, P], BF16)
            pen = sb("pen", [P, NC, NT])
            pick = sb("pick", [P, NC, NT])
            t1 = sb("t1", [NT, 2 * DS])
            t1s = sb("t1s", [NT, 3, 2 * DS], BF16)
            t2 = sb("t2", [NT, TC])
            t2s = sb("t2s", [NT, 3, TC], BF16)
            t3 = sb("t3", [NT, 4])
            t3s = sb("t3s", [NT, 3, 4], BF16)
            gb = sb("gb", [P, NC, 2 * DS])
            x1s = sb("x1s", [P, NC, DS])
            xfs = sb("xfs", [P, NC, DS])
            mm = sb("mm", [P, 2, NC])
            ext = sb("ext", [P, 2, NT])
            rng3 = sb("rng3", [P, NC, 4])
            rng = sb("rng", [P, NC])
            gcell = sb("gcell", [P, NC, DS])
            tmp = sb("tmp", [P, NC, DS])
            ohg = sb("ohg", [P, 4, DS, GRID])
            pr = sb("pr", [P, 4, TC])
            bsv = sb("bsv", [P, BT, 2, DS])
            dl = sb("dl", [P, BT, DS])
            w_a = sb("w_a", [P, BT, DS])
            sm = sb("sm", [P, 7, BT])
            coef = sb("coef", [P, 2, 2, BT])
            outs = sb("outs", [P, NC, DS])
            mh8 = sb("mh8", [P, BT])
            ident_bf = sb("ident_bf", [P, P], BF16)
            rows = [sb(f"rows{i}", [P, BT, D]) for i in range(2)]

            Z = [psum(f"Z{i}", [P, HALF]) for i in range(4)]
            OT = [psum(f"OT{i}", [NT, 8, P], BF16) for i in range(2)]
            QA = psum("QA", [P, HALF])
            QB = psum("QB", [P, HALF])

            p_tab, p_i, p_gi = sem("p_tab"), sem("p_i"), sem("p_gi")
            p_oh, p_ohT, p_ohTe, p_t1, p_g1, p_g1e = (sem(n) for n in ("p_oh", "p_ohT", "p_ohTe", "p_t1", "p_g1", "p_g1e"))
            p_v, p_ext, p_extT, p_t3, p_r3, p_u = (sem(n) for n in ("p_v", "p_ext", "p_extT", "p_t3", "p_r3", "p_u"))
            p_z, p_zf, p_b, p_coef, p_pw, p_ve = (sem(n) for n in ("p_z", "p_zf", "p_b", "p_coef", "p_pw", "p_ve"))
            p_row, p_sc, p_bb, p_g = (sem(n) for n in ("p_row", "p_sc", "p_bb", "p_g"))
            p_ld = [[sem(f"p_ld{p}{h}") for h in range(2)] for p in range(2)]
            p_st = [[sem(f"p_st{p}{h}") for h in range(2)] for p in range(2)]
            VB = 14

            y_b = y_dram.rearrange("(q n p) d -> q p n d", n=BT, p=P)
            out_b = out.rearrange("b l d -> (b l) d").rearrange("(q n p) d -> q p n d", n=BT, p=P)
            block = ctx.enter_context(nc.Block())

            @block.sync
            def _(sp):
                sp.dma_start(t1[:, 0:DS], gamma.rearrange("(t j) -> t j", j=DS)).then_inc(p_tab, 16)
                sp.dma_start(t1[:, DS:2 * DS], beta.rearrange("(t j) -> t j", j=DS)).then_inc(p_tab, 16)
                sp.dma_start(t2[:, 0:TC // 2], bases.rearrange("t j g -> t (j g)")).then_inc(p_tab, 16)
                sp.dma_start(t2[:, TC // 2:TC], slopes.rearrange("t j g -> t (j g)")).then_inc(p_tab, 16)
                sp.dma_start(t3[:, 2:3], oscale).then_inc(p_tab, 16)

                def load(q, p, after_store=False):
                    src = y_b[q] if isinstance(q, int) else y_b[bass.ds(q, 1)].rearrange("q p n d -> (q p) n d")
                    for h in range(2):
                        if after_store:
                            sp.wait_ge(p_st[p][h], (q - p) * 8)
                        hs = slice(h * BT // 2, (h + 1) * BT // 2)
                        sp.dma_start(rows[p][:, hs, :], src[:, hs, :]).then_inc(p_ld[p][h], 16)

                def store(q, p):
                    dst = out_b[q] if isinstance(q, int) else out_b[bass.ds(q, 1)].rearrange("q p n d -> (q p) n d")
                    for h in range(2):
                        hs = slice(h * BT // 2, (h + 1) * BT // 2)
                        sp.wait_ge(p_row, q * BT + (h + 1) * BT // 2)
                        sp.dma_start(dst[:, hs, :], rows[p][:, hs, :]).then_inc(p_st[p][h], 16)

                load(0, 0)
                load(1, 1)
                with sp.Fori(0, NBT // 2 - 1) as pair:
                    for p in range(2):
                        store(pair * 2 + p, p)
                        load(pair * 2 + p + 2, p, after_store=True)
                for p in range(2):
                    store(NBT - 2 + p, p)
                for p in range(2):
                    for h in range(2):
                        sp.wait_ge(p_st[p][h], 8 * NBT)

            @block.gpsimd
            def _(pool):
                q = nc.gpsimd
                q.iota(iota_g[:], pattern=[[1, GRID]], base=0, channel_multiplier=0,
                       allow_small_or_imprecise_dtypes=True).then_inc(p_i, 1)
                q.memset(mh8[:], -0.5).then_inc(p_i, 1)
                pool.wait_ge(p_gi, 1)
                for n in range(EARLY, NC):
                    q.indirect_dma_start(y_sl[:, n, :], None, y_slices,
                                         bass.IndirectOffsetOnAxis(ap=gidx[:, n:n + 1], axis=0)).then_inc(s_gat, 16)

                def batch(k):
                    pool.wait_ge(p_ve, k + 1)
                    q.tensor_tensor(sm[:, 6, :], sm[:, 5, :], mh8[:], ALU.pow).then_inc(p_pw, 1)

                def scatter(k):
                    pool.wait_ge(p_b, VB * (k + 1))
                    for h in range(2):
                        pool.wait_ge(p_st[k % 2][h], 16 * (k // 2 + 1))
                    for n in range(k * BT, (k + 1) * BT):
                        q.indirect_dma_start(out_slices, bass.IndirectOffsetOnAxis(ap=gidx[:, n:n + 1], axis=0),
                                             outs[:, n, :], None).then_inc(p_sc, 16)

                pool.wait_ge(p_i, 2)
                for k in range(NBT):
                    batch(k)
                    if k >= 2:
                        scatter(k - 2)
                scatter(NBT - 2)
                scatter(NBT - 1)
                pool.wait_ge(p_sc, 16 * NC)

            @block.tensor
            def _(pe):
                pe.wait_ge(p_oh, 2)
                for f in range(NC // 8):
                    if f >= 2:
                        pe.wait_ge(p_ohTe, f - 1)
                    for j in range(8):
                        i = pe.transpose(OT[f % 2][:, j, :], oh[:, f * 8 + j, :], ident_bf[:])
                    i.then_inc(p_ohT, 1)
                pe.wait_ge(p_ohTe, NC // 8)
                pe.wait_ge(p_t1, 1)
                for f in range(NC // 16):
                    for j in range(16):
                        for k in range(3):
                            i = pe.matmul(Z[f % 4][:, j * 32:(j + 1) * 32], ohT[:, f * 16 + j, :], t1s[:, k, :],
                                          start=(k == 0), stop=(k == 2))
                    i.then_inc(p_g1, 1)
                pe.wait_ge(p_ext, 1)
                for k in range(2):
                    i = pe.transpose(QA[0:NT, k * P:(k + 1) * P], ext[:, k, :], ident[:])
                i.then_inc(p_extT, 1)
                pe.wait_ge(p_t3, 1)
                for n in range(NC):
                    for k in range(3):
                        i = pe.matmul(QB[:, n * 4:(n + 1) * 4], ohT[:, n, :], t3s[:, k, :], start=(k == 0), stop=(k == 2))
                i.then_inc(p_r3, 1)
                pe.wait_ge(p_g1e, NC // 16)

                def tables(n, j):
                    if not isinstance(n, int):
                        pe.wait_ge(p_zf, n - 3)
                    elif n >= 4:
                        pe.wait_ge(p_zf, n - 3)
                    lhs = ohT[:, n, :] if isinstance(n, int) else ohT[:, bass.ds(n, 1), :].rearrange("t n p -> t (n p)")
                    for k in range(3):
                        i = pe.matmul(Z[j % 4][:], lhs, t2s[:, k, :], start=(k == 0), stop=(k == 2))
                    i.then_inc(p_z, 1)

                for j in range(4):
                    tables(j, j)
                with pe.Fori(1, NC // 4) as four:
                    for j in range(4):
                        tables(four * 4 + j, j)

            @block.scalar
            def _(act):
                for f in range(NC // 8):
                    act.wait_ge(p_ohT, f + 1)
                    nc.scalar.activation(ohT[:, f * 8:(f + 1) * 8, :], OT[f % 2][:], ACT.Copy).then_inc(p_ohTe, 1)
                for f in range(NC // 16):
                    act.wait_ge(p_g1, f + 1)
                    nc.scalar.activation(gb[:, f * 16:(f + 1) * 16, :],
                                         Z[f % 4][:].rearrange("p (n j) -> p n j", n=16), ACT.Copy).then_inc(p_g1e, 1)

                def scale_rows(k, p):
                    act.wait_ge(p_coef, k + 1)
                    for h in range(2):
                        act.wait_ge(p_ld[p][h], (k - p) * 8 + 16)
                        for n in range(h * BT // 2, (h + 1) * BT // 2):
                            nc.scalar.activation(rows[p][:, n, :], rows[p][:, n, :], ACT.Identity,
                                                 scale=coef[:, p, 0, n:n + 1], bias=coef[:, p, 1, n:n + 1])\
                                .then_inc(p_row, 1)

                with act.Fori(0, NBT // 2) as pair:
                    for p in range(2):
                        scale_rows(pair * 2 + p, p)

            @block.vector
            def _(dve):
                v = nc.vector
                count = [0]

                def link(ins):
                    count[0] += 1
                    ins.then_inc(p_v, 1)
                    dve.wait_ge(p_v, count[0])

                v.tensor_tensor(gidx[:, EARLY:NC], gidx_f[:, EARLY:NC], idx_all[:, EARLY:NC], ALU.add).then_inc(p_gi, 1)
                v.tensor_copy(ident_bf[:], ident[:]).then_inc(p_oh, 1)
                v.tensor_tensor(oh[:], iota_t[:].unsqueeze(1).to_broadcast([P, NC, NT]),
                                idx_all[:].unsqueeze(2).to_broadcast([P, NC, NT]), ALU.is_equal).then_inc(p_oh, 1)
                dve.wait_ge(p_tab, 16 * 5)

                def split(dst, src):
                    for k in range(3):
                        link(v.tensor_copy(dst[:, k, :], src))
                        if k < 2:
                            link(v.tensor_tensor(src, src, dst[:, k, :], ALU.subtract))

                split(t1s, t1[:])
                v.memset(t3[:, 3:4], 0.0).then_inc(p_t1, 1)
                split(t2s, t2[:])
                dve.wait_ge(p_oh, 2)
                link(v.tensor_scalar(pen[:], oh[:], 2.0 * BIG, -BIG, ALU.mult, ALU.add))

                def per_tile(a):
                    return a.unsqueeze(2).to_broadcast([P, NC, DS])

                dve.wait_ge(s_gat, 16 * NC)
                dve.wait_ge(p_g1e, NC // 16)
                link(v.tensor_tensor(xfs[:], y_sl, per_tile(nm_all[:]), ALU.add))
                link(v.tensor_tensor(x1s[:], xfs[:], per_tile(r1_all[:]), ALU.mult))
                link(v.tensor_tensor(xfs[:], xfs[:], per_tile(r12_all[:]), ALU.mult))
                link(v.tensor_tensor(xfs[:], xfs[:], gb[:, :, 0:DS], ALU.mult))
                link(v.tensor_tensor(xfs[:], xfs[:], gb[:, :, DS:2 * DS], ALU.add))
                link(v.tensor_reduce(mm[:, 0, :], xfs[:], AX_X, ALU.max))
                link(v.tensor_reduce(mm[:, 1, :], xfs[:], AX_X, ALU.min))
                link(v.tensor_scalar(mm[:, 1, :], mm[:, 1, :], -1.0, None, ALU.mult))
                for k in range(2):
                    link(v.tensor_tensor(pick[:], pen[:], mm[:, k, :].unsqueeze(2).to_broadcast([P, NC, NT]), ALU.min))
                    link(v.tensor_reduce(ext[:, k, :], pick[:].rearrange("p n t -> p t n"), AX_X, ALU.max))
                v.memset(sm[:], 0.0).then_inc(p_ext, 1)
                dve.wait_ge(p_extT, 1)
                link(v.tensor_reduce(t3[:, 0:2], QA[0:NT, 0:2 * P].rearrange("t (k p) -> t k p", k=2), AX_X, ALU.max))
                split(t3s, t3[:])
                v.memset(sm[:], 0.0).then_inc(p_t3, 1)
                dve.wait_ge(p_r3, 1)
                link(v.tensor_copy(rng3[:], QB[:, 0:NC * 4].rearrange("p (n k) -> p n k", k=4)))
                link(v.scalar_tensor_tensor(rng[:], rng3[:, :, 0], 0.0, rng3[:, :, 1], ALU.add, ALU.add))
                link(v.tensor_scalar(rng[:], rng[:], 1e-8, None, ALU.add))
                link(v.reciprocal(rng[:], rng[:]))
                link(v.tensor_tensor(xfs[:], xfs[:], per_tile(rng3[:, :, 1]), ALU.add))
                link(v.tensor_tensor(xfs[:], xfs[:], per_tile(rng[:]), ALU.mult))
                link(v.tensor_scalar(xfs[:], xfs[:], 0.0, 1.0 - 1e-6, ALU.max, ALU.min))
                link(v.tensor_scalar(xfs[:], xfs[:], float(GRID), None, ALU.mult))
                link(v.tensor_scalar(gcell[:], xfs[:], MAGIC, None, ALU.add))
                link(v.tensor_scalar(gcell[:], gcell[:], -MAGIC, None, ALU.add))
                link(v.tensor_tensor(tmp[:], gcell[:], xfs[:], ALU.is_gt))
                link(v.tensor_tensor(gcell[:], gcell[:], tmp[:], ALU.subtract))
                link(v.tensor_tensor(xfs[:], xfs[:], gcell[:], ALU.subtract))
                dve.wait_ge(p_i, 2)

                def batch(k, p):
                    n0 = k * BT
                    at = bass.ds(n0, BT)
                    def onehot(j):
                        n = n0 + j
                        gc = gcell[:, bass.ds(n, 1), :].rearrange("p n j -> p (n j)").unsqueeze(2)\
                            .to_broadcast([P, DS, GRID])
                        v.tensor_tensor(ohg[:, j % 4, :, :], iota_g[:].unsqueeze(1).to_broadcast([P, DS, GRID]), gc,
                                        ALU.is_equal).then_inc(p_g, 1)

                    def chosen(j):
                        dve.wait_ge(p_z, n0 + j + 1)
                        dve.wait_ge(p_g, n0 + j + 1)
                        if j >= 4:
                            dve.wait_ge(p_bb, n0 + j - 3)
                        v.tensor_tensor(pr[:, j % 4, :].rearrange("p (k j g) -> p k j g", k=2, g=GRID),
                                        Z[j % 4][:].rearrange("p (k j g) -> p k j g", k=2, g=GRID),
                                        ohg[:, j % 4, :, :].unsqueeze(1).to_broadcast([P, 2, DS, GRID]), ALU.mult)\
                            .then_inc(p_zf, 1)

                    def summed(j):
                        dve.wait_ge(p_zf, n0 + j + 1)
                        v.tensor_reduce(bsv[:, j, :, :], pr[:, j % 4, :].rearrange("p (k j g) -> p k j g", k=2, g=GRID),
                                        AX_X, ALU.add).then_inc(p_bb, 1)

                    onehot(0)
                    for j in range(BT):
                        if j + 1 < BT:
                            onehot(j + 1)
                        chosen(j)
                        if j:
                            summed(j - 1)
                    summed(BT - 1)
                    c = [0]

                    def then(ins):
                        ins.then_inc(p_b, 1)
                        c[0] += 1
                        dve.wait_ge(p_b, k * VB + c[0])

                    def by_tile(a):
                        return a.unsqueeze(2).to_broadcast([P, BT, DS])

                    dve.wait_ge(p_bb, (k + 1) * BT)
                    x_at = x1s[:, at, :]
                    then(v.tensor_tensor(dl[:], bsv[:, :, 1, :], xfs[:, at, :], ALU.mult))
                    then(v.tensor_tensor(dl[:], dl[:], bsv[:, :, 0, :], ALU.add))
                    then(v.tensor_tensor(dl[:], dl[:], rng3[:, at, 2:3].to_broadcast([P, BT, DS]), ALU.mult))
                    then(v.tensor_reduce(sm[:, 0, :], dl[:], AX_X, ALU.add))
                    then(v.scalar_tensor_tensor(w_a[:], x_at, 4.0, dl[:], ALU.mult, ALU.add))
                    then(v.tensor_tensor(w_a[:], w_a[:], dl[:], ALU.mult))
                    then(v.tensor_reduce(sm[:, 1, :], w_a[:], AX_X, ALU.add))
                    then(v.tensor_scalar(sm[:, 0, :], sm[:, 0, :], 1.0 / D, None, ALU.mult))
                    then(v.scalar_tensor_tensor(sm[:, 1, :], ss_all[:, at], 4.0, sm[:, 1, :], ALU.mult, ALU.add))
                    then(v.tensor_tensor(sm[:, 2, :], sm[:, 0, :], sm[:, 0, :], ALU.mult))
                    then(v.scalar_tensor_tensor(sm[:, 1, :], sm[:, 1, :], 1.0 / D, sm[:, 2, :], ALU.mult, ALU.subtract))
                    v.tensor_scalar(sm[:, 5, :], sm[:, 1, :], LN_EPS, None, ALU.add).then_inc(p_ve, 1)
                    then(v.scalar_tensor_tensor(w_a[:], x_at, 2.0, dl[:], ALU.mult, ALU.add))
                    then(v.tensor_tensor(w_a[:], w_a[:], by_tile(sm[:, 0, :]), ALU.subtract))
                    dve.wait_ge(p_pw, k + 1)
                    then(v.tensor_tensor(outs[:, at, :], w_a[:], by_tile(sm[:, 6, :]), ALU.mult))
                    if not (isinstance(k, int) and k < 2):
                        dve.wait_ge(p_row, (k - 1) * BT)
                    v.scalar_tensor_tensor(coef[:, p, 0, :], r1_all[:, at], 2.0, sm[:, 6, :], ALU.mult, ALU.mult)
                    v.scalar_tensor_tensor(sm[:, 3, :], r1_all[:, at], 2.0, nm_all[:, at], ALU.mult, ALU.mult).then_inc(p_u, 1)
                    dve.wait_ge(p_u, 2 * k + 1)
                    v.tensor_tensor(sm[:, 4, :], sm[:, 3, :], sm[:, 0, :], ALU.subtract).then_inc(p_u, 1)
                    dve.wait_ge(p_u, 2 * k + 2)
                    v.tensor_tensor(coef[:, p, 1, :], sm[:, 4, :], sm[:, 6, :], ALU.mult).then_inc(p_coef, 1)

                batch(0, 0)
                batch(1, 1)
                with dve.Fori(1, NBT // 2) as pair:
                    for p in range(2):
                        batch(pair * 2 + p, p)


def kernel(**inputs):
    import numpy as np
    import concourse.bacc as bacc
    from concourse.bass_utils import run_bass_kernel_spmd

    def arr(name):
        return np.asarray(inputs[name])

    def by_block(w):
        return np.ascontiguousarray(w.T.reshape(-1, 128, w.shape[0]).transpose(1, 0, 2))

    def column(v):
        return np.ascontiguousarray(v.reshape(-1, 128).T)

    x = np.ascontiguousarray(arr("L0_attn_hidden_states"))
    slopes = np.ascontiguousarray(arr("L0_ffn_spline_slopes"))
    conv_w = arr("L0_attn_conv_w")
    host = dict(
        x=x,
        w_rk=by_block(arr("L0_attn_in_proj_w")),
        w_mg=by_block(arr("L0_attn_mem_gate_w")),
        w0=by_block(arr("L0_attn_ch_gate_w0")),
        w1=np.ascontiguousarray(arr("L0_attn_ch_gate_w1").T),
        conv_w=np.ascontiguousarray(conv_w.reshape(-1, 128, conv_w.shape[1]).transpose(1, 0, 2)),
        conv_b=column(arr("L0_attn_conv_b")),
        gate_b1=np.ascontiguousarray(arr("L0_attn_ch_gate_b1")[None, :]),
        mem_b=np.ascontiguousarray(arr("L0_attn_mem_gate_b")[:, None]),
        res_w=column(arr("L0_attn_residual_weight")),
        gamma=np.ascontiguousarray(arr("L0_ffn_ln_gamma")),
        beta=np.ascontiguousarray(arr("L0_ffn_ln_beta")),
        bases=np.ascontiguousarray(arr("L0_ffn_spline_bases")),
        slopes=slopes,
        oscale=np.ascontiguousarray(arr("L0_ffn_output_scale")[:, None]),
    )
    nc = bacc.Bacc("TRN2", target_bir_lowering=False, num_devices=1)
    args = {k: nc.dram_tensor(f"in_{k}", v.shape, mybir.dt.from_np(v.dtype), kind="ExternalInput").ap()
            for k, v in host.items()}
    out = nc.dram_tensor("out", x.shape, F32, kind="ExternalOutput").ap()
    build(nc, out=out, **args)
    r = run_bass_kernel_spmd(nc, [{f"in_{k}": v for k, v in host.items()}], core_ids=[0])
    return r.results[0]["out"]
```
